# Optimizing a Trainium2 kernel written in Bass

```python
import numpy as np
import jax
import jax.numpy as jnp

def _softmax(x, axis=-1):
    return jax.nn.softmax(x, axis=axis)

def _gelu(x):
    return jax.nn.gelu(x, approximate=True)

def _silu(x):
    return jax.nn.silu(x)

def _sigmoid(x):
    return jax.nn.sigmoid(x)

def _layernorm(x, axis=-1, eps=1e-05):
    m = jnp.mean(x, axis=axis, keepdims=True)
    v = jnp.var(x, axis=axis, keepdims=True)
    return (x - m) / jnp.sqrt(v + eps)

def _scatter_add(tgt, idx, src, axis=0):
    return tgt.at[idx].add(src)

def _segment_sum(src, seg, n):
    return jax.ops.segment_sum(src, seg, n)
kernel_name = 'mk_flamingo_gated_d1_seqx_r4_4c2f77'

def setup_inputs(seed: int=0):
    np.random.seed(seed)
    _w = jnp.asarray

    def _rec_inputs():
        import jax
        import jax.numpy as jnp
        _rk = jax.random.key(seed)
        x = -0.0002928 + 1 * jax.random.normal(jax.random.fold_in(_rk, 1), (4, 1024, 256), jnp.float32)
        _lenS = 1024 - jax.random.randint(jax.random.fold_in(_rk, 7), (4,), 0, max(1, 1024 // 4) + 1, jnp.int32)
        _lenS2 = 64 - jax.random.randint(jax.random.fold_in(_rk, 8), (4,), 0, max(1, 64 // 4) + 1, jnp.int32)
        _ctx_1024P = jax.random.normal(jax.random.fold_in(_rk, 11), (4, 16, 256), jnp.float32)
        _ctx_1024c = jax.random.dirichlet(jax.random.fold_in(_rk, 511), 0.3 * jnp.ones((16,), jnp.float32), (4, 64))
        _ctx_1024t = jnp.einsum('bsk,bkd->bsd', _ctx_1024c, _ctx_1024P)
        _ctx_1024t = _ctx_1024t * jax.lax.rsqrt(jnp.mean(jnp.square(_ctx_1024t)) + 1e-12) * 0.953939
        ctx_1024 = -1.39393e-06 + 0.999914 * (_ctx_1024t + 0.3 * jax.random.normal(jax.random.fold_in(_rk, 611), (4, 64, 256), jnp.float32))
        _validS = jnp.arange(1024)[None, :] < _lenS[:, None]
        _validS2 = jnp.arange(64)[None, :] < _lenS2[:, None]
        _causal = jnp.tril(jnp.ones((1024, 1024), dtype=bool))
        mask_BxSxS2_if1 = jnp.where(jnp.ones((4, 1024, 64), dtype=bool), 1, 0).astype(jnp.int32)
        _g = jax.random.normal(jax.random.fold_in(_rk, 9001), (2, 1), jnp.float32)
        _g = jnp.sign(_g) * jnp.maximum(jnp.abs(_g), 1.0) + (_g == 0) * 1.0
        g_xattn = _g[0]
        g_ffn = _g[1]
        return (x, ctx_1024, mask_BxSxS2_if1, g_xattn, g_ffn)
    x, ctx_1024, mask_BxSxS2_if1, g_xattn, g_ffn = _rec_inputs()

    def _L0_xattn_setup():
        import jax, jax.numpy as jnp
        import numpy as np
        HIDDEN = 256
        HEADS = 16
        D_K = HIDDEN // HEADS
        B, S = (2, 512)

        def _split_heads(x):
            b, s, _ = x.shape
            return x.reshape(b, s, HEADS, D_K).transpose(0, 2, 1, 3)
        key = jax.random.key(seed)
        ks = jax.random.split(key, 12)
        sc = 1.0 / np.sqrt(HIDDEN)
        return {'q': jax.random.normal(ks[0], (B, S, HIDDEN), jnp.float32), 'k': jax.random.normal(ks[1], (B, S, HIDDEN), jnp.float32), 'v': jax.random.normal(ks[2], (B, S, HIDDEN), jnp.float32), 'mask': jnp.ones((B, S, S), jnp.int32), 'Wq': jax.random.normal(ks[3], (HIDDEN, HIDDEN), jnp.float32) * sc, 'bq': jnp.zeros((HIDDEN,), jnp.float32), 'Wk': jax.random.normal(ks[4], (HIDDEN, HIDDEN), jnp.float32) * sc, 'bk': jnp.zeros((HIDDEN,), jnp.float32), 'Wv': jax.random.normal(ks[5], (HIDDEN, HIDDEN), jnp.float32) * sc, 'bv': jnp.zeros((HIDDEN,), jnp.float32), 'Wo': jax.random.normal(ks[6], (HIDDEN, HIDDEN), jnp.float32) * sc, 'bo': jnp.zeros((HIDDEN,), jnp.float32)}
    _L0_xattn_all = _L0_xattn_setup()
    _L0_xattn_in = {k: v for k, v in _L0_xattn_all.items() if k in ('Wq', 'bq', 'Wk', 'bk', 'Wv', 'bv', 'Wo', 'bo')}
    del _L0_xattn_all

    def _L0_ffn_setup():
        import jax, jax.numpy as jnp
        import numpy as np
        B, S, H, FFN, E = (2, 512, 256, 1024, 8)
        key = jax.random.key(seed)
        k0, k1, k2, k3 = jax.random.split(key, 4)
        return {'hidden_states': jax.random.normal(k0, (B, S, H), dtype=jnp.float32), 'Wr': jax.random.normal(k1, (H, E), dtype=jnp.float32) * 0.02, 'br': jnp.zeros((E,), dtype=jnp.float32), 'W1': jax.random.normal(k2, (E, H, FFN), dtype=jnp.float32) * 0.02, 'W2': jax.random.normal(k3, (E, FFN, H), dtype=jnp.float32) * 0.02}
    _L0_ffn_all = _L0_ffn_setup()
    _L0_ffn_in = {k: v for k, v in _L0_ffn_all.items() if k in ('Wr', 'br', 'W1', 'W2')}
    del _L0_ffn_all
    return {'x': x, 'ctx_1024': ctx_1024, 'mask_BxSxS2_if1': mask_BxSxS2_if1, 'g_xattn': g_xattn, 'g_ffn': g_ffn, 'L0_xattn_Wq': _L0_xattn_in['Wq'], 'L0_xattn_bq': _L0_xattn_in['bq'], 'L0_xattn_Wk': _L0_xattn_in['Wk'], 'L0_xattn_bk': _L0_xattn_in['bk'], 'L0_xattn_Wv': _L0_xattn_in['Wv'], 'L0_xattn_bv': _L0_xattn_in['bv'], 'L0_xattn_Wo': _L0_xattn_in['Wo'], 'L0_xattn_bo': _L0_xattn_in['bo'], 'L0_ffn_Wr': _L0_ffn_in['Wr'], 'L0_ffn_br': _L0_ffn_in['br'], 'L0_ffn_W1': _L0_ffn_in['W1'], 'L0_ffn_W2': _L0_ffn_in['W2']}

def reference(x, ctx_1024, mask_BxSxS2_if1, g_xattn, g_ffn, L0_xattn_Wq, L0_xattn_bq, L0_xattn_Wk, L0_xattn_bk, L0_xattn_Wv, L0_xattn_bv, L0_xattn_Wo, L0_xattn_bo, L0_ffn_Wr, L0_ffn_br, L0_ffn_W1, L0_ffn_W2):
    import jax
    import jax.numpy as jnp

    def _L0_xattn_ref(q, k, v, mask, Wq, bq, Wk, bk, Wv, bv, Wo, bo):
        import jax, jax.numpy as jnp
        import numpy as np
        HIDDEN = 256
        HEADS = 16
        D_K = HIDDEN // HEADS
        B, S = (2, 512)

        def _split_heads(x):
            b, s, _ = x.shape
            return x.reshape(b, s, HEADS, D_K).transpose(0, 2, 1, 3)
        qh = _split_heads(q @ Wq.T + bq)
        kh = _split_heads(k @ Wk.T + bk)
        vh = _split_heads(v @ Wv.T + bv)
        scores = jnp.einsum('bhqd,bhkd->bhqk', qh, kh) / np.sqrt(D_K).astype(np.float32)
        scores = jnp.where(mask[:, None, :, :] == 0, jnp.float32(-1000000000.0), scores)
        probs = jax.nn.softmax(scores, axis=-1)
        ctx = jnp.einsum('bhqk,bhkd->bhqd', probs, vh)
        concat = ctx.transpose(0, 2, 1, 3).reshape(q.shape[0], -1, HIDDEN)
        return concat @ Wo.T + bo

    def _L0_ffn_ref(hidden_states, Wr, br, W1, W2):
        import jax, jax.numpy as jnp
        import numpy as np
        B, S, H, FFN, E = (2, 512, 256, 1024, 8)
        b, s, h = hidden_states.shape
        x = hidden_states.reshape(-1, h)
        route = jax.nn.sigmoid(x @ Wr + br)
        max_prob = jnp.max(route, axis=1, keepdims=True)
        max_ind = jnp.argmax(route, axis=1)
        out = jnp.zeros_like(x)
        n_experts = Wr.shape[1]
        for e in range(n_experts):
            mask = (max_ind == e)[:, None].astype(x.dtype)
            y = jax.nn.gelu(x @ W1[e], approximate=False) @ W2[e]
            out = out + mask * y
        out = out * max_prob
        return out.reshape(b, s, h)
    x = x + jnp.tanh(g_xattn[0]) * _L0_xattn_ref(_layernorm(x, axis=-1), ctx_1024, ctx_1024, mask_BxSxS2_if1, L0_xattn_Wq, L0_xattn_bq, L0_xattn_Wk, L0_xattn_bk, L0_xattn_Wv, L0_xattn_bv, L0_xattn_Wo, L0_xattn_bo)
    x = x + jnp.tanh(g_ffn[0]) * _L0_ffn_ref(_layernorm(x, axis=-1), L0_ffn_Wr, L0_ffn_br, L0_ffn_W1, L0_ffn_W2)
    return x

_drawn_inputs = setup_inputs


def setup_inputs(seed=0):
    import zlib

    import numpy as np

    out = dict(_drawn_inputs(seed))
    spreads = {'L0_xattn_bq': (0.0, 0.366),
     'L0_xattn_bk': (0.0, 0.8),
     'L0_xattn_bv': (0.0, 0.1),
     'L0_xattn_bo': (0.0, 0.1),
     'L0_ffn_br': (0.0, 0.1)}
    factors = {}
    for name, (base, spread) in spreads.items():
        noise = np.random.default_rng([zlib.crc32(name.encode()), seed]).standard_normal(out[name].shape)
        drawn = base * np.exp(spread * noise) if base else spread * noise
        out[name] = jnp.asarray(drawn.astype(out[name].dtype))
    for name, factor in factors.items():
        out[name] = (out[name] * factor).astype(out[name].dtype)
    return out
```

```python
import concourse.bass as bass
from concourse import mybir
from contextlib import ExitStack

B, S, H = 4, 1024, 256
SK = 64
NH, DK = 16, 16
E, F = 8, 1024
P = 128
HC = H // P
BLK, T = 512, 4
NBLK = B * S // BLK
NPAIR = NH // 2
BIG = float(2.0 ** 100)
TT = 256
CAP = B * S + TT
NT = (B * S + E * (TT - 1)) // TT
MIN_TILES = B * S // TT
SPARE = (NT - MIN_TILES) * TT
BINS = E * CAP + SPARE
C_MEAN, C_RSTD, C_COEF, C_ID, ROW = H, H + 1, H + 2, H + 3, H + 4
NO_TOKEN = float(1 << 20)
FC = F // P
EPS = 1e-5


class Blk:

    def __init__(self, m, h):
        self.m, self.h, self.k = m, h, 2 * m + h


def wait(eng, sem, value, passed=None):
    if not isinstance(value, int) or value > 0:
        eng.wait_ge(sem, value)
        if passed is not None and not isinstance(value, int):
            eng.sem_inc(passed, 1)


def run_blocks(eng, step):
    step(Blk(0, 0), None, None)
    step(Blk(0, 1), Blk(0, 0), None)
    with eng.Fori(0, B - 1) as i:
        step(Blk(i + 1, 0), Blk(i, 1), Blk(i, 0))
        step(Blk(i + 1, 1), Blk(i + 1, 0), Blk(i, 1))
    step(None, Blk(B - 1, 1), Blk(B - 1, 0))
    step(None, None, Blk(B - 1, 1))


def run_tiles(eng, step):
    assert NT % 2 == 1
    step(Blk(0, 0), None, None)
    step(Blk(0, 1), Blk(0, 0), None)
    step(Blk(1, 0), Blk(0, 1), Blk(0, 0))
    with eng.Fori(0, (NT - 3) // 2) as i:
        step(Blk(i + 1, 1), Blk(i + 1, 0), Blk(i, 1))
        step(Blk(i + 2, 0), Blk(i + 1, 1), Blk(i + 1, 0))
    last = (NT - 1) // 2
    step(None, Blk(last, 0), Blk(last - 1, 1))
    step(None, None, Blk(last, 0))


POOL_CONST, SETUP_DVE, NCONST = 24, 36, 16


class Chain:

    def __init__(self, eng, sem, per):
        self.eng, self.sem, self.per = eng, sem, per

    def begin(self, k):
        self.base, self.n = self.per * k, 0

    def add(self, ins):
        self.n += 1
        return ins.then_inc(self.sem, 1)

    def sync(self):
        self.eng.wait_ge(self.sem, self.base + self.n)

    def link(self, ins):
        self.add(ins)
        self.sync()

    def end(self):
        assert self.n == self.per, (self.n, self.per)


def build(nc, x, ctxT, mask, maskT, g_xattn, g_ffn, WqT, bq, WkT, bk, WvT, bv, WoT, bo, Wr, br, W1, W2, out):
    f32, f32r, bf16, i32 = mybir.dt.float32, mybir.dt.float32r, mybir.dt.bfloat16, mybir.dt.int32
    ALU, ACT, AX = mybir.AluOpType, mybir.ActivationFunctionType, mybir.AxisListType

    bins = nc.dram_tensor("bins", (BINS, ROW), f32, kind="Internal").ap()
    x_v = x.rearrange("b (h t p) c -> (b h) p t c", h=2, t=T)
    mask_v = mask.rearrange("b (h t p) s -> (b h) p t s", h=2, t=T)
    maskT_v = maskT.rearrange("b s (h n) -> b h s n", h=2)
    W1_v = W1.rearrange("e (c p) n -> e p c n", p=P)
    W2_v = W2.rearrange("e (c p) n -> e p c n", p=P)
    out_rows = out.rearrange("b s c -> (b s) c")

    ctx = ExitStack()
    with ctx:
        def sem(name):
            return ctx.enter_context(nc.semaphore(name))

        def sb(name, shape, dt, scope=ctx):
            return scope.enter_context(nc.sbuf_tensor(name, shape, dt))

        bank = {n: ctx.enter_context(nc.psum_tensor(n, [P, 512], f32))
                for n in ("X0", "X1", "S0", "S1", "T0", "T1", "O0", "O1")}
        X, SC, TS, O = ([bank[f"{n}{i}"] for i in range(2)] for n in "XSTO")

        identf = sb("identf", [P, P], f32)
        padding = sb("padding", [P, ROW], f32)
        tab = sb("tab", [P, 2, NT], i32)
        padrow = sb("padrow", [P, E], i32)
        w1_raw = [sb(f"w1_raw{i}", [P, HC, F], f32) for i in range(2)]
        w2_raw = [sb(f"w2_raw{i}", [P, FC, H], f32) for i in range(2)]

        A = ExitStack()
        ident_bf = sb("ident_bf", [P, P], bf16, A)
        ones_bf = sb("ones_bf", [P, P], bf16, A)
        before_bf = sb("before_bf", [P, P], bf16, A)
        ones_row = sb("ones_row", [1, P], f32, A)
        headmask = sb("headmask", [P, NH // 2], f32, A)
        halfmask = sb("halfmask", [P, 2], f32, A)
        sel = sb("sel", [SK + NH, NPAIR, 2 * SK], f32r, A)
        ecap = sb("ecap", [P, E], f32, A)
        ecap_i = sb("ecap_i", [P, E], i32, A)
        base = sb("base", [P, E], f32, A)
        tokid = sb("tokid", [P, T], f32, A)
        tokid_i = sb("tokid_i", [P, T], i32, A)
        prio = sb("prio", [P, E], f32, A)
        prio_i = sb("prio_i", [P, E], i32, A)
        half_exp = sb("half_exp", [P, T], f32, A)
        tg = sb("tg", [P, 2], f32, A)
        tgt = sb("tgt", [P, 2], f32, A)
        bq_c = sb("bq_c", [P, HC], f32, A)
        bk_c = sb("bk_c", [P, HC], f32, A)
        bv_r = sb("bv_r", [1, H], f32, A)
        bo_r = sb("bo_r", [1, H], f32, A)
        br_r = sb("br_r", [1, E], f32, A)
        wr_sb = sb("wr_sb", [P, HC, E], f32, A)
        wq_h = sb("wq_h", [P, HC, H], f32r, A)
        wq_l = sb("wq_l", [P, HC, H], f32r, A)
        wo_h = sb("wo_h", [P, HC, H], f32r, A)
        wo_l = sb("wo_l", [P, HC, H], f32r, A)
        bo_b = sb("bo_b", [P, H], f32, A)
        kT = sb("kT", [P, HC, B, SK], f32, A)
        kT_h = sb("kT_h", [P, HC, B, SK], f32r, A)
        kT_l = sb("kT_l", [P, HC, B, SK], f32r, A)
        kbd = sb("kbd", [P, B, HC, (NH // 2) * SK], f32r, A)
        kp_h = sb("kp_h", [P, HC, 2 * SK], f32r, A)
        kp_l = sb("kp_l", [P, HC, 2 * SK], f32r, A)
        v_h = sb("v_h", [P, B, H], f32r, A)
        v_l = sb("v_l", [P, B, H], f32r, A)
        vbd_h = sb("vbd_h", [P, NPAIR, P], f32r, A)
        vbd_l = sb("vbd_l", [P, NPAIR, P], f32r, A)
        xt = [sb(f"xt{i}", [P, T, H], f32, A) for i in range(2)]
        xb = [sb(f"xb{i}", [P, T, H], f32, A) for i in range(2)]
        mi = [sb(f"mi{i}", [P, T, SK], i32, A) for i in range(2)]
        miT = [sb(f"miT{i}", [SK, BLK], i32, A) for i in range(2)]
        mb = [sb(f"mb{i}", [P, T, SK], bf16, A) for i in range(2)]
        mx = [sb(f"mx{i}", [SK + NH, BLK], f32r, A) for i in range(2)]
        st = sb("st", [P, T, 6], f32, A)
        mv = sb("mv", [P, T, 2], f32, A)
        ve = sb("ve", [P, T], f32, A)
        rs = sb("rs", [P, T], f32, A)
        xn = sb("xn", [P, T, H], f32, A)
        xnT_h = sb("xnT_h", [P, HC, BLK], f32r, A)
        xnT_l = sb("xnT_l", [P, HC, BLK], f32r, A)
        q_h = [sb(f"q_h{i}", [P, HC, BLK], f32r, A) for i in range(2)]
        q_l = [sb(f"q_l{i}", [P, HC, BLK], f32r, A) for i in range(2)]
        smax = sb("smax", [P, T, NH], f32, A)
        NPB = 4
        p_f = [sb(f"p_f{i}", [P, BLK], f32, A) for i in range(NPB)]
        p_h = [sb(f"p_h{i}", [P, BLK], f32r, A) for i in range(NPB)]
        p_l = [sb(f"p_l{i}", [P, BLK], f32r, A) for i in range(NPB)]
        rden = sb("rden", [P // 2, BLK], f32, A)
        cn = sb("cn", [P, HC, BLK], f32, A)
        c_h = sb("c_h", [P, HC, BLK], f32r, A)
        c_l = sb("c_l", [P, HC, BLK], f32r, A)
        pay = [sb(f"pay{i}", [P, T, ROW], f32, A) for i in range(2)]
        st2 = sb("st2", [P, T, 6], f32, A)
        mv2 = sb("mv2", [P, T, 2], f32, A)
        ve2 = sb("ve2", [P, T], f32, A)
        xn2 = sb("xn2", [P, T, H], f32, A)
        xn2T = sb("xn2T", [P, HC, BLK], f32, A)
        ez = sb("ez", [P, T, E], f32, A)
        e1 = sb("e1", [P, T, E], f32, A)
        pr = sb("pr", [P, T, E], f32, A)
        pm = sb("pm", [P, T], f32, A)
        eq = sb("eq", [P, T, E], f32, A)
        w_ = sb("w_", [P, T, E], f32, A)
        wm = sb("wm", [P, T], f32, A)
        onehot = sb("onehot", [P, T + 1, E], bf16, A)
        rk = sb("rk", [P, T, E], f32, A)
        rsel = sb("rsel", [P, T, E], f32, A)
        slot_f = sb("slot_f", [P, T], f32, A)
        slot = [sb(f"slot{i}", [P, T], i32, A) for i in range(2)]
        th_i = sb("th_i", [P, MIN_TILES], i32, A)
        th = sb("th", [P, MIN_TILES], f32, A)
        cnt = sb("cnt", [P, E], f32, A)
        over = sb("over", [P, E, MIN_TILES], f32, A)
        ntl = sb("ntl", [P, E], f32, A)
        tri = sb("tri", [P, E, E], f32, A)
        ctri = sb("ctri", [P, E, E], f32, A)
        cend = sb("cend", [P, E], f32, A)
        ti_i = sb("ti_i", [P, NT], i32, A)
        ti = sb("ti", [P, NT], f32, A)
        ge = sb("ge", [P, NT, E], f32, A)
        gen = sb("gen", [P, NT, E], f32, A)
        et = sb("et", [P, NT], f32, A)
        cs = sb("cs", [P, NT], f32, A)
        row_f = sb("row_f", [P, 2, NT], f32, A)
        s = {n: sem(n) for n in (
            "consts_in", "x_in0", "x_in1", "m_in0", "m_in1",
            "pool_const", "setup_dve", "setup_act", "setup_pe",
            "mask_ready", "xb_done", "rstd_ready", "rstd2_ready", "k_ready", "v_ready",
            "stat_ready", "xn_ready", "xT_done", "xnT_hi", "xnT_ready", "q_done", "q_hi", "q_ready",
            "tok_scored", "max_done", "mxT_done", "mx_ready",
            "tsc_done", "exp_done", "p_hi", "p_split", "pv_done", "ctx_done", "ctx_ready", "wo_done", "x1_done",
            "stat2_ready", "xn2_ready", "x2T_done", "xn2T_ready", "lg_done", "ez_ready", "pay_ready",
            "onehot_ready", "rank_done", "slot_ready", "scat0", "scat1",
            "stats1", "stats2", "eps1", "eps2", "chain_ctx", "chain_route", "chain_slot", "chain_tab", "chain_tab2",
            "tab_ready", "osc0", "osc1", "pool_passed", "sp_passed", "dve_passed",
            "w1_in0", "w1_in1", "w2_in0", "w2_in1", "g_in0", "g_in1",
            "w1_hi", "w1_ready", "w2_hi", "w2_ready", "xe_ready", "xeT_done", "xeT_hi", "xeT_ready",
            "l1_done", "gelu_done", "h_hi", "h_ready", "y_done", "o_ready",
        )}
        x_in = [s["x_in0"], s["x_in1"]]
        m_in = [s["m_in0"], s["m_in1"]]
        scat = [s["scat0"], s["scat1"]]

        sel_f = cn[0:SK + NH].rearrange("p c n -> p (c n)").rearrange("p (j h k) -> p j h k", h=2, k=SK)
        ctx_t = xn2T[:].rearrange("p c (b d k) -> p c b d k", b=B, d=2)
        wos, wv_t = xn[:, 0:HC, :], xn[:, HC:2 * HC, :]
        wk_t, wq_t = xn2[:, 0:HC, :], xn2[:, HC:2 * HC, :]
        wo_t = xb[0][:, 0:HC, :]

        with nc.Block() as blk:
            @blk.sync
            def _(sp):
                def const(dst, src):
                    sp.dma_start(dst, src).then_inc(s["consts_in"], 16)

                def load(b):
                    wait(sp, s["xn_ready"], T * (b.k - 1))
                    wait(sp, s["xb_done"], b.k - 1)
                    sp.dma_start(xt[b.h][:], x_v[b.k]).then_inc(x_in[b.h], 16)
                    wait(sp, s["mask_ready"], 2 * (b.k - 1))
                    sp.dma_start(mi[b.h][:], mask_v[b.k]).then_inc(m_in[b.h], 16)
                    sp.dma_start(miT[b.h][:], maskT_v[b.m, b.h]).then_inc(m_in[b.h], 16)

                load(Blk(0, 0))
                for d in range(2):
                    for c in range(HC):
                        const(ctx_t[:, c, :, d, :], ctxT[c * P:(c + 1) * P, :].rearrange("p (b k) -> p b k", b=B))
                for t, w in ((wk_t, WkT), (wv_t, WvT), (wq_t, WqT), (wo_t, WoT), (wr_sb[:], Wr)):
                    const(t, w.rearrange("(c p) n -> p c n", p=P))
                const(tg[:, 0:1], g_xattn.partition_broadcast(P))
                const(tg[:, 1:2], g_ffn.partition_broadcast(P))
                const(bq_c[:], bq)
                const(bk_c[:], bk)
                const(bv_r[:], bv)
                const(bo_r[:], bo)
                const(br_r[:], br)
                load(Blk(0, 1))
                with sp.Fori(0, B - 1) as i:
                    for h in range(2):
                        load(Blk(i + 1, h))

            @blk.gpsimd
            def _(pool):
                n = 0

                def done(ins):
                    nonlocal n
                    n += 1
                    ins.then_inc(s["pool_const"], 1)

                def sync():
                    pool.wait_ge(s["pool_const"], n)

                done(pool.memset(identf[:], 0.0))
                done(pool.memset(padding[:], 0.0))
                done(pool.memset(ones_bf[:], 1.0))
                done(pool.memset(before_bf[:], 1.0))
                done(pool.memset(ones_row[:], 1.0))
                done(pool.memset(headmask[:], 1.0))
                done(pool.memset(sel_f, 0.0))
                done(pool.memset(half_exp[:], -0.5))
                done(pool.memset(onehot[:], 0.0))
                done(pool.memset(tri[:], 1.0))
                done(pool.iota(ecap_i[:], [[CAP, E]], base=0, channel_multiplier=0))
                done(pool.iota(tokid_i[:], [[P, T]], base=0, channel_multiplier=1))
                done(pool.iota(prio_i[:], [[-1, E]], base=E, channel_multiplier=0))
                done(pool.iota(th_i[:], [[TT, MIN_TILES]], base=0, channel_multiplier=0))
                done(pool.iota(ti_i[:], [[1, NT]], base=0, channel_multiplier=0))
                sync()
                done(pool.memset(padding[:, C_ID:C_ID + 1], NO_TOKEN))
                done(pool.affine_select(out=identf[:], in_=identf[:], compare_op=ALU.not_equal, fill=1.0,
                                        base=0, pattern=[[-1, P]], channel_multiplier=1))
                done(pool.affine_select(out=before_bf[:], in_=before_bf[:], compare_op=ALU.is_gt, fill=0.0,
                                        base=0, pattern=[[1, P]], channel_multiplier=-1))
                done(pool.affine_select(out=headmask[:], in_=headmask[:], compare_op=ALU.is_ge, fill=0.0,
                                        base=0, pattern=[[-DK, NH // 2]], channel_multiplier=1))
                done(pool.affine_select(out=sel_f[0:SK], in_=sel_f[0:SK], compare_op=ALU.not_equal, fill=1.0,
                                        base=0, pattern=[[0, NPAIR], [0, 2], [-1, SK]], channel_multiplier=1))
                sync()
                done(pool.affine_select(out=sel_f[SK:SK + NH], in_=sel_f[SK:SK + NH], compare_op=ALU.not_equal,
                                        fill=-1.0, base=0, pattern=[[-2, NPAIR], [-1, 2], [0, SK]],
                                        channel_multiplier=1))
                sync()
                done(pool.affine_select(out=tri[:], in_=tri[:], compare_op=ALU.is_ge, fill=0.0,
                                        base=0, pattern=[[1, E], [-1, E]], channel_multiplier=0))
                sync()
                done(pool.affine_select(out=headmask[:], in_=headmask[:], compare_op=ALU.is_ge, fill=0.0,
                                        base=DK - 1, pattern=[[DK, NH // 2]], channel_multiplier=-1))
                done(pool.tensor_copy(ident_bf[:], identf[:]))
                assert n == POOL_CONST
                sync()
                half = SPARE // 2
                for h in range(2):
                    pool.dma_start(bins[E * CAP + h * half:E * CAP + (h + 1) * half, :].rearrange("(n p) c -> p n c", p=P),
                                   padding[:].unsqueeze(1).broadcast_to([P, half // P, ROW])).then_inc(scat[h], 16)

                def masks(b):
                    wait(pool, m_in[b.h], 32 * (b.m + 1), s["pool_passed"])
                    wait(pool, s["tok_scored"], 2 * T * (b.k - 1), s["pool_passed"])
                    pool.tensor_scalar(mb[b.h][:], mi[b.h][:], 0.0, -BIG, ALU.is_equal, ALU.mult)\
                        .then_inc(s["mask_ready"], 1)
                    wait(pool, s["tsc_done"], NPAIR * (b.k - 1), s["pool_passed"])
                    pool.tensor_scalar(mx[b.h][0:SK, :], miT[b.h][:], 0.0, -BIG, ALU.is_equal, ALU.mult)\
                        .then_inc(s["mask_ready"], 1)

                def xbias(b):
                    wait(pool, x_in[b.h], 16 * (b.m + 1), s["pool_passed"])
                    wait(pool, s["x1_done"], 2 * (b.k - 1), s["pool_passed"])
                    pool.tensor_tensor(xb[b.h][:], xt[b.h][:], bo_b[:].unsqueeze(1).broadcast_to([P, T, H]),
                                       ALU.add).then_inc(s["xb_done"], 1)

                def rstd(b, moments, eps_out, result, ready, done_, steps):
                    wait(pool, ready, T * (b.k + 1), s["pool_passed"])
                    pool.tensor_scalar(eps_out[:], moments[:, :, 1], EPS, None, ALU.add).then_inc(steps, 1)
                    wait(pool, steps, b.k + 1, s["pool_passed"])
                    pool.tensor_tensor(result, eps_out[:], half_exp[:], ALU.pow).then_inc(done_, 1)

                def keys(m):
                    wait(pool, s["tsc_done"], NPAIR * 2 * m, s["pool_passed"])
                    for src, dst in ((kT_h, kp_h), (kT_l, kp_l)):
                        for c in range(HC):
                            pool.tensor_tensor(
                                dst[:, c, :].rearrange("p (h k) -> p h k", h=2),
                                src[:, c, m, :].bitcast(f32).unsqueeze(1).broadcast_to([P, 2, SK]),
                                halfmask[:].unsqueeze(2).broadcast_to([P, 2, SK]), ALU.mult)\
                                .then_inc(s["k_ready"], 1)

                def scatter(b):
                    wait(pool, s["slot_ready"], b.k + 1, s["pool_passed"])
                    wait(pool, s["pay_ready"], 2 * (b.k + 1), s["pool_passed"])
                    wait(pool, s["rstd2_ready"], b.k + 1, s["pool_passed"])
                    for t in range(T):
                        pool.indirect_dma_start(
                            out=bins, out_offset=bass.IndirectOffsetOnAxis(ap=slot[b.h][:, t:t + 1], axis=0),
                            in_=pay[b.h][:, t, :], in_offset=None).then_inc(scat[b.h], 16)

                def step(a, b, c):
                    if b is not None and b.h == 0:
                        keys(b.m)
                    if a is not None:
                        masks(a)
                        rstd(a, mv, ve, rs[:], s["stat_ready"], s["rstd_ready"], s["eps1"])
                        xbias(a)
                    if c is not None:
                        scatter(c)
                    if b is not None:
                        rstd(b, mv2, ve2, pay[b.h][:, :, C_RSTD], s["stat2_ready"], s["rstd2_ready"], s["eps2"])

                wait(pool, s["setup_dve"], SETUP_DVE, s["pool_passed"])
                run_blocks(pool, step)
                for h in range(2):
                    wait(pool, scat[h], 16 + 16 * T * NBLK // 2, s["pool_passed"])

            @blk.scalar
            def _(act):
                act.wait_ge(s["consts_in"], 16 * NCONST)
                act.activation(tgt[:], tg[:], ACT.Tanh).then_inc(s["setup_act"], 1)

                def xn_hi(a):
                    for c in range(HC):
                        act.wait_ge(s["xT_done"], HC * a.k + c + 1)
                        wait(act, s["q_done"], HC * a.k)
                        act.copy(xnT_h[:, c, :], X[c][:]).then_inc(s["xnT_hi"], 1)

                def q_hi(a):
                    for c in range(HC):
                        act.wait_ge(s["q_done"], HC * a.k + c + 1)
                        wait(act, s["tsc_done"], NPAIR * (a.k - 1))
                        act.activation(q_h[a.h][:, c, :], X[c][:], ACT.Identity, bias=bq_c[:, c:c + 1])\
                           .then_inc(s["q_hi"], 1)

                def maxima(a):
                    act.wait_ge(s["mxT_done"], a.k + 1)
                    act.copy(mx[a.h][SK:SK + NH, :], SC[0][0:NH, :]).then_inc(s["mx_ready"], 1)

                def exps(b, g):
                    for j in (2 * g, 2 * g + 1):
                        n = NPAIR * b.k + j
                        act.wait_ge(s["tsc_done"], n + 1)
                        wait(act, s["p_split"], n - NPB + 1)
                        act.activation(p_f[j % NPB][:], TS[j % 2][:], ACT.Exp).then_inc(s["exp_done"], 1)

                def xn2_copy(c):
                    for i in range(HC):
                        act.wait_ge(s["x2T_done"], HC * c.k + i + 1)
                        act.copy(xn2T[:, i, :], X[i][:]).then_inc(s["xn2T_ready"], 1)

                def route_exp(c):
                    act.wait_ge(s["lg_done"], c.k + 1)
                    act.activation(ez[:].rearrange("p t e -> p (t e)"), O[0][:, 0:T * E], ACT.Exp, scale=-1.0)\
                       .then_inc(s["ez_ready"], 1)

                def step(a, b, c):
                    if c is not None:
                        xn2_copy(c)
                    if b is not None:
                        exps(b, 0)
                    if a is not None:
                        xn_hi(a)
                    if c is not None:
                        route_exp(c)
                    if a is not None:
                        q_hi(a)
                    if b is not None:
                        for g in range(1, 4):
                            exps(b, g)
                    if a is not None:
                        maxima(a)

                act.wait_ge(s["setup_dve"], SETUP_DVE)
                run_blocks(act, step)

            @blk.vector
            def _(dve):
                su = Chain(dve, s["setup_dve"], SETUP_DVE)
                su.begin(0)
                dve.wait_ge(s["pool_const"], POOL_CONST)
                dve.wait_ge(s["consts_in"], 16 * NCONST)
                su.add(dve.tensor_copy(ecap[:], ecap_i[:]))
                su.add(dve.tensor_copy(base[:], ecap_i[:]))
                su.add(dve.tensor_copy(tokid[:], tokid_i[:]))
                su.add(dve.tensor_copy(prio[:], prio_i[:]))
                su.add(dve.tensor_copy(th[:], th_i[:]))
                su.add(dve.tensor_copy(ti[:], ti_i[:]))
                su.add(dve.tensor_copy(sel[:], sel_f.rearrange("p j h k -> p j (h k)")))
                su.add(dve.tensor_reduce(halfmask[:], headmask[:].rearrange("p (a h) -> p h a", h=2), AX.X, ALU.add))
                su.add(dve.tensor_copy(wq_h[:], wq_t))
                su.add(dve.memset(vbd_h[:].bitcast(f32), 0.0))
                su.add(dve.memset(vbd_l[:].bitcast(f32), 0.0))
                dve.wait_ge(s["setup_act"], 1)
                su.add(dve.tensor_scalar(wos, wo_t, tgt[:, 0:1], None, ALU.mult))
                su.sync()
                su.add(dve.tensor_tensor(wq_l[:], wq_t, wq_h[:].bitcast(f32), ALU.subtract))
                su.add(dve.tensor_copy(wo_h[:], wos))
                for h2 in range(2):
                    for j2 in range(2):
                        o = SK + 32 * j2 + DK * h2
                        su.add(dve.memset(vbd_h[h2 * SK:(h2 + 1) * SK].rearrange("p (g j) c -> p g j c", j=2)
                                          [:, :, j2, o:o + DK].bitcast(f32), 1.0))
                su.sync()
                su.add(dve.tensor_tensor(wo_l[:], wos, wo_h[:].bitcast(f32), ALU.subtract))
                for c in range(HC):
                    dve.wait_ge(s["setup_pe"], c + 1)
                    su.add(dve.tensor_scalar(kT[:, c], X[c][:, 0:B * SK].rearrange("p (b k) -> p b k", b=B),
                                             bk_c[:, c:c + 1], DK ** -0.5, ALU.add, ALU.mult))
                su.sync()
                su.link(dve.tensor_copy(kT_h[:], kT[:]))
                su.link(dve.tensor_tensor(kT_l[:], kT[:], kT_h[:].bitcast(f32), ALU.subtract))
                for b in range(B):
                    for c in range(HC):
                        su.add(dve.tensor_tensor(
                            kbd[:, b, c, :].rearrange("p (h k) -> p h k", k=SK),
                            kT_h[:, c, b, :].bitcast(f32).unsqueeze(1).broadcast_to([P, NH // 2, SK]),
                            headmask[:].unsqueeze(2).broadcast_to([P, NH // 2, SK]), ALU.mult))
                for n in range(2):
                    dve.wait_ge(s["setup_pe"], 3 + n)
                    o = SC[n][:].rearrange("p (b c) -> p b c", b=2)
                    su.link(dve.tensor_copy(v_h[:, 2 * n:2 * n + 2, :], o))
                    su.add(dve.tensor_tensor(v_l[:, 2 * n:2 * n + 2, :], o, v_h[:, 2 * n:2 * n + 2, :].bitcast(f32),
                                             ALU.subtract))
                dve.wait_ge(s["setup_pe"], 5)
                su.link(dve.tensor_scalar(bo_b[:], O[0][:, 0:H], tgt[:, 0:1], None, ALU.mult))
                su.end()

                def place_values(m):
                    wait(dve, s["pv_done"], NPAIR * 2 * m)
                    for src, dst in ((v_h, vbd_h), (v_l, vbd_l)):
                        for h2 in range(2):
                            r = slice(h2 * SK, (h2 + 1) * SK)
                            for j2 in range(2):
                                dve.tensor_copy(
                                    dst[r].rearrange("p (g j) c -> p g j c", j=2)[:, :, j2, 32 * j2 + DK * h2:32 * j2 + DK * h2 + DK],
                                    src[r, m, :].rearrange("p (g j h d) -> p g j h d", j=2, h=2, d=DK)[:, :, j2, h2, :])\
                                    .then_inc(s["v_ready"], 1)

                def norm_stats(b, src, stats, moments, ready, ch):
                    for t in range(T):
                        ch.add(dve.bn_stats(stats[:, t, :], src[:, t, 0:H]))
                    wait(dve, ch.sem, ch.base + ch.n, s["dve_passed"])
                    for t in range(T):
                        dve.bn_aggr(moments[:, t, :], stats[:, t, :]).then_inc(ready, 1)

                def normalize(b, src, moments, r, dst, ready, rstd_done):
                    dve.wait_ge(rstd_done, b.k + 1)
                    dve.wait_ge(s["stat_ready"] if dst is xn else s["stat2_ready"], T * (b.k + 1))
                    for t in range(T):
                        dve.tensor_scalar(dst[:, t, :], src[:, t, 0:H], moments[:, t, 0:1], r(t),
                                          ALU.subtract, ALU.mult).then_inc(ready, 1)

                lnc = Chain(dve, s["stats1"], T)
                ln2c = Chain(dve, s["stats2"], T)

                def norm1(a):
                    dve.wait_ge(x_in[a.h], 16 * (a.m + 1))
                    lnc.begin(a.k)
                    norm_stats(a, xt[a.h], st, mv, s["stat_ready"], lnc)
                    wait(dve, s["xT_done"], HC * a.k)
                    normalize(a, xt[a.h], mv, lambda t: rs[:, t:t + 1], xn, s["xn_ready"], s["rstd_ready"])

                def xn_lo(a):
                    for c in range(HC):
                        dve.wait_ge(s["xnT_hi"], HC * a.k + c + 1)
                        dve.tensor_tensor(xnT_l[:, c, :], X[c][:], xnT_h[:, c, :].bitcast(f32), ALU.subtract)\
                           .then_inc(s["xnT_ready"], 1)

                def q_lo(a):
                    for c in range(HC):
                        dve.wait_ge(s["q_hi"], HC * a.k + c + 1)
                        dve.scalar_tensor_tensor(q_l[a.h][:, c, :], X[c][:], bq_c[:, c:c + 1],
                                                 q_h[a.h][:, c, :].bitcast(f32), ALU.add, ALU.subtract)\
                           .then_inc(s["q_ready"], 1)

                def maxes(a, t):
                    for c in range(HC):
                        n = HC * T * a.k + HC * t + c
                        dve.wait_ge(s["tok_scored"], n + 1)
                        if t == 0 and c == 0:
                            wait(dve, s["mxT_done"], a.k)
                        dve.tensor_reduce(smax[:, t, c * 8:c * 8 + 8], SC[c][:].rearrange("p (h k) -> p h k", k=SK),
                                          AX.X, ALU.max).then_inc(s["max_done"], 1)

                def split(b, g):
                    for j in (2 * g, 2 * g + 1):
                        n = NPAIR * b.k + j
                        i = j % NPB
                        dve.wait_ge(s["exp_done"], n + 1)
                        wait(dve, s["pv_done"], n - NPB + 1)
                        dve.tensor_copy(p_h[i][:], p_f[i][:]).then_inc(s["p_hi"], 1)
                        dve.wait_ge(s["p_hi"], n + 1)
                        dve.tensor_tensor(p_l[i][:], p_f[i][:], p_h[i][:].bitcast(f32), ALU.subtract)\
                           .then_inc(s["p_split"], 1)

                cch = Chain(dve, s["chain_ctx"], 4 + HC)

                def context(b, g):
                    if g == 0:
                        cch.begin(b.k)
                    dve.wait_ge(s["pv_done"], NPAIR * b.k + 2 * g + 2)
                    o, r = O[g % 2], slice(64 * (g % 2), 64 * (g % 2) + 64)
                    cch.link(dve.reciprocal(rden[:], o[64:128, :]))
                    dve.tensor_tensor(cn[r, g // 2, :], o[0:64, :], rden[:], ALU.mult).then_inc(s["ctx_done"], 1)
                    if g % 2:
                        c = g // 2
                        dve.wait_ge(s["ctx_done"], 4 * b.k + g + 1)
                        if c == 0:
                            wait(dve, s["wo_done"], T * b.k)
                        cch.link(dve.tensor_copy(c_h[:, c, :], cn[:, c, :]))
                        dve.tensor_tensor(c_l[:, c, :], cn[:, c, :], c_h[:, c, :].bitcast(f32), ALU.subtract)\
                           .then_inc(s["ctx_ready"], 1)
                    if g == 3:
                        cch.end()

                def residual(b):
                    for u in range(2):
                        dve.wait_ge(s["wo_done"], T * b.k + 2 * u + 2)
                        if u == 0:
                            dve.wait_ge(scat[b.h], 16 + 16 * T * b.m)
                            dve.wait_ge(s["xb_done"], b.k + 1)
                        dve.tensor_tensor(pay[b.h][:, 2 * u:2 * u + 2, 0:H],
                                          O[u][:].rearrange("p (t c) -> p t c", t=2),
                                          xb[b.h][:, 2 * u:2 * u + 2, :], ALU.add).then_inc(s["x1_done"], 1)

                def norm2(b):
                    ln2c.begin(b.k)
                    dve.wait_ge(s["x1_done"], 2 * (b.k + 1))
                    norm_stats(b, pay[b.h], st2, mv2, s["stat2_ready"], ln2c)
                    wait(dve, s["x2T_done"], HC * b.k)
                    normalize(b, pay[b.h], mv2, lambda t: pay[b.h][:, t, C_RSTD:C_RSTD + 1], xn2,
                              s["xn2_ready"], s["rstd2_ready"])
                    dve.tensor_copy(pay[b.h][:, :, C_MEAN], mv2[:, :, 0]).then_inc(s["pay_ready"], 1)

                rch = Chain(dve, s["chain_route"], 7)

                def route(c):
                    rch.begin(c.k)
                    dve.wait_ge(s["ez_ready"], c.k + 1)
                    rch.link(dve.tensor_scalar(e1[:], ez[:], 1.0, None, ALU.add))
                    rch.link(dve.reciprocal(pr[:], e1[:]))
                    rch.link(dve.tensor_reduce(pm[:], pr[:], AX.X, ALU.max))
                    rch.link(dve.tensor_tensor(eq[:], pr[:], pm[:].unsqueeze(2).broadcast_to([P, T, E]), ALU.is_equal))
                    rch.link(dve.tensor_tensor(w_[:], eq[:], prio[:].unsqueeze(1).broadcast_to([P, T, E]), ALU.mult))
                    rch.link(dve.tensor_reduce(wm[:], w_[:], AX.X, ALU.max))
                    dve.tensor_tensor(onehot[:, 0:T, :], w_[:], wm[:].unsqueeze(2).broadcast_to([P, T, E]),
                                      ALU.is_equal).then_inc(s["onehot_ready"], 1)
                    dve.tensor_scalar(pay[c.h][:, :, C_COEF], pm[:], tgt[:, 1:2], None, ALU.mult)
                    dve.tensor_copy(pay[c.h][:, :, C_ID], tokid[:]).then_inc(s["pay_ready"], 1)
                    rch.link(dve.tensor_scalar(tokid[:], tokid[:], float(BLK), None, ALU.add))
                    rch.end()

                sch = Chain(dve, s["chain_slot"], 4)

                def slots(c):
                    sch.begin(c.k)
                    dve.wait_ge(s["rank_done"], c.k + 1)
                    sch.link(dve.tensor_tensor(rk[:], SC[1][:, 0:T * E].rearrange("p (t e) -> p t e", t=T),
                                               base[:].unsqueeze(1).broadcast_to([P, T, E]), ALU.add))
                    sch.add(dve.tensor_tensor(base[:], base[:], SC[1][:, T * E:(T + 1) * E], ALU.add))
                    sch.add(dve.tensor_tensor(rsel[:], rk[:], onehot[:, 0:T, :], ALU.mult))
                    sch.sync()
                    sch.link(dve.tensor_reduce(slot_f[:], rsel[:], AX.X, ALU.add))
                    sch.end()
                    dve.wait_ge(scat[c.h], 16 + 16 * T * c.m)
                    dve.tensor_copy(slot[c.h][:], slot_f[:]).then_inc(s["slot_ready"], 1)

                def step(a, b, c):
                    if b is not None and b.h == 0:
                        place_values(b.m)
                    if a is not None:
                        norm1(a)
                        xn_lo(a)
                    if a is not None:
                        q_lo(a)
                    if c is not None:
                        route(c)
                    for g in range(4):
                        if b is not None:
                            split(b, g)
                        if a is not None:
                            maxes(a, g)
                        if b is not None:
                            context(b, g)
                    if c is not None:
                        slots(c)
                    if b is not None:
                        residual(b)
                        norm2(b)

                run_blocks(dve, step)

                tc = Chain(dve, s["chain_tab"], 10)
                tc.begin(0)
                dve.wait_ge(s["chain_slot"], 4 * NBLK)
                tc.link(dve.tensor_tensor(cnt[:], base[:], ecap[:], ALU.subtract))
                tc.link(dve.tensor_tensor(over[:], cnt[:].unsqueeze(2).broadcast_to([P, E, MIN_TILES]),
                                          th[:].unsqueeze(1).broadcast_to([P, E, MIN_TILES]), ALU.is_gt))
                tc.link(dve.tensor_reduce(ntl[:], over[:], AX.X, ALU.add))
                tc.link(dve.tensor_tensor(ctri[:], tri[:], ntl[:].unsqueeze(1).broadcast_to([P, E, E]), ALU.mult))
                tc.link(dve.tensor_reduce(cend[:], ctri[:], AX.X, ALU.add))
                tc.link(dve.tensor_tensor(ge[:], cend[:].unsqueeze(1).broadcast_to([P, NT, E]),
                                          ti[:].unsqueeze(2).broadcast_to([P, NT, E]), ALU.is_le))
                tc.add(dve.tensor_reduce(et[:], ge[:], AX.X, ALU.add))
                tc.link(dve.tensor_tensor(gen[:], ge[:], ntl[:].unsqueeze(1).broadcast_to([P, NT, E]), ALU.mult))
                tc.link(dve.tensor_reduce(cs[:], gen[:], AX.X, ALU.add))
                tc.link(dve.tensor_tensor(cs[:], ti[:], cs[:], ALU.subtract))
                tc.end()
                tl = Chain(dve, s["chain_tab2"], 3)
                tl.begin(0)
                tl.link(dve.tensor_scalar(cs[:], cs[:], float(TT), None, ALU.mult))
                tl.add(dve.scalar_tensor_tensor(row_f[:, 0, :], et[:], float(CAP), cs[:], ALU.mult, ALU.add))
                tl.link(dve.tensor_scalar(row_f[:, 1, :], et[:], float(E - 1), None, ALU.min))
                tl.end()
                dve.tensor_copy(padrow[:], base[:])
                dve.tensor_copy(tab[:], row_f[:]).then_inc(s["tab_ready"], 1)
                dve.wait_ge(s["tab_ready"], 1)

            @blk.tensor
            def _(pe):
                pe.wait_ge(s["consts_in"], 16 * NCONST)
                pe.wait_ge(s["pool_const"], POOL_CONST)
                for oc in range(HC):
                    for c in range(HC):
                        mm = pe.matmul(X[oc][:, 0:B * SK], wk_t[:, c, oc * P:(oc + 1) * P],
                                       ctx_t[:, c, :, 0, :], start=(c == 0), stop=(c == HC - 1))
                    mm.then_inc(s["setup_pe"], 1)
                for b in range(B):
                    o = SC[b // 2][:, (b % 2) * H:(b % 2 + 1) * H]
                    pe.matmul(o, ones_row[:], bv_r[:], start=True, stop=False)
                    for c in range(HC):
                        mm = pe.matmul(o, ctx_t[:, c, b].rearrange("p d k -> p (d k)"), wv_t[:, c, :],
                                       start=False, stop=(c == HC - 1))
                    if b % 2:
                        mm.then_inc(s["setup_pe"], 1)
                pe.matmul(O[0][:, 0:H], ones_row[:], bo_r[:], start=True, stop=True).then_inc(s["setup_pe"], 1)
                pe.wait_ge(s["setup_dve"], SETUP_DVE)

                def product(o, terms):
                    for n, (l, r) in enumerate(terms):
                        mm = pe.matmul(o, l, r, start=(n == 0), stop=(n == len(terms) - 1))
                    return mm

                def turn_x(a):
                    for c in range(HC):
                        for t in range(T):
                            if c == 0:
                                pe.wait_ge(s["xn_ready"], T * a.k + t + 1)
                            mm = pe.transpose(X[c][:, t * P:(t + 1) * P], xn[:, t, c * P:(c + 1) * P], identf[:])
                        mm.then_inc(s["xT_done"], 1)

                def queries(a):
                    pe.wait_ge(s["xnT_ready"], HC * (a.k + 1))
                    for oc in range(HC):
                        o = slice(oc * P, (oc + 1) * P)
                        product(X[oc][:], [(w[:, c, o], z[:, c, :]) for c in range(HC) for w, z in
                                           ((wq_h, xnT_h), (wq_l, xnT_h), (wq_h, xnT_l))])\
                            .then_inc(s["q_done"], 1)

                def token_scores(a, t):
                    pe.wait_ge(s["q_hi"], HC * (a.k + 1))
                    pe.wait_ge(s["mask_ready"], 2 * (a.k + 1))
                    for c in range(HC):
                        n = HC * T * a.k + HC * t + c
                        wait(pe, s["max_done"], n - 1)
                        if t == 0 and c == 0:
                            wait(pe, s["mx_ready"], a.k)
                        pe.matmul(SC[c][:], q_h[a.h][:, c, t * P:(t + 1) * P], kbd[:, a.m, c, :],
                                  start=True, stop=False)
                        pe.matmul(SC[c][:], ident_bf[:], mb[a.h][:, t, :].unsqueeze(1).broadcast_to([P, NH // 2, SK]),
                                  start=False, stop=True).then_inc(s["tok_scored"], 1)

                def turn_maxima(a):
                    pe.wait_ge(s["max_done"], HC * T * (a.k + 1))
                    for t in range(T):
                        mm = pe.transpose(SC[0][0:NH, t * P:(t + 1) * P], smax[:, t, :], identf[:])
                    mm.then_inc(s["mxT_done"], 1)

                def key_scores(b, g):
                    if g == 0:
                        pe.wait_ge(s["mx_ready"], b.k + 1)
                        pe.wait_ge(s["k_ready"], 2 * HC * (b.m + 1))
                        pe.wait_ge(s["q_ready"], HC * (b.k + 1))
                    for j in (2 * g, 2 * g + 1):
                        wait(pe, s["exp_done"], NPAIR * b.k + j - 1)
                        pe.matmul(TS[j % 2][:], sel[:, j, :], mx[b.h][:], start=True, stop=False)
                    for n, (kk, qq) in enumerate(((kp_h, q_h), (kp_l, q_h), (kp_h, q_l))):
                        for j in (2 * g, 2 * g + 1):
                            r, c = slice(32 * (j % 4), 32 * (j % 4) + 32), j // 4
                            mm = pe.matmul(TS[j % 2][:], kk[r, c, :], qq[b.h][r, c, :], start=False, stop=(n == 2))
                            if n == 2:
                                mm.then_inc(s["tsc_done"], 1)

                def values(b, g):
                    if g >= 2:
                        pe.wait_ge(s["ctx_done"], 4 * b.k + g - 1)
                    if g == 0:
                        pe.wait_ge(s["v_ready"], 8 * (b.m + 1))
                        wait(pe, s["ez_ready"], b.k)
                        wait(pe, s["x1_done"], 2 * b.k)
                    for j in (2 * g, 2 * g + 1):
                        i = j % NPB
                        pe.wait_ge(s["p_split"], NPAIR * b.k + j + 1)
                        for n, (vv, pp) in enumerate(((vbd_h, p_h), (vbd_l, p_h), (vbd_h, p_l))):
                            mm = pe.matmul(O[g % 2][:], vv[:, j, :], pp[i][:], start=(j % 2 == 0 and n == 0),
                                           stop=(j % 2 == 1 and n == 2))
                        mm.then_inc(s["pv_done"], 1)

                def project(b):
                    pe.wait_ge(s["ctx_ready"], HC * (b.k + 1))
                    for t in range(T):
                        z = slice(t * P, (t + 1) * P)
                        product(O[t // 2][:, (t % 2) * H:(t % 2 + 1) * H],
                                [(l[:, c, z], w[:, c, :]) for c in range(HC) for l, w in
                                 ((c_h, wo_h), (c_h, wo_l), (c_l, wo_h))]).then_inc(s["wo_done"], 1)

                def turn_x2(c):
                    pe.wait_ge(s["q_ready"], HC * min(c.k + 2, NBLK) if isinstance(c.k, int) else HC * (c.k + 2))
                    for i in range(HC):
                        for t in range(T):
                            if i == 0:
                                pe.wait_ge(s["xn2_ready"], T * c.k + t + 1)
                            mm = pe.transpose(X[i][:, t * P:(t + 1) * P], xn2[:, t, i * P:(i + 1) * P], identf[:])
                        mm.then_inc(s["x2T_done"], 1)

                def logits(c):
                    pe.wait_ge(s["xn2T_ready"], HC * (c.k + 1))
                    pe.wait_ge(s["x1_done"], 2 * (c.k + 1))
                    for t in range(T):
                        o = O[0][:, t * E:(t + 1) * E]
                        pe.matmul(o, ones_row[:], br_r[:], start=True, stop=False)
                        for i in range(HC):
                            mm = pe.matmul(o, xn2T[:, i, t * P:(t + 1) * P], wr_sb[:, i, :],
                                           start=False, stop=(i == HC - 1))
                    mm.then_inc(s["lg_done"], 1)

                def ranks(c):
                    pe.wait_ge(s["onehot_ready"], c.k + 1)
                    o = SC[1][:, 0:(T + 1) * E].rearrange("p (t e) -> p t e", e=E)
                    for t in range(T):
                        pe.matmul(o[:, t + 1:T + 1, :], ones_bf[:],
                                  onehot[:, t:t + 1, :].broadcast_to([P, T - t, E]),
                                  start=(t == 0), stop=False, skip_group_check=True)
                    mm = pe.matmul(o, before_bf[:], onehot[:], start=False, stop=True, skip_group_check=True)
                    mm.then_inc(s["rank_done"], 1)

                def step(a, b, c):
                    if c is not None:
                        turn_x2(c)
                    if b is not None:
                        key_scores(b, 0)
                    if a is not None:
                        if c is not None:
                            pe.wait_ge(s["xn2T_ready"], HC * (c.k + 1))
                        wait(pe, s["q_ready"], HC * a.k)
                        turn_x(a)
                    if c is not None:
                        logits(c)
                    if a is not None:
                        queries(a)
                    for g in range(4):
                        if a is not None:
                            token_scores(a, g)
                        if b is not None:
                            values(b, g)
                            if g < 3:
                                key_scores(b, g + 1)
                    if a is not None:
                        turn_maxima(a)
                    if c is not None:
                        ranks(c)
                    if b is not None:
                        project(b)

                run_blocks(pe, step)
        A.close()

        g_sb = [sb(f"g{i}", [P, 2, ROW], f32) for i in range(2)]
        xe = sb("xe", [P, 2, H], f32)
        xeT_h = sb("xeT_h", [P, HC, TT], f32r)
        xeT_l = sb("xeT_l", [P, HC, TT], f32r)
        w1_h = [sb(f"w1_h{i}", [P, HC, F], f32r) for i in range(2)]
        w1_l = [sb(f"w1_l{i}", [P, HC, F], f32r) for i in range(2)]
        w2_h = [sb(f"w2_h{i}", [P, FC, H], f32r) for i in range(2)]
        w2_l = [sb(f"w2_l{i}", [P, FC, H], f32r) for i in range(2)]
        NU = FC // 2
        h_f = [sb(f"h_f{i}", [P, 2, TT], f32) for i in range(NU)]
        h_h = [sb(f"h_h{i}", [P, FC, TT], f32r) for i in range(2)]
        h_l = [sb(f"h_l{i}", [P, FC, TT], f32r) for i in range(2)]
        o_sb = [sb(f"o{i}", [P, 2, H], f32) for i in range(2)]
        o_idx = [sb(f"o_idx{i}", [P, 2], i32) for i in range(2)]
        HB = [bank[n] for n in ("S0", "S1", "T0", "T1")]
        w1_in, w2_in, g_in, osc = ([s[f"{n}{i}"] for i in range(2)] for n in ("w1_in", "w2_in", "g_in", "osc"))

        with nc.Block() as blk:

            @blk.sync
            def _(sp):
                def expert(b):
                    return sp.value_load(tab[0:1, 1, bass.ds(b.k, 1)], min_val=0, max_val=E - 1)

                def load_w1(b):
                    wait(sp, s["w1_ready"], b.k - 1, s["sp_passed"])
                    sp.dma_start(w1_raw[b.h][:], W1_v[bass.ds(expert(b), 1)].rearrange("e p c n -> p (e c) n"))\
                      .then_inc(w1_in[b.h], 16)

                def load_tile(b):
                    wait(sp, s["w2_ready"], b.k - 1, s["sp_passed"])
                    sp.dma_start(w2_raw[b.h][:], W2_v[bass.ds(expert(b), 1)].rearrange("e p c n -> p (e c) n"))\
                      .then_inc(w2_in[b.h], 16)
                    if isinstance(b.k, int) and b.k == 0:
                        for h in range(2):
                            wait(sp, osc[h], 16 * E // 2, s["sp_passed"])
                    wait(sp, s["o_ready"], 2 * (b.k - 1), s["sp_passed"])
                    r = sp.value_load(tab[0:1, 0, bass.ds(b.k, 1)], min_val=0, max_val=BINS - TT)
                    sp.dma_start(g_sb[b.h][:], bins[bass.ds(r, TT), :].rearrange("(n p) c -> p n c", p=P))\
                      .then_inc(g_in[b.h], 16)

                load_w1(Blk(0, 0))
                load_w1(Blk(0, 1))
                load_tile(Blk(0, 0))
                load_w1(Blk(1, 0))
                load_tile(Blk(0, 1))
                with sp.Fori(0, (NT - 3) // 2) as i:
                    load_w1(Blk(i + 1, 1))
                    load_tile(Blk(i + 1, 0))
                    load_w1(Blk(i + 2, 0))
                    load_tile(Blk(i + 1, 1))
                load_tile(Blk((NT - 1) // 2, 0))

            @blk.gpsimd
            def _(pool):
                for e in range(E):
                    r = pool.value_load(padrow[0:1, e:e + 1], min_val=0, max_val=E * CAP - TT)
                    pool.dma_start(bins[bass.ds(r, TT), :].rearrange("(n p) c -> p n c", p=P),
                                 padding[:].unsqueeze(1).broadcast_to([P, TT // P, ROW])).then_inc(osc[e % 2], 16)

                def store(b):
                    wait(pool, s["o_ready"], 2 * (b.k + 1), s["pool_passed"])
                    for t in range(2):
                        pool.indirect_dma_start(
                            out=out_rows, out_offset=bass.IndirectOffsetOnAxis(ap=o_idx[b.h][:, t:t + 1], axis=0),
                            in_=o_sb[b.h][:, t, :], in_offset=None, bounds_check=B * S - 1, oob_is_err=False)\
                            .then_inc(osc[b.h], 16)

                def step(w, a, b):
                    if b is not None:
                        store(b)

                run_tiles(pool, step)
                for h in range(2):
                    wait(pool, osc[h], 16 * E // 2 + 32 * ((NT + 1 - h) // 2), s["pool_passed"])

            @blk.scalar
            def _(act):
                def w1_high(w):
                    act.wait_ge(w1_in[w.h], 16 * (w.m + 1))
                    wait(act, s["l1_done"], NU * (w.k - 1))
                    act.copy(w1_h[w.h][:], w1_raw[w.h][:]).then_inc(s["w1_hi"], 1)

                def w2_high(a):
                    act.wait_ge(w2_in[a.h], 16 * (a.m + 1))
                    wait(act, s["y_done"], 2 * (a.k - 1))
                    act.copy(w2_h[a.h][:], w2_raw[a.h][:]).then_inc(s["w2_hi"], 1)

                def rows_high(a):
                    act.wait_ge(s["xeT_done"], a.k + 1)
                    act.copy(xeT_h[:].rearrange("p c n -> p (c n)"), X[0][:]).then_inc(s["xeT_hi"], 1)

                def hidden(a, u):
                    act.wait_ge(s["l1_done"], NU * a.k + u + 1)
                    wait(act, s["h_ready"], NU * (a.k - 1) + u + 1)
                    act.activation(h_f[u][:].rearrange("p c n -> p (c n)"), HB[u][:], ACT.Gelu)\
                       .then_inc(s["gelu_done"], 1)
                    if u == 0:
                        wait(act, s["y_done"], 2 * (a.k - 1))
                    act.wait_ge(s["gelu_done"], NU * a.k + u + 1)
                    act.copy(h_h[a.h][:, 2 * u:2 * u + 2, :], h_f[u][:]).then_inc(s["h_hi"], 1)

                def step(w, a, b):
                    if a is not None:
                        w2_high(a)
                        rows_high(a)
                    if w is not None:
                        w1_high(w)
                    if a is not None:
                        for u in range(NU):
                            hidden(a, u)

                run_tiles(act, step)

            @blk.vector
            def _(dve):
                def w1_low(w):
                    dve.wait_ge(s["w1_hi"], w.k + 1)
                    dve.tensor_tensor(w1_l[w.h][:], w1_raw[w.h][:], w1_h[w.h][:].bitcast(f32), ALU.subtract)\
                       .then_inc(s["w1_ready"], 1)

                def w2_low(a):
                    dve.wait_ge(s["w2_hi"], a.k + 1)
                    dve.tensor_tensor(w2_l[a.h][:], w2_raw[a.h][:], w2_h[a.h][:].bitcast(f32), ALU.subtract)\
                       .then_inc(s["w2_ready"], 1)

                def normalize(a):
                    dve.wait_ge(g_in[a.h], 16 * (a.m + 1))
                    wait(dve, s["xeT_done"], a.k)
                    g = g_sb[a.h]
                    for t in range(2):
                        dve.tensor_scalar(xe[:, t, :], g[:, t, 0:H], g[:, t, C_MEAN:C_MEAN + 1],
                                          g[:, t, C_RSTD:C_RSTD + 1], ALU.subtract, ALU.mult).then_inc(s["xe_ready"], 1)

                def hidden_low(a, u):
                    dve.wait_ge(s["h_hi"], NU * a.k + u + 1)
                    dve.tensor_tensor(h_l[a.h][:, 2 * u:2 * u + 2, :], h_f[u][:],
                                      h_h[a.h][:, 2 * u:2 * u + 2, :].bitcast(f32), ALU.subtract).then_inc(s["h_ready"], 1)

                def rows_low(a):
                    dve.wait_ge(s["xeT_hi"], a.k + 1)
                    dve.tensor_tensor(xeT_l[:].rearrange("p c n -> p (c n)"), X[0][:],
                                      xeT_h[:].rearrange("p c n -> p (c n)").bitcast(f32), ALU.subtract)\
                       .then_inc(s["xeT_ready"], 1)

                def output(b, t):
                    g = g_sb[b.h]
                    if t == 0:
                        dve.wait_ge(osc[b.h], 16 * E // 2 + 32 * b.m)
                        dve.tensor_copy(o_idx[b.h][:], g[:, :, C_ID])
                    dve.wait_ge(s["y_done"], 2 * b.k + t + 1)
                    dve.scalar_tensor_tensor(o_sb[b.h][:, t, :], O[t][:, 0:H], g[:, t, C_COEF:C_COEF + 1],
                                             g[:, t, 0:H], ALU.mult, ALU.add).then_inc(s["o_ready"], 1)

                def step(w, a, b):
                    if a is not None:
                        normalize(a)
                        w2_low(a)
                    if b is not None:
                        output(b, 0)
                    if a is not None:
                        rows_low(a)
                    if b is not None:
                        output(b, 1)
                    if a is not None:
                        hidden_low(a, 0)
                    if w is not None:
                        w1_low(w)
                    if a is not None:
                        for u in range(1, NU):
                            hidden_low(a, u)

                run_tiles(dve, step)

            @blk.tensor
            def _(pe):
                def turn(a):
                    wait(pe, s["xeT_ready"], a.k)
                    for t in range(2):
                        pe.wait_ge(s["xe_ready"], 2 * a.k + t + 1)
                        for c in range(HC):
                            mm = pe.transpose(X[0][:, c * TT + t * P:c * TT + (t + 1) * P],
                                              xe[:, t, c * P:(c + 1) * P], identf[:])
                    mm.then_inc(s["xeT_done"], 1)

                def first_layer(a, u):
                    if u == 0:
                        pe.wait_ge(s["xeT_ready"], a.k + 1)
                        pe.wait_ge(s["w1_ready"], a.k + 1)
                    wait(pe, s["gelu_done"], NU * (a.k - 1) + u + 1)
                    for f in (2 * u, 2 * u + 1):
                        z = slice(f * P, (f + 1) * P)
                        terms = [(w[:, c, z], xx[:, c, :]) for c in range(HC) for w, xx in
                                 ((w1_h[a.h], xeT_h), (w1_h[a.h], xeT_l), (w1_l[a.h], xeT_h))]
                        for n, (l, r) in enumerate(terms):
                            mm = pe.matmul(HB[u][:, (f % 2) * TT:(f % 2 + 1) * TT], l, r,
                                           start=(n == 0), stop=(n == len(terms) - 1))
                    mm.then_inc(s["l1_done"], 1)

                def second_layer(b, t):
                    if t == 0:
                        wait(pe, s["o_ready"], 2 * b.k)
                        pe.wait_ge(s["w2_ready"], b.k + 1)
                    z = slice(t * P, (t + 1) * P)
                    for f in range(FC):
                        if t == 0 and f % 2 == 0:
                            pe.wait_ge(s["h_ready"], NU * b.k + f // 2 + 1)
                        for n, (hh, ww) in enumerate(((h_h, w2_h), (h_h, w2_l), (h_l, w2_h))):
                            mm = pe.matmul(O[t][:, 0:H], hh[b.h][:, f, z], ww[b.h][:, f, :],
                                           start=(f == 0 and n == 0), stop=(f == FC - 1 and n == 2))
                    mm.then_inc(s["y_done"], 1)

                def step(w, a, b):
                    if b is not None:
                        second_layer(b, 0)
                    if a is not None:
                        turn(a)
                    if b is not None:
                        second_layer(b, 1)
                    if a is not None:
                        for u in range(NU):
                            first_layer(a, u)

                run_tiles(pe, step)


def kernel(**inputs):
    import numpy as np
    import concourse.bacc as bacc
    from concourse import mybir as mb
    from concourse.bass_utils import run_bass_kernel_spmd

    def host(name):
        return np.asarray(inputs[name])

    def flat_row(name):
        return np.ascontiguousarray(host(name).reshape(1, -1))

    arrays = {
        "x": host("x"),
        "ctxT": np.ascontiguousarray(host("ctx_1024").reshape(B * SK, H).T),
        "mask": host("mask_BxSxS2_if1"),
        "maskT": np.ascontiguousarray(host("mask_BxSxS2_if1").transpose(0, 2, 1)),
        "g_xattn": host("g_xattn").reshape(1), "g_ffn": host("g_ffn").reshape(1),
        "WqT": np.ascontiguousarray(host("L0_xattn_Wq").T),
        "bq": np.ascontiguousarray(host("L0_xattn_bq").reshape(HC, P).T),
        "WkT": np.ascontiguousarray(host("L0_xattn_Wk").T),
        "bk": np.ascontiguousarray(host("L0_xattn_bk").reshape(HC, P).T),
        "WvT": np.ascontiguousarray(host("L0_xattn_Wv").T), "bv": flat_row("L0_xattn_bv"),
        "WoT": np.ascontiguousarray(host("L0_xattn_Wo").T), "bo": flat_row("L0_xattn_bo"),
        "Wr": host("L0_ffn_Wr"), "br": flat_row("L0_ffn_br"),
        "W1": host("L0_ffn_W1"), "W2": host("L0_ffn_W2"),
    }
    nc = bacc.Bacc("TRN2", target_bir_lowering=False, num_devices=1)
    args = [nc.dram_tensor(n, a.shape, mb.dt.from_np(a.dtype), kind="ExternalInput").ap() for n, a in arrays.items()]
    out = nc.dram_tensor("out", (B, S, H), mb.dt.float32, kind="ExternalOutput").ap()
    build(nc, *args, out)
    result = run_bass_kernel_spmd(nc, [{n: np.ascontiguousarray(a) for n, a in arrays.items()}], core_ids=[0])
    return result.results[0]["out"]
```

```python
import concourse.bass as bass
from concourse import mybir
from contextlib import ExitStack

B, S, H = 4, 1024, 256
SK = 64
NH, DK = 16, 16
E, F = 8, 1024
P = 128
HC = H // P
BLK, T = 512, 4
NBLK = B * S // BLK
NPAIR = NH // 2
BIG = float(2.0 ** 100)
TT = 256
CAP = B * S + TT
NT = (B * S + E * (TT - 1)) // TT
MIN_TILES = B * S // TT
SPARE = (NT - MIN_TILES) * TT
BINS = E * CAP + SPARE
C_MEAN, C_RSTD, C_COEF, C_ID, ROW = H, H + 1, H + 2, H + 3, H + 4
NO_TOKEN = float(1 << 20)
FC = F // P
EPS = 1e-5


class Blk:

    def __init__(self, m, h):
        self.m, self.h, self.k = m, h, 2 * m + h


def wait(eng, sem, value, passed=None):
    if not isinstance(value, int) or value > 0:
        eng.wait_ge(sem, value)
        if passed is not None and not isinstance(value, int):
            eng.sem_inc(passed, 1)


def run_blocks(eng, step):
    step(Blk(0, 0), None, None, None, None)
    step(Blk(0, 1), Blk(0, 0), None, None, None)
    step(Blk(1, 0), Blk(0, 1), Blk(0, 0), None, None)
    step(Blk(1, 1), Blk(1, 0), Blk(0, 1), Blk(0, 0), None)
    with eng.Fori(0, B - 2) as i:
        step(Blk(i + 2, 0), Blk(i + 1, 1), Blk(i + 1, 0), Blk(i, 1), Blk(i, 0))
        step(Blk(i + 2, 1), Blk(i + 2, 0), Blk(i + 1, 1), Blk(i + 1, 0), Blk(i, 1))
    step(None, Blk(B - 1, 1), Blk(B - 1, 0), Blk(B - 2, 1), Blk(B - 2, 0))
    step(None, None, Blk(B - 1, 1), Blk(B - 1, 0), Blk(B - 2, 1))
    step(None, None, None, Blk(B - 1, 1), Blk(B - 1, 0))
    step(None, None, None, None, Blk(B - 1, 1))


def run_tiles(eng, step):
    assert NT % 2 == 1
    step(Blk(0, 0), None, None)
    step(Blk(0, 1), Blk(0, 0), None)
    step(Blk(1, 0), Blk(0, 1), Blk(0, 0))
    with eng.Fori(0, (NT - 3) // 2) as i:
        step(Blk(i + 1, 1), Blk(i + 1, 0), Blk(i, 1))
        step(Blk(i + 2, 0), Blk(i + 1, 1), Blk(i + 1, 0))
    last = (NT - 1) // 2
    step(None, Blk(last, 0), Blk(last - 1, 1))
    step(None, None, Blk(last, 0))


POOL_CONST, SETUP_DVE, NCONST = 24, 41, 16


class Chain:

    def __init__(self, eng, sem, per):
        self.eng, self.sem, self.per = eng, sem, per

    def begin(self, k):
        self.base, self.n = self.per * k, 0

    def add(self, ins):
        self.n += 1
        return ins.then_inc(self.sem, 1)

    def sync(self):
        self.eng.wait_ge(self.sem, self.base + self.n)

    def link(self, ins):
        self.add(ins)
        self.sync()

    def end(self):
        assert self.n == self.per, (self.n, self.per)


def build(nc, x, ctxT, mask, maskT, g_xattn, g_ffn, WqT, bq, WkT, bk, WvT, bv, WoT, bo, Wr, br, W1, W2, out):
    f32, f32r, bf16, i32 = mybir.dt.float32, mybir.dt.float32r, mybir.dt.bfloat16, mybir.dt.int32
    ALU, ACT, AX = mybir.AluOpType, mybir.ActivationFunctionType, mybir.AxisListType

    bins = nc.dram_tensor("bins", (BINS, ROW), f32, kind="Internal").ap()
    x_v = x.rearrange("b (h t p) c -> (b h) p t c", h=2, t=T)
    mask_v = mask.rearrange("b (h t p) s -> (b h) p t s", h=2, t=T)
    maskT_v = maskT.rearrange("b s (h n) -> b h s n", h=2)
    W1_v = W1.rearrange("e (c p) n -> e p c n", p=P)
    W2_v = W2.rearrange("e (c p) n -> e p c n", p=P)
    out_rows = out.rearrange("b s c -> (b s) c")

    ctx = ExitStack()
    with ctx:
        def sem(name):
            return ctx.enter_context(nc.semaphore(name))

        def sb(name, shape, dt, scope=ctx):
            return scope.enter_context(nc.sbuf_tensor(name, shape, dt))

        bank = {n: ctx.enter_context(nc.psum_tensor(n, [P, 512], f32))
                for n in ("X0", "X1", "S0", "S1", "T0", "T1", "O0", "O1")}
        X, SC, TS, O = ([bank[f"{n}{i}"] for i in range(2)] for n in "XSTO")

        identf = sb("identf", [P, P], f32)
        padding = sb("padding", [P, ROW], f32)
        tab = sb("tab", [P, 2, NT], i32)
        padrow = sb("padrow", [P, E], i32)
        w1_raw = [sb(f"w1_raw{i}", [P, HC, F], f32) for i in range(2)]
        w2_raw = [sb(f"w2_raw{i}", [P, FC, H], f32) for i in range(2)]

        A = ExitStack()
        ident_bf = sb("ident_bf", [P, P], bf16, A)
        ones_bf = sb("ones_bf", [P, P], bf16, A)
        before_bf = sb("before_bf", [P, P], bf16, A)
        ones_row = sb("ones_row", [1, P], f32, A)
        headmask = sb("headmask", [P, NH // 2], f32, A)
        halfmask = sb("halfmask", [P, 2], f32, A)
        sel = sb("sel", [SK + NH, NPAIR, 2 * SK], f32r, A)
        ecap = sb("ecap", [P, E], f32, A)
        ecap_i = sb("ecap_i", [P, E], i32, A)
        base = sb("base", [P, E], f32, A)
        tokid = sb("tokid", [P, T], f32, A)
        tokid_i = sb("tokid_i", [P, T], i32, A)
        prio = sb("prio", [P, E], f32, A)
        prio_i = sb("prio_i", [P, E], i32, A)
        half_exp = sb("half_exp", [P, T], f32, A)
        tg = sb("tg", [P, 2], f32, A)
        tgt = sb("tgt", [P, 2], f32, A)
        bq_c = sb("bq_c", [P, HC], f32, A)
        bk_c = sb("bk_c", [P, HC], f32, A)
        bv_r = sb("bv_r", [1, H], f32, A)
        bo_r = sb("bo_r", [1, H], f32, A)
        br_c = sb("br_c", [E, 1], f32, A)
        nbr_c = sb("nbr_c", [E, 1], f32, A)
        wr_sb = sb("wr_sb", [P, HC, E], f32, A)
        wq_h = sb("wq_h", [P, HC, H], f32r, A)
        wq_l = sb("wq_l", [P, HC, H], f32r, A)
        wo_h = sb("wo_h", [P, HC, H], f32r, A)
        wo_l = sb("wo_l", [P, HC, H], f32r, A)
        bo_b = sb("bo_b", [P, H], f32, A)
        kT = sb("kT", [P, HC, B, SK], f32, A)
        kT_h = sb("kT_h", [P, HC, B, SK], f32r, A)
        kT_l = sb("kT_l", [P, HC, B, SK], f32r, A)
        kbd = sb("kbd", [P, B, HC, (NH // 2) * SK], f32r, A)
        kp_h = sb("kp_h", [P, HC, 2 * SK], f32r, A)
        kp_l = sb("kp_l", [P, HC, 2 * SK], f32r, A)
        v_h = sb("v_h", [P, B, H], f32r, A)
        v_l = sb("v_l", [P, B, H], f32r, A)
        vbd_h = sb("vbd_h", [P, NPAIR, P], f32r, A)
        vbd_l = sb("vbd_l", [P, NPAIR, P], f32r, A)
        xt = [sb(f"xt{i}", [P, T, H], f32, A) for i in range(2)]
        mi = [sb(f"mi{i}", [P, T, SK], i32, A) for i in range(2)]
        miT = [sb(f"miT{i}", [SK, BLK], i32, A) for i in range(2)]
        mb = [sb(f"mb{i}", [P, T, SK], bf16, A) for i in range(2)]
        mx = [sb(f"mx{i}", [SK + NH, BLK], f32r, A) for i in range(2)]
        st = sb("st", [P, T, 6], f32, A)
        mv = sb("mv", [P, T, 2], f32, A)
        ve = sb("ve", [P, T], f32, A)
        rs = sb("rs", [P, T], f32, A)
        xn = sb("xn", [P, T, H], f32, A)
        xnT_h = sb("xnT_h", [P, HC, BLK], f32r, A)
        xnT_l = sb("xnT_l", [P, HC, BLK], f32r, A)
        q_h = [sb(f"q_h{i}", [P, HC, BLK], f32r, A) for i in range(2)]
        q_l = [sb(f"q_l{i}", [P, HC, BLK], f32r, A) for i in range(2)]
        smax = sb("smax", [P, T, NH], f32, A)
        NPB = 4
        p_f = [sb(f"p_f{i}", [P, BLK], f32, A) for i in range(NPB)]
        p_h = [sb(f"p_h{i}", [P, BLK], f32r, A) for i in range(NPB)]
        p_l = [sb(f"p_l{i}", [P, BLK], f32r, A) for i in range(NPB)]
        den = sb("den", [P, BLK], f32, A)
        rden = sb("rden", [P, BLK], f32, A)
        cn = sb("cn", [P, HC, BLK], f32, A)
        c_h = sb("c_h", [P, HC, BLK], f32r, A)
        c_l = sb("c_l", [P, HC, BLK], f32r, A)
        pay = [sb(f"pay{i}", [P, T, ROW], f32, A) for i in range(2)]
        st2 = sb("st2", [P, T, 6], f32, A)
        mv2 = sb("mv2", [P, T, 2], f32, A)
        ve2 = sb("ve2", [P, T], f32, A)
        xn2 = sb("xn2", [P, T, H], f32, A)
        xn2T = sb("xn2T", [P, HC, BLK], f32, A)
        ez = sb("ez", [E, BLK], f32, A)
        e1 = sb("e1", [P, T, E], f32, A)
        pr = sb("pr", [P, T, E], f32, A)
        pm = sb("pm", [P, T], f32, A)
        eq = sb("eq", [P, T, E], f32, A)
        w_ = sb("w_", [P, T, E], f32, A)
        wm = sb("wm", [P, T], f32, A)
        onehot = sb("onehot", [P, T + 1, E], bf16, A)
        rk = sb("rk", [P, T, E], f32, A)
        rsel = sb("rsel", [P, T, E], f32, A)
        slot_f = sb("slot_f", [P, T], f32, A)
        slot = [sb(f"slot{i}", [P, T], i32, A) for i in range(2)]
        th_i = sb("th_i", [P, MIN_TILES], i32, A)
        th = sb("th", [P, MIN_TILES], f32, A)
        cnt = sb("cnt", [P, E], f32, A)
        over = sb("over", [P, E, MIN_TILES], f32, A)
        ntl = sb("ntl", [P, E], f32, A)
        tri = sb("tri", [P, E, E], f32, A)
        ctri = sb("ctri", [P, E, E], f32, A)
        cend = sb("cend", [P, E], f32, A)
        ti_i = sb("ti_i", [P, NT], i32, A)
        ti = sb("ti", [P, NT], f32, A)
        ge = sb("ge", [P, NT, E], f32, A)
        gen = sb("gen", [P, NT, E], f32, A)
        et = sb("et", [P, NT], f32, A)
        cs = sb("cs", [P, NT], f32, A)
        row_f = sb("row_f", [P, 2, NT], f32, A)
        s = {n: sem(n) for n in (
            "consts_in", "x_in0", "x_in1", "m_in0", "m_in1",
            "pool_const", "setup_dve", "setup_act", "setup_pe",
            "mask_ready", "xb_done", "rstd_ready", "rstd2_ready", "k_ready", "v_ready",
            "stat_ready", "xn_ready", "xT_done", "xnT_hi", "xnT_ready", "q_done", "pads_done", "rows_in0", "rows_in1", "den_ready", "ezT_done", "ez_used", "q_hi", "q_ready",
            "tok_scored", "max_done", "mxT_done", "mx_ready",
            "tsc_done", "exp_done", "p_hi", "p_even", "p_odd", "pv_done", "ctx_done", "ctx_hi", "ctx_ready", "wo_done",
            "x1_done",
            "stat2_ready", "xn2_ready", "x2T_done", "xn2T_ready", "lg_done", "ez_ready", "pay_ready",
            "onehot_ready", "rank_done", "slot_ready", "scat0", "scat1",
            "stats1", "stats2", "eps1", "eps2", "chain_ctx", "chain_route", "chain_slot", "chain_tab", "chain_tab2",
            "tab_ready", "osc0", "osc1", "pool_passed", "sp_passed", "dve_passed", "pe_passed",
            "w1_in0", "w1_in1", "w2_in0", "w2_in1", "g_in0", "g_in1",
            "w1_hi", "w1_ready", "w2_hi", "w2_ready", "xe_ready", "xeT_done", "xeT_hi", "xeT_ready",
            "l1_done", "gelu_done", "h_hi", "h_ready", "y_done", "o_ready",
        )}
        x_in = [s["x_in0"], s["x_in1"]]
        m_in = [s["m_in0"], s["m_in1"]]
        scat = [s["scat0"], s["scat1"]]
        rows_in = [s["rows_in0"], s["rows_in1"]]

        sel_f = cn[0:SK + NH].rearrange("p c n -> p (c n)").rearrange("p (j h k) -> p j h k", h=2, k=SK)
        ctx_t = xn2T[:].rearrange("p c (b d k) -> p c b d k", b=B, d=2)
        wos, wv_t = xn[:, 0:HC, :], xn[:, HC:2 * HC, :]
        wk_t, wq_t = xn2[:, 0:HC, :], xn2[:, HC:2 * HC, :]
        wo_t = rden[:].rearrange("p (c n) -> p c n", c=HC)

        with nc.Block() as blk:
            @blk.sync
            def _(sp):
                def const(dst, src):
                    sp.dma_start(dst, src).then_inc(s["consts_in"], 16)

                def load(n):
                    wait(sp, s["xn_ready"], T * (n.k - 1), s["sp_passed"])
                    sp.dma_start(xt[n.h][:], x_v[n.k]).then_inc(x_in[n.h], 16)
                    wait(sp, s["mask_ready"], 2 * (n.k - 1), s["sp_passed"])
                    sp.dma_start(mi[n.h][:], mask_v[n.k]).then_inc(m_in[n.h], 16)
                    sp.dma_start(miT[n.h][:], maskT_v[n.m, n.h]).then_inc(m_in[n.h], 16)

                def load_rows(b):
                    wait(sp, scat[b.h], 16 + 16 * T * b.m, s["sp_passed"])
                    sp.dma_start(pay[b.h][:, :, 0:H], x_v[b.k]).then_inc(rows_in[b.h], 16)

                def step(n, a, b, c, d):
                    if n is not None and not (isinstance(n.k, int) and n.k == 0):
                        load(n)
                    if b is not None:
                        load_rows(b)

                load(Blk(0, 0))
                for d in range(2):
                    for c in range(HC):
                        const(ctx_t[:, c, :, d, :], ctxT[c * P:(c + 1) * P, :].rearrange("p (b k) -> p b k", b=B))
                for t, w in ((wk_t, WkT), (wv_t, WvT), (wq_t, WqT), (wo_t, WoT), (wr_sb[:], Wr)):
                    const(t, w.rearrange("(c p) n -> p c n", p=P))
                const(tg[:, 0:1], g_xattn.partition_broadcast(P))
                const(tg[:, 1:2], g_ffn.partition_broadcast(P))
                const(bq_c[:], bq)
                const(bk_c[:], bk)
                const(bv_r[:], bv)
                const(bo_r[:], bo)
                const(br_c[:], br)
                run_blocks(sp, step)

            @blk.gpsimd
            def _(pool):
                n = 0

                def done(ins):
                    nonlocal n
                    n += 1
                    ins.then_inc(s["pool_const"], 1)

                def sync():
                    pool.wait_ge(s["pool_const"], n)

                done(pool.memset(identf[:], 0.0))
                done(pool.memset(padding[:], 0.0))
                done(pool.memset(ones_bf[:], 1.0))
                done(pool.memset(before_bf[:], 1.0))
                done(pool.memset(ones_row[:], 1.0))
                done(pool.memset(headmask[:], 1.0))
                done(pool.memset(sel_f, 0.0))
                done(pool.memset(half_exp[:], -0.5))
                done(pool.memset(onehot[:], 0.0))
                done(pool.memset(tri[:], 1.0))
                done(pool.iota(ecap_i[:], [[CAP, E]], base=0, channel_multiplier=0))
                done(pool.iota(tokid_i[:], [[P, T]], base=0, channel_multiplier=1))
                done(pool.iota(prio_i[:], [[-1, E]], base=E, channel_multiplier=0))
                done(pool.iota(th_i[:], [[TT, MIN_TILES]], base=0, channel_multiplier=0))
                done(pool.iota(ti_i[:], [[1, NT]], base=0, channel_multiplier=0))
                sync()
                done(pool.memset(padding[:, C_ID:C_ID + 1], NO_TOKEN))
                done(pool.affine_select(out=identf[:], in_=identf[:], compare_op=ALU.not_equal, fill=1.0,
                                        base=0, pattern=[[-1, P]], channel_multiplier=1))
                done(pool.affine_select(out=before_bf[:], in_=before_bf[:], compare_op=ALU.is_gt, fill=0.0,
                                        base=0, pattern=[[1, P]], channel_multiplier=-1))
                done(pool.affine_select(out=headmask[:], in_=headmask[:], compare_op=ALU.is_ge, fill=0.0,
                                        base=0, pattern=[[-DK, NH // 2]], channel_multiplier=1))
                done(pool.affine_select(out=sel_f[0:SK], in_=sel_f[0:SK], compare_op=ALU.not_equal, fill=1.0,
                                        base=0, pattern=[[0, NPAIR], [0, 2], [-1, SK]], channel_multiplier=1))
                sync()
                done(pool.affine_select(out=sel_f[SK:SK + NH], in_=sel_f[SK:SK + NH], compare_op=ALU.not_equal,
                                        fill=-1.0, base=0, pattern=[[-2, NPAIR], [-1, 2], [0, SK]],
                                        channel_multiplier=1))
                sync()
                done(pool.affine_select(out=tri[:], in_=tri[:], compare_op=ALU.is_ge, fill=0.0,
                                        base=0, pattern=[[1, E], [-1, E]], channel_multiplier=0))
                sync()
                done(pool.affine_select(out=headmask[:], in_=headmask[:], compare_op=ALU.is_ge, fill=0.0,
                                        base=DK - 1, pattern=[[DK, NH // 2]], channel_multiplier=-1))
                done(pool.tensor_copy(ident_bf[:], identf[:]))
                assert n == POOL_CONST
                sync()
                half = SPARE // 2
                for h in range(2):
                    pool.dma_start(bins[E * CAP + h * half:E * CAP + (h + 1) * half, :].rearrange("(n p) c -> p n c", p=P),
                                   padding[:].unsqueeze(1).broadcast_to([P, half // P, ROW])).then_inc(scat[h], 16)

                def token_masks(a):
                    wait(pool, m_in[a.h], 32 * (a.m + 1), s["pool_passed"])
                    wait(pool, s["tok_scored"], 2 * T * (a.k - 1), s["pool_passed"])
                    pool.tensor_scalar(mb[a.h][:], mi[a.h][:], 0.0, -BIG, ALU.is_equal, ALU.mult)\
                        .then_inc(s["mask_ready"], 1)

                def key_masks(a):
                    wait(pool, s["tsc_done"], NPAIR * (a.k - 1), s["pool_passed"])
                    pool.tensor_scalar(mx[a.h][0:SK, :], miT[a.h][:], 0.0, -BIG, ALU.is_equal, ALU.mult)\
                        .then_inc(s["mask_ready"], 1)

                def bias_rows(b):
                    wait(pool, rows_in[b.h], 16 * (b.m + 1), s["pool_passed"])
                    pool.tensor_tensor(pay[b.h][:, :, 0:H], pay[b.h][:, :, 0:H],
                                       bo_b[:].unsqueeze(1).broadcast_to([P, T, H]),
                                       ALU.add).then_inc(s["xb_done"], 1)

                def rstd(b, moments, eps_out, result, ready, done_, steps):
                    wait(pool, ready, T * (b.k + 1), s["pool_passed"])
                    pool.tensor_scalar(eps_out[:], moments[:, :, 1], EPS, None, ALU.add).then_inc(steps, 1)
                    wait(pool, steps, b.k + 1, s["pool_passed"])
                    pool.tensor_tensor(result, eps_out[:], half_exp[:], ALU.pow).then_inc(done_, 1)

                def keys(m):
                    wait(pool, s["tsc_done"], NPAIR * 2 * m, s["pool_passed"])
                    for src, dst in ((kT_h, kp_h), (kT_l, kp_l)):
                        for c in range(HC):
                            pool.tensor_tensor(
                                dst[:, c, :].rearrange("p (h k) -> p h k", h=2),
                                src[:, c, m, :].bitcast(f32).unsqueeze(1).broadcast_to([P, 2, SK]),
                                halfmask[:].unsqueeze(2).broadcast_to([P, 2, SK]), ALU.mult)\
                                .then_inc(s["k_ready"], 1)

                def scatter(b):
                    wait(pool, s["slot_ready"], b.k + 1, s["pool_passed"])
                    wait(pool, s["pay_ready"], 2 * (b.k + 1), s["pool_passed"])
                    wait(pool, s["rstd2_ready"], b.k + 1, s["pool_passed"])
                    for t in range(T):
                        pool.indirect_dma_start(
                            out=bins, out_offset=bass.IndirectOffsetOnAxis(ap=slot[b.h][:, t:t + 1], axis=0),
                            in_=pay[b.h][:, t, :], in_offset=None).then_inc(scat[b.h], 16)

                def split_odd(b, g):
                    i = (2 * g + 1) % NPB
                    wait(pool, s["p_hi"], NPAIR * b.k + 2 * g + 2, s["pool_passed"])
                    pool.tensor_tensor(p_l[i][:], p_f[i][:], p_h[i][:].bitcast(f32), ALU.subtract)\
                        .then_inc(s["p_odd"], 1)

                def normalize_x(n):
                    wait(pool, s["rstd_ready"], n.k + 1, s["pool_passed"])
                    wait(pool, s["xT_done"], HC * n.k, s["pool_passed"])
                    for t in range(T):
                        pool.tensor_scalar(xn[:, t, :], xt[n.h][:, t, :], mv[:, t, 0:1], rs[:, t:t + 1],
                                           ALU.subtract, ALU.mult).then_inc(s["xn_ready"], 1)

                def step(n, a, b, c, d):
                    if b is not None and b.h == 0:
                        keys(b.m)
                    if a is not None:
                        token_masks(a)
                    if b is not None:
                        split_odd(b, 0)
                    if a is not None:
                        key_masks(a)
                    if b is not None:
                        split_odd(b, 1)
                    if c is not None:
                        rstd(c, mv2, ve2, pay[c.h][:, :, C_RSTD], s["stat2_ready"], s["rstd2_ready"], s["eps2"])
                    if d is not None:
                        scatter(d)
                    if b is not None:
                        split_odd(b, 2)
                    if n is not None:
                        rstd(n, mv, ve, rs[:], s["stat_ready"], s["rstd_ready"], s["eps1"])
                    if b is not None:
                        split_odd(b, 3)
                    if n is not None:
                        normalize_x(n)
                    if b is not None:
                        bias_rows(b)

                wait(pool, s["setup_dve"], SETUP_DVE, s["pool_passed"])
                run_blocks(pool, step)
                for h in range(2):
                    wait(pool, scat[h], 16 + 16 * T * NBLK // 2, s["pool_passed"])

            @blk.scalar
            def _(act):
                act.wait_ge(s["consts_in"], 16 * NCONST)
                act.activation(tgt[:], tg[:], ACT.Tanh).then_inc(s["setup_act"], 1)

                def xn_hi(a):
                    for c in range(HC):
                        act.wait_ge(s["xT_done"], HC * a.k + c + 1)
                        wait(act, s["q_done"], HC * a.k)
                        act.copy(xnT_h[:, c, :], X[c][:]).then_inc(s["xnT_hi"], 1)

                def q_hi(a):
                    for c in range(HC):
                        act.wait_ge(s["q_done"], HC * a.k + c + 1)
                        wait(act, s["tsc_done"], NPAIR * (a.k - 1))
                        act.activation(q_h[a.h][:, c, :], X[c][:], ACT.Identity, bias=bq_c[:, c:c + 1])\
                           .then_inc(s["q_hi"], 1)

                def maxima(a):
                    act.wait_ge(s["mxT_done"], a.k + 1)
                    act.copy(mx[a.h][SK:SK + NH, :], SC[0][0:NH, :]).then_inc(s["mx_ready"], 1)

                def exps(b, g):
                    for j in (2 * g, 2 * g + 1):
                        n = NPAIR * b.k + j
                        act.wait_ge(s["tsc_done"], n + 1)
                        wait(act, (s["p_even"], s["p_odd"])[j % 2], 4 * b.k + g - 1)
                        act.activation(p_f[j % NPB][:], TS[j % 2][:], ACT.Exp).then_inc(s["exp_done"], 1)
                    for j in (2 * g, 2 * g + 1):
                        n = NPAIR * b.k + j
                        act.wait_ge(s["exp_done"], n + 1)
                        wait(act, s["pv_done"], n - NPB + 1)
                        act.copy(p_h[j % NPB][:], p_f[j % NPB][:]).then_inc(s["p_hi"], 1)

                def sums(b, g):
                    act.wait_ge(s["pv_done"], NPAIR * b.k + 2 * g + 2)
                    v, r = 64 * (g % 2), 64 - 64 * (g % 2)
                    if g % 2 == 0:
                        wait(act, s["ctx_done"], 2 * b.k + g // 2)
                        wait(act, s["ctx_ready"], HC * (b.k - 1) + g // 2 + 1)
                    act.copy(den[v:v + 64, :], O[g % 2][r:r + 64, :]).then_inc(s["den_ready"], 1)
                    act.copy(cn[v:v + 64, g // 2, :], O[g % 2][v:v + 64, :]).then_inc(s["den_ready"], 1)

                def ctx_high(b, c):
                    act.wait_ge(s["ctx_done"], 2 * b.k + c + 1)
                    wait(act, s["wo_done"], T * b.k)
                    act.copy(c_h[:, c, :], cn[:, c, :]).then_inc(s["ctx_hi"], 1)

                def xn2_copy(c):
                    for i in range(HC):
                        act.wait_ge(s["x2T_done"], HC * c.k + i + 1)
                        act.copy(xn2T[:, i, :], X[i][:]).then_inc(s["xn2T_ready"], 1)

                def route_exp(c):
                    act.wait_ge(s["lg_done"], c.k + 1)
                    wait(act, s["ezT_done"], c.k)
                    act.activation(ez[:], X[0][0:E, :], ACT.Exp, bias=nbr_c[:, 0:1], scale=-1.0)\
                       .then_inc(s["ez_ready"], 1)

                def step(n, a, b, c, d):
                    if a is not None:
                        xn_hi(a)
                    if b is not None:
                        exps(b, 0)
                        exps(b, 1)
                    if a is not None:
                        q_hi(a)
                    if b is not None:
                        sums(b, 0)
                        exps(b, 2)
                        sums(b, 1)
                        exps(b, 3)
                    if c is not None:
                        xn2_copy(c)
                    if b is not None:
                        ctx_high(b, 0)
                        sums(b, 2)
                    if c is not None:
                        route_exp(c)
                    if b is not None:
                        sums(b, 3)
                    if a is not None:
                        maxima(a)
                    if b is not None:
                        ctx_high(b, 1)

                act.wait_ge(s["setup_dve"], SETUP_DVE)
                run_blocks(act, step)

            @blk.vector
            def _(dve):
                su = Chain(dve, s["setup_dve"], SETUP_DVE)
                su.begin(0)
                dve.wait_ge(s["pool_const"], POOL_CONST)
                dve.wait_ge(s["consts_in"], 16 * NCONST)
                su.add(dve.tensor_copy(ecap[:], ecap_i[:]))
                su.add(dve.tensor_copy(base[:], ecap_i[:]))
                su.add(dve.tensor_copy(tokid[:], tokid_i[:]))
                su.add(dve.tensor_copy(prio[:], prio_i[:]))
                su.add(dve.tensor_copy(th[:], th_i[:]))
                su.add(dve.tensor_copy(ti[:], ti_i[:]))
                su.add(dve.tensor_copy(sel[:], sel_f.rearrange("p j h k -> p j (h k)")))
                su.add(dve.tensor_reduce(halfmask[:], headmask[:].rearrange("p (a h) -> p h a", h=2), AX.X, ALU.add))
                su.add(dve.tensor_copy(wq_h[:], wq_t))
                su.add(dve.memset(vbd_h[:].bitcast(f32), 0.0))
                su.add(dve.memset(vbd_l[:].bitcast(f32), 0.0))
                su.add(dve.tensor_scalar(nbr_c[:], br_c[:], -1.0, None, ALU.mult))
                dve.wait_ge(s["setup_act"], 1)
                su.add(dve.tensor_scalar(wos, wo_t, tgt[:, 0:1], None, ALU.mult))
                su.sync()
                su.add(dve.tensor_tensor(wq_l[:], wq_t, wq_h[:].bitcast(f32), ALU.subtract))
                su.add(dve.tensor_copy(wo_h[:], wos))
                for h2 in range(2):
                    for j2 in range(2):
                        for odd in range(2):
                            o = SK * (1 - odd) + 32 * j2 + DK * h2
                            su.add(dve.memset(vbd_h[h2 * SK:(h2 + 1) * SK].rearrange("p (g o j) c -> p g o j c", j=2, o=2)
                                              [:, :, odd, j2, o:o + DK].bitcast(f32), 1.0))
                su.sync()
                su.add(dve.tensor_tensor(wo_l[:], wos, wo_h[:].bitcast(f32), ALU.subtract))
                for c in range(HC):
                    dve.wait_ge(s["setup_pe"], c + 1)
                    su.add(dve.tensor_scalar(kT[:, c], X[c][:, 0:B * SK].rearrange("p (b k) -> p b k", b=B),
                                             bk_c[:, c:c + 1], DK ** -0.5, ALU.add, ALU.mult))
                su.sync()
                su.link(dve.tensor_copy(kT_h[:], kT[:]))
                su.link(dve.tensor_tensor(kT_l[:], kT[:], kT_h[:].bitcast(f32), ALU.subtract))
                for b in range(B):
                    for c in range(HC):
                        su.add(dve.tensor_tensor(
                            kbd[:, b, c, :].rearrange("p (h k) -> p h k", k=SK),
                            kT_h[:, c, b, :].bitcast(f32).unsqueeze(1).broadcast_to([P, NH // 2, SK]),
                            headmask[:].unsqueeze(2).broadcast_to([P, NH // 2, SK]), ALU.mult))
                for n in range(2):
                    dve.wait_ge(s["setup_pe"], 3 + n)
                    o = SC[n][:].rearrange("p (b c) -> p b c", b=2)
                    su.link(dve.tensor_copy(v_h[:, 2 * n:2 * n + 2, :], o))
                    su.add(dve.tensor_tensor(v_l[:, 2 * n:2 * n + 2, :], o, v_h[:, 2 * n:2 * n + 2, :].bitcast(f32),
                                             ALU.subtract))
                dve.wait_ge(s["setup_pe"], 5)
                su.link(dve.tensor_scalar(bo_b[:], O[0][:, 0:H], tgt[:, 0:1], None, ALU.mult))
                su.end()

                def place_values(m):
                    wait(dve, s["pv_done"], NPAIR * 2 * m)
                    for src, dst in ((v_h, vbd_h), (v_l, vbd_l)):
                        for h2 in range(2):
                            r = slice(h2 * SK, (h2 + 1) * SK)
                            for j2 in range(2):
                                for odd in range(2):
                                    o = SK * odd + 32 * j2 + DK * h2
                                    dve.tensor_copy(
                                        dst[r].rearrange("p (g o j) c -> p g o j c", j=2, o=2)[:, :, odd, j2, o:o + DK],
                                        src[r, m, :].rearrange("p (g o j h d) -> p g o j h d", o=2, j=2, h=2, d=DK)
                                        [:, :, odd, j2, h2, :]).then_inc(s["v_ready"], 1)

                def norm_stats(b, src, stats, moments, ready, ch):
                    for t in range(T):
                        ch.add(dve.bn_stats(stats[:, t, :], src[:, t, 0:H]))
                    wait(dve, ch.sem, ch.base + ch.n, s["dve_passed"])
                    for t in range(T):
                        dve.bn_aggr(moments[:, t, :], stats[:, t, :]).then_inc(ready, 1)

                lnc = Chain(dve, s["stats1"], T)
                ln2c = Chain(dve, s["stats2"], T)

                def norm1_stats(n):
                    dve.wait_ge(x_in[n.h], 16 * (n.m + 1))
                    wait(dve, s["xn_ready"], T * n.k, s["dve_passed"])
                    lnc.begin(n.k)
                    norm_stats(n, xt[n.h], st, mv, s["stat_ready"], lnc)

                def xn_lo(a):
                    for c in range(HC):
                        dve.wait_ge(s["xnT_hi"], HC * a.k + c + 1)
                        dve.tensor_tensor(xnT_l[:, c, :], X[c][:], xnT_h[:, c, :].bitcast(f32), ALU.subtract)\
                           .then_inc(s["xnT_ready"], 1)

                def q_lo(a):
                    for c in range(HC):
                        dve.wait_ge(s["q_hi"], HC * a.k + c + 1)
                        dve.scalar_tensor_tensor(q_l[a.h][:, c, :], X[c][:], bq_c[:, c:c + 1],
                                                 q_h[a.h][:, c, :].bitcast(f32), ALU.add, ALU.subtract)\
                           .then_inc(s["q_ready"], 1)

                def maxes(a, t):
                    for c in range(HC):
                        n = HC * T * a.k + HC * t + c
                        dve.wait_ge(s["tok_scored"], n + 1)
                        if t == 0 and c == 0:
                            wait(dve, s["mxT_done"], a.k)
                        dve.tensor_reduce(smax[:, t, c * 8:c * 8 + 8], SC[c][:].rearrange("p (h k) -> p h k", k=SK),
                                          AX.X, ALU.max).then_inc(s["max_done"], 1)

                def split_even(b, g):
                    i = 2 * g % NPB
                    dve.wait_ge(s["p_hi"], NPAIR * b.k + 2 * g + 1)
                    dve.tensor_tensor(p_l[i][:], p_f[i][:], p_h[i][:].bitcast(f32), ALU.subtract)\
                       .then_inc(s["p_even"], 1)

                cch = Chain(dve, s["chain_ctx"], HC)

                def context(b, c):
                    if c == 0:
                        cch.begin(b.k)
                    dve.wait_ge(s["den_ready"], 8 * b.k + 4 * c + 4)
                    cch.link(dve.reciprocal(rden[:], den[:]))
                    dve.tensor_tensor(cn[:, c, :], cn[:, c, :], rden[:], ALU.mult).then_inc(s["ctx_done"], 1)

                def ctx_low(b, c):
                    dve.wait_ge(s["ctx_hi"], HC * b.k + c + 1)
                    dve.tensor_tensor(c_l[:, c, :], cn[:, c, :], c_h[:, c, :].bitcast(f32), ALU.subtract)\
                       .then_inc(s["ctx_ready"], 1)

                def residual(b):
                    for u in range(2):
                        dve.wait_ge(s["wo_done"], T * b.k + 2 * u + 2)
                        if u == 0:
                            dve.wait_ge(s["xb_done"], b.k + 1)
                        dve.tensor_tensor(pay[b.h][:, 2 * u:2 * u + 2, 0:H],
                                          O[u][:].rearrange("p (t c) -> p t c", t=2),
                                          pay[b.h][:, 2 * u:2 * u + 2, 0:H], ALU.add).then_inc(s["x1_done"], 1)

                def norm2_stats(c):
                    ln2c.begin(c.k)
                    dve.wait_ge(s["x1_done"], 2 * (c.k + 1))
                    norm_stats(c, pay[c.h], st2, mv2, s["stat2_ready"], ln2c)

                def norm2(c):
                    dve.wait_ge(s["rstd2_ready"], c.k + 1)
                    wait(dve, s["x2T_done"], HC * c.k)
                    for t in range(T):
                        dve.tensor_scalar(xn2[:, t, :], pay[c.h][:, t, 0:H], mv2[:, t, 0:1],
                                          pay[c.h][:, t, C_RSTD:C_RSTD + 1], ALU.subtract, ALU.mult)\
                           .then_inc(s["xn2_ready"], 1)
                    dve.tensor_copy(pay[c.h][:, :, C_MEAN], mv2[:, :, 0]).then_inc(s["pay_ready"], 1)

                rch = Chain(dve, s["chain_route"], 7)

                def route(c):
                    rch.begin(c.k)
                    dve.wait_ge(s["ezT_done"], c.k + 1)
                    rch.link(dve.tensor_scalar(e1[:], X[1][:, 0:T * E].rearrange("p (t e) -> p t e", e=E),
                                               1.0, None, ALU.add))
                    rch.link(dve.reciprocal(pr[:], e1[:]))
                    rch.link(dve.tensor_reduce(pm[:], pr[:], AX.X, ALU.max))
                    rch.link(dve.tensor_tensor(eq[:], pr[:], pm[:].unsqueeze(2).broadcast_to([P, T, E]), ALU.is_equal))
                    rch.link(dve.tensor_tensor(w_[:], eq[:], prio[:].unsqueeze(1).broadcast_to([P, T, E]), ALU.mult))
                    rch.link(dve.tensor_reduce(wm[:], w_[:], AX.X, ALU.max))
                    dve.tensor_tensor(onehot[:, 0:T, :], w_[:], wm[:].unsqueeze(2).broadcast_to([P, T, E]),
                                      ALU.is_equal).then_inc(s["onehot_ready"], 1)
                    dve.tensor_scalar(pay[c.h][:, :, C_COEF], pm[:], tgt[:, 1:2], None, ALU.mult)
                    dve.tensor_copy(pay[c.h][:, :, C_ID], tokid[:]).then_inc(s["pay_ready"], 1)
                    rch.link(dve.tensor_scalar(tokid[:], tokid[:], float(BLK), None, ALU.add))
                    rch.end()

                sch = Chain(dve, s["chain_slot"], 4)

                def slots(c):
                    sch.begin(c.k)
                    dve.wait_ge(s["rank_done"], c.k + 1)
                    sch.link(dve.tensor_tensor(rk[:], SC[1][:, 0:T * E].rearrange("p (t e) -> p t e", t=T),
                                               base[:].unsqueeze(1).broadcast_to([P, T, E]), ALU.add))
                    sch.add(dve.tensor_tensor(base[:], base[:], SC[1][:, T * E:(T + 1) * E], ALU.add))
                    sch.add(dve.tensor_tensor(rsel[:], rk[:], onehot[:, 0:T, :], ALU.mult))
                    sch.sync()
                    sch.link(dve.tensor_reduce(slot_f[:], rsel[:], AX.X, ALU.add))
                    sch.end()
                    dve.wait_ge(scat[c.h], 16 + 16 * T * c.m)
                    dve.tensor_copy(slot[c.h][:], slot_f[:]).then_inc(s["slot_ready"], 1)

                def step(n, a, b, c, d):
                    if b is not None and b.h == 0:
                        place_values(b.m)
                    if a is not None:
                        xn_lo(a)
                    if d is not None:
                        slots(d)
                    if b is not None:
                        split_even(b, 0)
                    if c is not None:
                        residual(c)
                        norm2_stats(c)
                    if b is not None:
                        split_even(b, 1)
                    if a is not None:
                        q_lo(a)
                    if c is not None:
                        norm2(c)
                    if a is not None:
                        maxes(a, 0)
                    if b is not None:
                        split_even(b, 2)
                    if a is not None:
                        maxes(a, 1)
                    if b is not None:
                        context(b, 0)
                        split_even(b, 3)
                    if n is not None:
                        norm1_stats(n)
                    if b is not None:
                        ctx_low(b, 0)
                    if a is not None:
                        maxes(a, 2)
                        maxes(a, 3)
                    if c is not None:
                        route(c)
                    if b is not None:
                        context(b, 1)
                        ctx_low(b, 1)

                run_blocks(dve, step)

                tc = Chain(dve, s["chain_tab"], 10)
                tc.begin(0)
                dve.wait_ge(s["chain_slot"], 4 * NBLK)
                tc.link(dve.tensor_tensor(cnt[:], base[:], ecap[:], ALU.subtract))
                tc.link(dve.tensor_tensor(over[:], cnt[:].unsqueeze(2).broadcast_to([P, E, MIN_TILES]),
                                          th[:].unsqueeze(1).broadcast_to([P, E, MIN_TILES]), ALU.is_gt))
                tc.link(dve.tensor_reduce(ntl[:], over[:], AX.X, ALU.add))
                tc.link(dve.tensor_tensor(ctri[:], tri[:], ntl[:].unsqueeze(1).broadcast_to([P, E, E]), ALU.mult))
                tc.link(dve.tensor_reduce(cend[:], ctri[:], AX.X, ALU.add))
                tc.link(dve.tensor_tensor(ge[:], cend[:].unsqueeze(1).broadcast_to([P, NT, E]),
                                          ti[:].unsqueeze(2).broadcast_to([P, NT, E]), ALU.is_le))
                tc.add(dve.tensor_reduce(et[:], ge[:], AX.X, ALU.add))
                tc.link(dve.tensor_tensor(gen[:], ge[:], ntl[:].unsqueeze(1).broadcast_to([P, NT, E]), ALU.mult))
                tc.link(dve.tensor_reduce(cs[:], gen[:], AX.X, ALU.add))
                tc.link(dve.tensor_tensor(cs[:], ti[:], cs[:], ALU.subtract))
                tc.end()
                tl = Chain(dve, s["chain_tab2"], 3)
                tl.begin(0)
                tl.link(dve.tensor_scalar(cs[:], cs[:], float(TT), None, ALU.mult))
                tl.add(dve.scalar_tensor_tensor(row_f[:, 0, :], et[:], float(CAP), cs[:], ALU.mult, ALU.add))
                tl.link(dve.tensor_scalar(row_f[:, 1, :], et[:], float(E - 1), None, ALU.min))
                tl.end()
                dve.tensor_copy(padrow[:], base[:])
                dve.tensor_copy(tab[:], row_f[:]).then_inc(s["tab_ready"], 1)
                dve.wait_ge(s["tab_ready"], 1)

            @blk.tensor
            def _(pe):
                pe.wait_ge(s["consts_in"], 16 * NCONST)
                pe.wait_ge(s["pool_const"], POOL_CONST)
                for oc in range(HC):
                    for c in range(HC):
                        mm = pe.matmul(X[oc][:, 0:B * SK], wk_t[:, c, oc * P:(oc + 1) * P],
                                       ctx_t[:, c, :, 0, :], start=(c == 0), stop=(c == HC - 1))
                    mm.then_inc(s["setup_pe"], 1)
                for b in range(B):
                    o = SC[b // 2][:, (b % 2) * H:(b % 2 + 1) * H]
                    pe.matmul(o, ones_row[:], bv_r[:], start=True, stop=False)
                    for c in range(HC):
                        mm = pe.matmul(o, ctx_t[:, c, b].rearrange("p d k -> p (d k)"), wv_t[:, c, :],
                                       start=False, stop=(c == HC - 1))
                    if b % 2:
                        mm.then_inc(s["setup_pe"], 1)
                pe.matmul(O[0][:, 0:H], ones_row[:], bo_r[:], start=True, stop=True).then_inc(s["setup_pe"], 1)
                pe.wait_ge(s["setup_dve"], SETUP_DVE)

                def product(o, terms):
                    for n, (l, r) in enumerate(terms):
                        mm = pe.matmul(o, l, r, start=(n == 0), stop=(n == len(terms) - 1))
                    return mm

                def turn_x(a):
                    for c in range(HC):
                        for t in range(T):
                            if c == 0:
                                pe.wait_ge(s["xn_ready"], T * a.k + t + 1)
                            mm = pe.transpose(X[c][:, t * P:(t + 1) * P], xn[:, t, c * P:(c + 1) * P], identf[:])
                        mm.then_inc(s["xT_done"], 1)

                def queries(a):
                    pe.wait_ge(s["xnT_ready"], HC * (a.k + 1))
                    for oc in range(HC):
                        o = slice(oc * P, (oc + 1) * P)
                        product(X[oc][:], [(w[:, c, o], z[:, c, :]) for c in range(HC) for w, z in
                                           ((wq_h, xnT_h), (wq_l, xnT_h), (wq_h, xnT_l))])\
                            .then_inc(s["q_done"], 1)

                def token_scores(a, t):
                    pe.wait_ge(s["q_hi"], HC * (a.k + 1))
                    pe.wait_ge(s["mask_ready"], 2 * (a.k + 1))
                    for c in range(HC):
                        n = HC * T * a.k + HC * t + c
                        wait(pe, s["max_done"], n - 1)
                        if t == 0 and c == 0:
                            wait(pe, s["mx_ready"], a.k)
                        if t == 0 and c == 1:
                            wait(pe, s["slot_ready"], a.k - 2)
                        pe.matmul(SC[c][:], q_h[a.h][:, c, t * P:(t + 1) * P], kbd[:, a.m, c, :],
                                  start=True, stop=False)
                        pe.matmul(SC[c][:], ident_bf[:], mb[a.h][:, t, :].unsqueeze(1).broadcast_to([P, NH // 2, SK]),
                                  start=False, stop=True).then_inc(s["tok_scored"], 1)

                def turn_maxima(a):
                    pe.wait_ge(s["max_done"], HC * T * (a.k + 1))
                    for t in range(T):
                        mm = pe.transpose(SC[0][0:NH, t * P:(t + 1) * P], smax[:, t, :], identf[:])
                    mm.then_inc(s["mxT_done"], 1)

                def key_scores(b, g):
                    if g == 0:
                        pe.wait_ge(s["mx_ready"], b.k + 1)
                        pe.wait_ge(s["k_ready"], 2 * HC * (b.m + 1))
                        pe.wait_ge(s["q_ready"], HC * (b.k + 1))
                    for j in (2 * g, 2 * g + 1):
                        wait(pe, s["exp_done"], NPAIR * b.k + j - 1)
                        pe.matmul(TS[j % 2][:], sel[:, j, :], mx[b.h][:], start=True, stop=False)
                    for n, (kk, qq) in enumerate(((kp_h, q_h), (kp_l, q_h), (kp_h, q_l))):
                        for j in (2 * g, 2 * g + 1):
                            r, c = slice(32 * (j % 4), 32 * (j % 4) + 32), j // 4
                            mm = pe.matmul(TS[j % 2][:], kk[r, c, :], qq[b.h][r, c, :], start=False, stop=(n == 2))
                            if n == 2:
                                mm.then_inc(s["tsc_done"], 1)

                def values(b, g):
                    if g >= 2:
                        pe.wait_ge(s["den_ready"], 8 * b.k + 2 * g - 2)
                    if g == 0:
                        pe.wait_ge(s["v_ready"], 16 * (b.m + 1))
                    if g < 2:
                        wait(pe, s["x1_done"], 2 * (b.k - 1) + 2)
                    for j in (2 * g, 2 * g + 1):
                        i = j % NPB
                        pe.wait_ge((s["p_even"], s["p_odd"])[j % 2], 4 * b.k + g + 1)
                        for n, (vv, pp) in enumerate(((vbd_h, p_h), (vbd_l, p_h), (vbd_h, p_l))):
                            mm = pe.matmul(O[g % 2][:], vv[:, j, :], pp[i][:], start=(j % 2 == 0 and n == 0),
                                           stop=(j % 2 == 1 and n == 2))
                        mm.then_inc(s["pv_done"], 1)

                def project(b):
                    pe.wait_ge(s["ctx_ready"], HC * (b.k + 1))
                    for t in range(T):
                        z = slice(t * P, (t + 1) * P)
                        product(O[t // 2][:, (t % 2) * H:(t % 2 + 1) * H],
                                [(l[:, c, z], w[:, c, :]) for c in range(HC) for l, w in
                                 ((c_h, wo_h), (c_h, wo_l), (c_l, wo_h))]).then_inc(s["wo_done"], 1)

                def turn_x2(c):
                    pe.wait_ge(s["q_ready"], HC * min(c.k + 3, NBLK) if isinstance(c.k, int) else HC * (c.k + 3))
                    for i in range(HC):
                        for t in range(T):
                            if i == 0:
                                pe.wait_ge(s["xn2_ready"], T * c.k + t + 1)
                            mm = pe.transpose(X[i][:, t * P:(t + 1) * P], xn2[:, t, i * P:(i + 1) * P], identf[:])
                        mm.then_inc(s["x2T_done"], 1)

                def logits(c):
                    pe.wait_ge(s["xn2T_ready"], HC * (c.k + 1))
                    for i in range(HC):
                        mm = pe.matmul(X[0][0:E, :], wr_sb[:, i, :], xn2T[:, i, :], start=(i == 0), stop=(i == HC - 1))
                    mm.then_inc(s["lg_done"], 1)

                def turn_logits(c):
                    wait(pe, s["ez_ready"], c.k + 1, s["pe_passed"])
                    for t in range(T):
                        mm = pe.transpose(X[1][:, t * E:(t + 1) * E], ez[:, t * P:(t + 1) * P], identf[0:E, 0:E])
                    mm.then_inc(s["ezT_done"], 1)

                def ranks(c):
                    pe.wait_ge(s["onehot_ready"], c.k + 1)
                    pe.wait_ge(s["max_done"], HC * T * (min(c.k + 3, NBLK) if isinstance(c.k, int) else c.k + 3))
                    o = SC[1][:, 0:(T + 1) * E].rearrange("p (t e) -> p t e", e=E)
                    for t in range(T):
                        pe.matmul(o[:, t + 1:T + 1, :], ones_bf[:],
                                  onehot[:, t:t + 1, :].broadcast_to([P, T - t, E]),
                                  start=(t == 0), stop=False, skip_group_check=True)
                    mm = pe.matmul(o, before_bf[:], onehot[:], start=False, stop=True, skip_group_check=True)
                    mm.then_inc(s["rank_done"], 1)

                def step(n, a, b, c, d):
                    if a is not None:
                        wait(pe, s["q_ready"], HC * a.k)
                        wait(pe, s["onehot_ready"], a.k - 2)
                        turn_x(a)
                    if b is not None:
                        key_scores(b, 0)
                    if d is not None:
                        ranks(d)
                    if c is not None:
                        project(c)
                    if b is not None:
                        key_scores(b, 1)
                    if a is not None:
                        queries(a)
                    if b is not None:
                        values(b, 0)
                        key_scores(b, 2)
                    if a is not None:
                        token_scores(a, 0)
                    if b is not None:
                        values(b, 1)
                    if a is not None:
                        token_scores(a, 1)
                    if b is not None:
                        key_scores(b, 3)
                    if c is not None:
                        turn_x2(c)
                    if a is not None:
                        token_scores(a, 2)
                    if b is not None:
                        values(b, 2)
                    if c is not None:
                        logits(c)
                    if a is not None:
                        token_scores(a, 3)
                    if b is not None:
                        values(b, 3)
                    if c is not None:
                        turn_logits(c)
                    if a is not None:
                        turn_maxima(a)

                run_blocks(pe, step)
        A.close()

        g_sb = [sb(f"g{i}", [P, 2, ROW], f32) for i in range(2)]
        xe = sb("xe", [P, 2, H], f32)
        xeT_h = sb("xeT_h", [P, HC, TT], f32r)
        xeT_l = sb("xeT_l", [P, HC, TT], f32r)
        w1_h = [sb(f"w1_h{i}", [P, HC, F], f32r) for i in range(2)]
        w1_l = [sb(f"w1_l{i}", [P, HC, F], f32r) for i in range(2)]
        w2_h = [sb(f"w2_h{i}", [P, FC, H], f32r) for i in range(2)]
        w2_l = [sb(f"w2_l{i}", [P, FC, H], f32r) for i in range(2)]
        NU = FC // 2
        h_f = [sb(f"h_f{i}", [P, 2, TT], f32) for i in range(NU)]
        h_h = [sb(f"h_h{i}", [P, FC, TT], f32r) for i in range(2)]
        h_l = [sb(f"h_l{i}", [P, FC, TT], f32r) for i in range(2)]
        o_sb = [sb(f"o{i}", [P, 2, H], f32) for i in range(2)]
        o_idx = [sb(f"o_idx{i}", [P, 2], i32) for i in range(2)]
        HB = [bank[n] for n in ("S0", "S1", "T0", "T1")]
        w1_in, w2_in, g_in, osc = ([s[f"{n}{i}"] for i in range(2)] for n in ("w1_in", "w2_in", "g_in", "osc"))

        with nc.Block() as blk:

            @blk.sync
            def _(sp):
                def expert(b):
                    return sp.value_load(tab[0:1, 1, bass.ds(b.k, 1)], min_val=0, max_val=E - 1)

                def load_w1(b):
                    wait(sp, s["w1_ready"], b.k - 1, s["sp_passed"])
                    sp.dma_start(w1_raw[b.h][:], W1_v[bass.ds(expert(b), 1)].rearrange("e p c n -> p (e c) n"))\
                      .then_inc(w1_in[b.h], 16)

                def load_tile(b):
                    wait(sp, s["w2_ready"], b.k - 1, s["sp_passed"])
                    sp.dma_start(w2_raw[b.h][:], W2_v[bass.ds(expert(b), 1)].rearrange("e p c n -> p (e c) n"))\
                      .then_inc(w2_in[b.h], 16)
                    if isinstance(b.k, int) and b.k == 0:
                        sp.wait_ge(s["pads_done"], 16 * E)
                    wait(sp, s["o_ready"], 2 * (b.k - 1), s["sp_passed"])
                    r = sp.value_load(tab[0:1, 0, bass.ds(b.k, 1)], min_val=0, max_val=BINS - TT)
                    sp.dma_start(g_sb[b.h][:], bins[bass.ds(r, TT), :].rearrange("(n p) c -> p n c", p=P))\
                      .then_inc(g_in[b.h], 16)

                load_w1(Blk(0, 0))
                for e in range(E):
                    r = sp.value_load(padrow[0:1, e:e + 1], min_val=0, max_val=E * CAP - TT)
                    sp.dma_start(bins[bass.ds(r, TT), :].rearrange("(n p) c -> p n c", p=P),
                                 padding[:].unsqueeze(1).broadcast_to([P, TT // P, ROW])).then_inc(s["pads_done"], 16)
                load_tile(Blk(0, 0))
                load_w1(Blk(0, 1))
                load_w1(Blk(1, 0))
                load_tile(Blk(0, 1))
                with sp.Fori(0, (NT - 3) // 2) as i:
                    load_w1(Blk(i + 1, 1))
                    load_tile(Blk(i + 1, 0))
                    load_w1(Blk(i + 2, 0))
                    load_tile(Blk(i + 1, 1))
                load_tile(Blk((NT - 1) // 2, 0))

            @blk.gpsimd
            def _(pool):
                def store(b):
                    wait(pool, s["o_ready"], 2 * (b.k + 1), s["pool_passed"])
                    for t in range(2):
                        pool.indirect_dma_start(
                            out=out_rows, out_offset=bass.IndirectOffsetOnAxis(ap=o_idx[b.h][:, t:t + 1], axis=0),
                            in_=o_sb[b.h][:, t, :], in_offset=None, bounds_check=B * S - 1, oob_is_err=False)\
                            .then_inc(osc[b.h], 16)

                def step(w, a, b):
                    if b is not None:
                        store(b)

                run_tiles(pool, step)
                for h in range(2):
                    wait(pool, osc[h], 32 * ((NT + 1 - h) // 2), s["pool_passed"])

            @blk.scalar
            def _(act):
                def w1_high(w):
                    act.wait_ge(w1_in[w.h], 16 * (w.m + 1))
                    wait(act, s["l1_done"], NU * (w.k - 1))
                    act.copy(w1_h[w.h][:], w1_raw[w.h][:]).then_inc(s["w1_hi"], 1)

                def w2_high(a):
                    act.wait_ge(w2_in[a.h], 16 * (a.m + 1))
                    wait(act, s["y_done"], 2 * (a.k - 1))
                    act.copy(w2_h[a.h][:], w2_raw[a.h][:]).then_inc(s["w2_hi"], 1)

                def rows_high(a):
                    act.wait_ge(s["xeT_done"], a.k + 1)
                    act.copy(xeT_h[:].rearrange("p c n -> p (c n)"), X[0][:]).then_inc(s["xeT_hi"], 1)

                def hidden(a, u):
                    act.wait_ge(s["l1_done"], NU * a.k + u + 1)
                    wait(act, s["h_ready"], NU * (a.k - 1) + u + 1)
                    act.activation(h_f[u][:].rearrange("p c n -> p (c n)"), HB[u][:], ACT.Gelu)\
                       .then_inc(s["gelu_done"], 1)
                    if u == 0:
                        wait(act, s["y_done"], 2 * (a.k - 1))
                    act.wait_ge(s["gelu_done"], NU * a.k + u + 1)
                    act.copy(h_h[a.h][:, 2 * u:2 * u + 2, :], h_f[u][:]).then_inc(s["h_hi"], 1)

                def step(w, a, b):
                    if a is not None:
                        rows_high(a)
                        w2_high(a)
                    if w is not None:
                        w1_high(w)
                    if a is not None:
                        for u in range(NU):
                            hidden(a, u)

                run_tiles(act, step)

            @blk.vector
            def _(dve):
                def w1_low(w):
                    dve.wait_ge(s["w1_hi"], w.k + 1)
                    dve.tensor_tensor(w1_l[w.h][:], w1_raw[w.h][:], w1_h[w.h][:].bitcast(f32), ALU.subtract)\
                       .then_inc(s["w1_ready"], 1)

                def w2_low(a):
                    dve.wait_ge(s["w2_hi"], a.k + 1)
                    dve.tensor_tensor(w2_l[a.h][:], w2_raw[a.h][:], w2_h[a.h][:].bitcast(f32), ALU.subtract)\
                       .then_inc(s["w2_ready"], 1)

                def normalize(a):
                    dve.wait_ge(g_in[a.h], 16 * (a.m + 1))
                    wait(dve, s["xeT_done"], a.k)
                    g = g_sb[a.h]
                    for t in range(2):
                        dve.tensor_scalar(xe[:, t, :], g[:, t, 0:H], g[:, t, C_MEAN:C_MEAN + 1],
                                          g[:, t, C_RSTD:C_RSTD + 1], ALU.subtract, ALU.mult).then_inc(s["xe_ready"], 1)

                def hidden_low(a, u):
                    dve.wait_ge(s["h_hi"], NU * a.k + u + 1)
                    dve.tensor_tensor(h_l[a.h][:, 2 * u:2 * u + 2, :], h_f[u][:],
                                      h_h[a.h][:, 2 * u:2 * u + 2, :].bitcast(f32), ALU.subtract).then_inc(s["h_ready"], 1)

                def rows_low(a):
                    dve.wait_ge(s["xeT_hi"], a.k + 1)
                    dve.tensor_tensor(xeT_l[:].rearrange("p c n -> p (c n)"), X[0][:],
                                      xeT_h[:].rearrange("p c n -> p (c n)").bitcast(f32), ALU.subtract)\
                       .then_inc(s["xeT_ready"], 1)

                def output(b, t):
                    g = g_sb[b.h]
                    if t == 0:
                        wait(dve, osc[b.h], 32 * b.m)
                        dve.tensor_copy(o_idx[b.h][:], g[:, :, C_ID])
                    dve.wait_ge(s["y_done"], 2 * b.k + t + 1)
                    dve.scalar_tensor_tensor(o_sb[b.h][:, t, :], O[t][:, 0:H], g[:, t, C_COEF:C_COEF + 1],
                                             g[:, t, 0:H], ALU.mult, ALU.add).then_inc(s["o_ready"], 1)

                def step(w, a, b):
                    if a is not None:
                        rows_low(a)
                        w2_low(a)
                    if b is not None:
                        for t in range(2):
                            output(b, t)
                    if w is not None:
                        w1_low(w)
                    if a is not None:
                        for u in range(NU - 1):
                            hidden_low(a, u)
                    if w is not None:
                        normalize(w)
                    if a is not None:
                        hidden_low(a, NU - 1)

                run_tiles(dve, step)

            @blk.tensor
            def _(pe):
                def turn(a):
                    wait(pe, s["xeT_ready"], a.k)
                    for t in range(2):
                        pe.wait_ge(s["xe_ready"], 2 * a.k + t + 1)
                        for c in range(HC):
                            mm = pe.transpose(X[0][:, c * TT + t * P:c * TT + (t + 1) * P],
                                              xe[:, t, c * P:(c + 1) * P], identf[:])
                    mm.then_inc(s["xeT_done"], 1)

                def first_layer(a, u):
                    if u == 0:
                        pe.wait_ge(s["xeT_ready"], a.k + 1)
                        pe.wait_ge(s["w1_ready"], a.k + 1)
                    wait(pe, s["gelu_done"], NU * (a.k - 1) + u + 1)
                    for f in (2 * u, 2 * u + 1):
                        z = slice(f * P, (f + 1) * P)
                        terms = [(w[:, c, z], xx[:, c, :]) for c in range(HC) for w, xx in
                                 ((w1_h[a.h], xeT_h), (w1_h[a.h], xeT_l), (w1_l[a.h], xeT_h))]
                        for n, (l, r) in enumerate(terms):
                            mm = pe.matmul(HB[u][:, (f % 2) * TT:(f % 2 + 1) * TT], l, r,
                                           start=(n == 0), stop=(n == len(terms) - 1))
                    mm.then_inc(s["l1_done"], 1)

                def second_layer(b, t, chunks):
                    if t == 0 and chunks[0] == 0:
                        wait(pe, s["o_ready"], 2 * b.k)
                        pe.wait_ge(s["w2_ready"], b.k + 1)
                    z = slice(t * P, (t + 1) * P)
                    for f in chunks:
                        if t == 0 and f % 2 == 0:
                            pe.wait_ge(s["h_ready"], NU * b.k + f // 2 + 1)
                        for n, (hh, ww) in enumerate(((h_h, w2_h), (h_h, w2_l), (h_l, w2_h))):
                            mm = pe.matmul(O[t][:, 0:H], hh[b.h][:, f, z], ww[b.h][:, f, :],
                                           start=(f == 0 and n == 0), stop=(f == FC - 1 and n == 2))
                    if chunks[-1] == FC - 1:
                        mm.then_inc(s["y_done"], 1)

                def step(w, a, b):
                    if b is not None:
                        second_layer(b, 0, range(0, FC - 2))
                    if a is not None:
                        turn(a)
                    if b is not None:
                        second_layer(b, 0, range(FC - 2, FC))
                        second_layer(b, 1, range(FC))
                    if a is not None:
                        for u in range(NU):
                            first_layer(a, u)

                run_tiles(pe, step)


def kernel(**inputs):
    import numpy as np
    import concourse.bacc as bacc
    from concourse import mybir as mb
    from concourse.bass_utils import run_bass_kernel_spmd

    def host(name):
        return np.asarray(inputs[name])

    def flat_row(name):
        return np.ascontiguousarray(host(name).reshape(1, -1))

    arrays = {
        "x": host("x"),
        "ctxT": np.ascontiguousarray(host("ctx_1024").reshape(B * SK, H).T),
        "mask": host("mask_BxSxS2_if1"),
        "maskT": np.ascontiguousarray(host("mask_BxSxS2_if1").transpose(0, 2, 1)),
        "g_xattn": host("g_xattn").reshape(1), "g_ffn": host("g_ffn").reshape(1),
        "WqT": np.ascontiguousarray(host("L0_xattn_Wq").T),
        "bq": np.ascontiguousarray(host("L0_xattn_bq").reshape(HC, P).T),
        "WkT": np.ascontiguousarray(host("L0_xattn_Wk").T),
        "bk": np.ascontiguousarray(host("L0_xattn_bk").reshape(HC, P).T),
        "WvT": np.ascontiguousarray(host("L0_xattn_Wv").T), "bv": flat_row("L0_xattn_bv"),
        "WoT": np.ascontiguousarray(host("L0_xattn_Wo").T), "bo": flat_row("L0_xattn_bo"),
        "Wr": host("L0_ffn_Wr"), "br": np.ascontiguousarray(host("L0_ffn_br").reshape(E, 1)),
        "W1": host("L0_ffn_W1"), "W2": host("L0_ffn_W2"),
    }
    nc = bacc.Bacc("TRN2", target_bir_lowering=False, num_devices=1)
    args = [nc.dram_tensor(n, a.shape, mb.dt.from_np(a.dtype), kind="ExternalInput").ap() for n, a in arrays.items()]
    out = nc.dram_tensor("out", (B, S, H), mb.dt.float32, kind="ExternalOutput").ap()
    build(nc, *args, out)
    result = run_bass_kernel_spmd(nc, [{n: np.ascontiguousarray(a) for n, a in arrays.items()}], core_ids=[0])
    return result.results[0]["out"]
```

```python
import concourse.bass as bass
from concourse import mybir
from contextlib import ExitStack

B, S, H = 4, 1024, 256
SK = 64
NH, DK = 16, 16
E, F = 8, 1024
P = 128
HC = H // P
BLK, T = 512, 4
NBLK = B * S // BLK
NPAIR = NH // 2
BIG = float(2.0 ** 100)
TT = 256
CAP = B * S + TT
NT = (B * S + E * (TT - 1)) // TT
MIN_TILES = B * S // TT
BINS = (E + 1) * CAP
C_MEAN, C_RSTD, C_COEF, C_ID, ROW = H, H + 1, H + 2, H + 3, H + 4
NO_TOKEN = float(1 << 20)
FC = F // P
EPS = 1e-5


class Blk:

    def __init__(self, m, h):
        self.m, self.h, self.k = m, h, 2 * m + h


def wait(eng, sem, value, passed=None):
    if not isinstance(value, int) or value > 0:
        eng.wait_ge(sem, value)
        if passed is not None and not isinstance(value, int):
            eng.sem_inc(passed, 1)


def run_blocks(eng, step):
    step(Blk(0, 0), None, None, None, None)
    step(Blk(0, 1), Blk(0, 0), None, None, None)
    step(Blk(1, 0), Blk(0, 1), Blk(0, 0), None, None)
    step(Blk(1, 1), Blk(1, 0), Blk(0, 1), Blk(0, 0), None)
    with eng.Fori(0, B - 2) as i:
        step(Blk(i + 2, 0), Blk(i + 1, 1), Blk(i + 1, 0), Blk(i, 1), Blk(i, 0))
        step(Blk(i + 2, 1), Blk(i + 2, 0), Blk(i + 1, 1), Blk(i + 1, 0), Blk(i, 1))
    step(None, Blk(B - 1, 1), Blk(B - 1, 0), Blk(B - 2, 1), Blk(B - 2, 0))
    step(None, None, Blk(B - 1, 1), Blk(B - 1, 0), Blk(B - 2, 1))
    step(None, None, None, Blk(B - 1, 1), Blk(B - 1, 0))
    step(None, None, None, None, Blk(B - 1, 1))


def run_tiles(eng, step):
    assert NT % 2 == 1
    step(Blk(0, 0), None, None)
    step(Blk(0, 1), Blk(0, 0), None)
    step(Blk(1, 0), Blk(0, 1), Blk(0, 0))
    with eng.Fori(0, (NT - 3) // 2) as i:
        step(Blk(i + 1, 1), Blk(i + 1, 0), Blk(i, 1))
        step(Blk(i + 2, 0), Blk(i + 1, 1), Blk(i + 1, 0))
    last = (NT - 1) // 2
    step(None, Blk(last, 0), Blk(last - 1, 1))
    step(None, None, Blk(last, 0))


POOL_CONST, KEYS_DVE, QUERIES_DVE, VALUES_DVE, SETUP_DVE = 23, 4, 10, 32, 37


class Chain:

    def __init__(self, eng, sem, per):
        self.eng, self.sem, self.per = eng, sem, per

    def begin(self, k):
        self.base, self.n = self.per * k, 0

    def add(self, ins):
        self.n += 1
        return ins.then_inc(self.sem, 1)

    def sync(self):
        self.eng.wait_ge(self.sem, self.base + self.n)

    def link(self, ins):
        self.add(ins)
        self.sync()

    def end(self):
        assert self.n == self.per, (self.n, self.per)


def build(nc, x, ctxT, mask, maskT, g_xattn, g_ffn, WqT, bq, WkT, bk, WvT, bv, WoT, bo, Wr, br, W1, W2, out):
    f32, f32r, bf16, i32 = mybir.dt.float32, mybir.dt.float32r, mybir.dt.bfloat16, mybir.dt.int32
    ALU, ACT, AX = mybir.AluOpType, mybir.ActivationFunctionType, mybir.AxisListType

    bins = nc.dram_tensor("bins", (BINS, ROW), f32, kind="Internal").ap()
    x_v = x.rearrange("b (h t p) c -> (b h) p t c", h=2, t=T)
    mask_v = mask.rearrange("b (h t p) s -> (b h) p t s", h=2, t=T)
    maskT_v = maskT.rearrange("b s (h n) -> b h s n", h=2)
    W1_v = W1.rearrange("e (c p) n -> e p c n", p=P)
    W2_v = W2.rearrange("e (c p) n -> e p c n", p=P)
    out_rows = out.rearrange("b s c -> (b s) c")

    ctx = ExitStack()
    with ctx:
        def sem(name):
            return ctx.enter_context(nc.semaphore(name))

        def sb(name, shape, dt, scope=ctx):
            return scope.enter_context(nc.sbuf_tensor(name, shape, dt))

        bank = {n: ctx.enter_context(nc.psum_tensor(n, [P, 512], f32))
                for n in ("X0", "X1", "S0", "S1", "T0", "T1", "O0", "O1")}
        X, SC, TS, O = ([bank[f"{n}{i}"] for i in range(2)] for n in "XSTO")

        identf = sb("identf", [P, P], f32)
        padding = sb("padding", [P, ROW], f32)
        tab = sb("tab", [P, 2, NT], i32)
        w1_raw = [sb(f"w1_raw{i}", [P, HC, F], f32) for i in range(2)]
        w2_raw = [sb(f"w2_raw{i}", [P, FC, H], f32) for i in range(2)]

        A = ExitStack()
        ident_bf = sb("ident_bf", [P, P], bf16, A)
        ones_bf = sb("ones_bf", [P, P], bf16, A)
        before_bf = sb("before_bf", [P, P], bf16, A)
        headmask = sb("headmask", [P, NH // 2], f32, A)
        halfmask = sb("halfmask", [P, 2], f32, A)
        sel = sb("sel", [SK + NH, NPAIR, 2 * SK], f32r, A)
        ecap = sb("ecap", [P, E + 1], f32, A)
        ecap_i = sb("ecap_i", [P, E + 1], i32, A)
        base = sb("base", [P, E + 1], f32, A)
        tokid = sb("tokid", [P, T], f32, A)
        tokid_i = sb("tokid_i", [P, T], i32, A)
        prio = sb("prio", [P, E], f32, A)
        prio_i = sb("prio_i", [P, E], i32, A)
        half_exp = sb("half_exp", [P, T], f32, A)
        tg = sb("tg", [P, 2], f32, A)
        tgt = sb("tgt", [P, 2], f32, A)
        bq_c = sb("bq_c", [P, HC], f32, A)
        bk_c = sb("bk_c", [P, HC], f32, A)
        br_c = sb("br_c", [E, 1], f32, A)
        nbr_c = sb("nbr_c", [E, 1], f32, A)
        wr_sb = sb("wr_sb", [P, HC, E], f32, A)
        wq_h = sb("wq_h", [P, HC, H], f32r, A)
        wq_l = sb("wq_l", [P, HC, H], f32r, A)
        wo_h = sb("wo_h", [P, HC, H], f32r, A)
        wo_l = sb("wo_l", [P, HC, H], f32r, A)
        bo_b = sb("bo_b", [P, H], f32, A)
        kbd = sb("kbd", [P, B, HC, (NH // 2) * SK], f32r, A)
        kT_h = sb("kT_h", [P, HC, B, SK], f32r, A)
        kT_l = sb("kT_l", [P, HC, B, SK], f32r, A)
        kp_h = sb("kp_h", [P, HC, 2 * SK], f32r, A)
        kp_l = sb("kp_l", [P, HC, 2 * SK], f32r, A)
        v_h = sb("v_h", [P, B, H], f32r, A)
        v_l = sb("v_l", [P, B, H], f32r, A)
        VSTEP = P + 2 * DK
        vbd_h = sb("vbd_h", [P, HC, 4, VSTEP], f32r, A)
        vbd_l = sb("vbd_l", [P, HC, 4, VSTEP], f32r, A)
        xt = [sb(f"xt{i}", [P, T, H], f32, A) for i in range(2)]
        mi = [sb(f"mi{i}", [P, T, SK], i32, A) for i in range(2)]
        miT = [sb(f"miT{i}", [SK, BLK], i32, A) for i in range(2)]
        mb = [sb(f"mb{i}", [P, T, SK], bf16, A) for i in range(2)]
        mx = [sb(f"mx{i}", [SK + NH, BLK], f32r, A) for i in range(2)]
        st = sb("st", [P, T, 6], f32, A)
        mv = sb("mv", [P, T, 2], f32, A)
        ve = sb("ve", [P, T], f32, A)
        rs = sb("rs", [P, T], f32, A)
        nm = sb("nm", [P, T], f32, A)
        xn = sb("xn", [P, T, H], f32, A)
        xnT_h = sb("xnT_h", [P, HC, BLK], f32r, A)
        xnT_l = sb("xnT_l", [P, HC, BLK], f32r, A)
        q_h = [sb(f"q_h{i}", [P, HC, BLK], f32r, A) for i in range(2)]
        q_l = [sb(f"q_l{i}", [P, HC, BLK], f32r, A) for i in range(2)]
        smax = sb("smax", [P, T, NH], f32, A)
        NPB = 4
        p_f = [sb(f"p_f{i}", [P, BLK], f32, A) for i in range(NPB)]
        p_h = [sb(f"p_h{i}", [P, BLK], f32r, A) for i in range(NPB)]
        p_l = [sb(f"p_l{i}", [P, BLK], f32r, A) for i in range(NPB)]
        den = sb("den", [P, HC, BLK], f32, A)
        rden = sb("rden", [P, BLK], f32, A)
        cn = sb("cn", [P, HC, BLK], f32, A)
        c_h = sb("c_h", [P, HC, BLK], f32r, A)
        c_l = sb("c_l", [P, HC, BLK], f32r, A)
        pay = [sb(f"pay{i}", [P, T, ROW], f32, A) for i in range(2)]
        st2 = sb("st2", [P, T, 6], f32, A)
        mv2 = sb("mv2", [P, T, 2], f32, A)
        ve2 = sb("ve2", [P, T], f32, A)
        xn2 = sb("xn2", [P, T, H], f32, A)
        xn2T = sb("xn2T", [P, HC, BLK], f32, A)
        ez = sb("ez", [E, BLK], f32, A)
        e1 = sb("e1", [P, T, E], f32, A)
        pr = sb("pr", [P, T, E], f32, A)
        pm = sb("pm", [P, T], f32, A)
        eq = sb("eq", [P, T, E], f32, A)
        w_ = sb("w_", [P, T, E], f32, A)
        wm = sb("wm", [P, T], f32, A)
        onehot = sb("onehot", [P, T + 1, E], bf16, A)
        rk = sb("rk", [P, T, E], f32, A)
        rsel = sb("rsel", [P, T, E], f32, A)
        slot_f = sb("slot_f", [P, T], f32, A)
        slot = [sb(f"slot{i}", [P, T], i32, A) for i in range(2)]
        th_i = sb("th_i", [P, MIN_TILES], i32, A)
        th = sb("th", [P, MIN_TILES], f32, A)
        cnt = sb("cnt", [P, E], f32, A)
        over = sb("over", [P, E, MIN_TILES], f32, A)
        ntl = sb("ntl", [P, E], f32, A)
        tri = sb("tri", [P, E, E], f32, A)
        ctri = sb("ctri", [P, E, E], f32, A)
        cend = sb("cend", [P, E], f32, A)
        ti_i = sb("ti_i", [P, NT], i32, A)
        ti = sb("ti", [P, NT], f32, A)
        ge = sb("ge", [P, NT, E], f32, A)
        gen = sb("gen", [P, NT, E], f32, A)
        et = sb("et", [P, NT], f32, A)
        cs = sb("cs", [P, NT], f32, A)
        step_end = sb("step_end", [P, E], f32, A)
        gel = sb("gel", [P, NT, E], f32, A)
        lim = sb("lim", [P, NT], f32, A)
        start = sb("start", [P, NT], f32, A)
        row_f = sb("row_f", [P, 2, NT], f32, A)
        s = {n: sem(n) for n in (
            "keys_in", "wq_in", "wv_in", "wo_in", "router_in", "keys_twice", "kbd_ready", "x_in0", "x_in1", "m_in0", "m_in1",
            "pool_const", "setup_dve", "setup_act", "setup_pe",
            "tmask_ready", "kmask_ready", "xb_done", "rstd_ready", "x_centred", "negated", "rstd2_ready", "k_ready", "v_ready",
            "stat_ready", "xn_ready", "xT_done", "xnT_hi", "xnT_ready", "q_done", "rows_in0", "rows_in1", "den_ready", "ezT_done", "ez_used", "q_hi", "q_ready",
            "tok_scored", "max_done", "mxT_done", "mx_ready",
            "tsc_done", "exp_done", "p_hi", "p_low", "pv_done", "ctx_done", "ctx_hi", "ctx_lo0", "ctx_lo1", "wo_done",
            "x1_done",
            "stat2_ready", "xn2_ready", "x2T_done", "xn2T_ready", "lg_done", "ez_ready", "pay_ready",
            "onehot_ready", "rank_done", "slot_ready", "scat0", "scat1",
            "stats1", "stats2", "eps1", "eps2", "chain_ctx", "chain_high", "chain_route", "chain_slot", "chain_tab", "chain_tab2",
            "tab_ready", "osc0", "osc1", "pool_passed", "sp_passed", "dve_passed", "pe_passed",
            "w1_in0", "w1_in1", "w2_in0", "w2_in1", "g_in0", "g_in1",
            "w1_hi", "w1_ready", "w2_hi", "w2_ready", "xe_ready", "xeT_done", "xeT_hi", "xeT_ready",
            "l1_done", "gelu_done", "h_hi", "h_ready", "y_done", "o_ready",
        )}
        x_in = [s["x_in0"], s["x_in1"]]
        m_in = [s["m_in0"], s["m_in1"]]
        scat = [s["scat0"], s["scat1"]]
        rows_in = [s["rows_in0"], s["rows_in1"]]

        sel_f = cn[0:SK + NH].rearrange("p c n -> p (c n)").rearrange("p (j h k) -> p j h k", h=2, k=SK)
        ctx_t = xn2T[:].rearrange("p c (b d k) -> p c b d k", b=B, d=2)
        bv_b, bo_r = p_f[1][:, 0:H], den[:, 0, 0:H]
        vf = [p_f[2 + i][:].rearrange("p (b c) -> p b c", b=2) for i in range(2)]
        wv_t, wos = (z[:, 0:HC, 0:H] for z in pay)
        wk_t, wq_t = xn2[:, 0:HC, :], xn2[:, HC:2 * HC, :]
        kT = p_f[0][:].rearrange("p (c b k) -> p c b k", c=HC, b=B)
        wo_t = rden[:].rearrange("p (c n) -> p c n", c=HC)

        w_in = [[s[f"w{n + 1}_in{i}"] for i in range(2)] for n in range(2)]

        def load_weights(sp, layer, b):
            e = sp.value_load(tab[0:1, 1, bass.ds(b.k, 1)], min_val=0, max_val=E - 1)
            sp.dma_start((w1_raw, w2_raw)[layer][b.h][:],
                         (W1_v, W2_v)[layer][bass.ds(e, 1)].rearrange("e p c n -> p (e c) n"))\
              .then_inc(w_in[layer][b.h], 16)

        with nc.Block() as blk:
            @blk.sync
            def _(sp):
                def const(name, dst, src):
                    sp.dma_start(dst, src).then_inc(s[name], 16)

                def weights(name, dst, w):
                    const(name, dst, w.rearrange("(c p) n -> p c n", p=P))

                def load(n):
                    load_x(n)
                    load_masks(n)

                def load_x(n):
                    wait(sp, s["xn_ready"], T * (n.k - 1), s["sp_passed"])
                    sp.dma_start(xt[n.h][:], x_v[n.k]).then_inc(x_in[n.h], 16)

                def load_masks(n):
                    wait(sp, s["tmask_ready"], n.k - 1, s["sp_passed"])
                    sp.dma_start(mi[n.h][:], mask_v[n.k]).then_inc(m_in[n.h], 16)
                    wait(sp, s["kmask_ready"], n.k - 1, s["sp_passed"])
                    sp.dma_start(miT[n.h][:], maskT_v[n.m, n.h]).then_inc(m_in[n.h], 16)

                def load_rows(b):
                    if isinstance(b.k, int) and b.k < 2:
                        sp.wait_ge(s["setup_dve"], SETUP_DVE)
                    wait(sp, scat[b.h], 16 + 16 * T * b.m, s["sp_passed"])
                    sp.dma_start(pay[b.h][:, :, 0:H], x_v[b.k]).then_inc(rows_in[b.h], 16)

                def step(n, a, b, c, d):
                    if n is not None and not (isinstance(n.k, int) and n.k == 0):
                        load(n)
                    if c is not None:
                        load_rows(c)

                for c in range(HC):
                    const("keys_in", ctx_t[:, c, :, 0, :], ctxT[c * P:(c + 1) * P, :].rearrange("p (b k) -> p b k", b=B))
                weights("keys_in", wk_t, WkT)
                const("keys_in", bk_c[:], bk)
                load_x(Blk(0, 0))
                weights("wq_in", wq_t, WqT)
                const("wq_in", bq_c[:], bq)
                weights("wv_in", wv_t, WvT)
                const("wv_in", bv_b, bv.partition_broadcast(P))
                load_masks(Blk(0, 0))
                weights("wo_in", wo_t, WoT)
                const("wo_in", tg[:, 0:1], g_xattn.partition_broadcast(P))
                const("wo_in", tg[:, 1:2], g_ffn.partition_broadcast(P))
                const("wo_in", bo_r, bo.partition_broadcast(P))
                weights("router_in", wr_sb[:], Wr)
                const("router_in", br_c[:], br)
                run_blocks(sp, step)

                sp.wait_ge(s["tab_ready"], 1)
                load_weights(sp, 0, Blk(0, 0))

            @blk.gpsimd
            def _(pool):
                n = 0

                def done(ins):
                    nonlocal n
                    n += 1
                    ins.then_inc(s["pool_const"], 1)

                def sync():
                    pool.wait_ge(s["pool_const"], n)

                done(pool.memset(identf[:], 0.0))
                done(pool.memset(padding[:], 0.0))
                done(pool.memset(ones_bf[:], 1.0))
                done(pool.memset(before_bf[:], 1.0))
                done(pool.memset(headmask[:], 1.0))
                done(pool.memset(sel_f, 0.0))
                done(pool.memset(half_exp[:], -0.5))
                done(pool.memset(onehot[:], 0.0))
                done(pool.memset(tri[:], 1.0))
                done(pool.iota(ecap_i[:], [[CAP, E + 1]], base=TT, channel_multiplier=0))
                done(pool.iota(tokid_i[:], [[P, T]], base=0, channel_multiplier=1))
                done(pool.iota(prio_i[:], [[-1, E]], base=E, channel_multiplier=0))
                done(pool.iota(th_i[:], [[TT, MIN_TILES]], base=0, channel_multiplier=0))
                done(pool.iota(ti_i[:], [[1, NT]], base=0, channel_multiplier=0))
                sync()
                done(pool.memset(padding[:, C_ID:C_ID + 1], NO_TOKEN))
                done(pool.affine_select(out=identf[:], in_=identf[:], compare_op=ALU.not_equal, fill=1.0,
                                        base=0, pattern=[[-1, P]], channel_multiplier=1))
                done(pool.affine_select(out=before_bf[:], in_=before_bf[:], compare_op=ALU.is_gt, fill=0.0,
                                        base=0, pattern=[[1, P]], channel_multiplier=-1))
                done(pool.affine_select(out=headmask[:], in_=headmask[:], compare_op=ALU.is_ge, fill=0.0,
                                        base=0, pattern=[[-DK, NH // 2]], channel_multiplier=1))
                done(pool.affine_select(out=sel_f[0:SK], in_=sel_f[0:SK], compare_op=ALU.not_equal, fill=1.0,
                                        base=0, pattern=[[0, NPAIR], [0, 2], [-1, SK]], channel_multiplier=1))
                sync()
                done(pool.affine_select(out=sel_f[SK:SK + NH], in_=sel_f[SK:SK + NH], compare_op=ALU.not_equal,
                                        fill=-1.0, base=0, pattern=[[-2, NPAIR], [-1, 2], [0, SK]],
                                        channel_multiplier=1))
                sync()
                done(pool.affine_select(out=tri[:], in_=tri[:], compare_op=ALU.is_ge, fill=0.0,
                                        base=0, pattern=[[1, E], [-1, E]], channel_multiplier=0))
                sync()
                done(pool.affine_select(out=headmask[:], in_=headmask[:], compare_op=ALU.is_ge, fill=0.0,
                                        base=DK - 1, pattern=[[DK, NH // 2]], channel_multiplier=-1))
                done(pool.tensor_copy(ident_bf[:], identf[:]))
                assert n == POOL_CONST
                sync()
                def padding_tiles():
                    regions = bins.rearrange("(e r) c -> r e c", e=E + 1)
                    for h in range(2):
                        pool.dma_start(regions[h * P:(h + 1) * P],
                                       padding[:].unsqueeze(1).broadcast_to([P, E + 1, ROW])).then_inc(scat[h], 16)

                def token_masks(a):
                    wait(pool, m_in[a.h], 32 * (a.m + 1), s["pool_passed"])
                    wait(pool, s["tok_scored"], 2 * T * (a.k - 1), s["pool_passed"])
                    pool.tensor_scalar(mb[a.h][:], mi[a.h][:], 0.0, -BIG, ALU.is_equal, ALU.mult)\
                        .then_inc(s["tmask_ready"], 1)

                def key_masks(a):
                    wait(pool, s["tsc_done"], NPAIR * (a.k - 1), s["pool_passed"])
                    pool.tensor_scalar(mx[a.h][0:SK, :], miT[a.h][:], 0.0, -BIG, ALU.is_equal, ALU.mult)\
                        .then_inc(s["kmask_ready"], 1)

                def bias_rows(b):
                    if isinstance(b.k, int) and b.k == 0:
                        pool.wait_ge(s["setup_dve"], SETUP_DVE)
                    wait(pool, rows_in[b.h], 16 * (b.m + 1), s["pool_passed"])
                    pool.tensor_tensor(pay[b.h][:, :, 0:H], pay[b.h][:, :, 0:H],
                                       bo_b[:].unsqueeze(1).broadcast_to([P, T, H]),
                                       ALU.add).then_inc(s["xb_done"], 1)

                def rstd(b, moments, eps_out, result, ready, done_, steps):
                    wait(pool, ready, T * (b.k + 1), s["pool_passed"])
                    pool.tensor_scalar(eps_out[:], moments[:, :, 1], EPS, None, ALU.add).then_inc(steps, 1)
                    wait(pool, steps, b.k + 1, s["pool_passed"])
                    pool.tensor_tensor(result, eps_out[:], half_exp[:], ALU.pow).then_inc(done_, 1)

                def norm1_scales(n):
                    wait(pool, s["stat_ready"], T * (n.k + 1), s["pool_passed"])
                    wait(pool, s["x_centred"], T * n.k, s["pool_passed"])
                    pool.tensor_scalar(nm[:], mv[:, :, 0], -1.0, None, ALU.mult).then_inc(s["negated"], 1)
                    wait(pool, s["xn_ready"], T * n.k, s["pool_passed"])
                    rstd(n, mv, ve, rs[:], s["stat_ready"], s["rstd_ready"], s["eps1"])
                    if isinstance(n.k, int) and n.k == 0:
                        other_keys()
                        padding_tiles()

                def keys(m):
                    wait(pool, s["tsc_done"], NPAIR * 2 * m, s["pool_passed"])
                    for src, dst in ((kT_h, kp_h), (kT_l, kp_l)):
                        for c in range(HC):
                            pool.tensor_tensor(
                                dst[:, c, :].rearrange("p (h k) -> p h k", h=2),
                                src[:, c, m, :].bitcast(f32).unsqueeze(1).broadcast_to([P, 2, SK]),
                                halfmask[:].unsqueeze(2).broadcast_to([P, 2, SK]), ALU.mult)\
                                .then_inc(s["k_ready"], 1)

                def scatter(b):
                    wait(pool, s["slot_ready"], b.k + 1, s["pool_passed"])
                    wait(pool, s["pay_ready"], 2 * (b.k + 1), s["pool_passed"])
                    wait(pool, s["rstd2_ready"], b.k + 1, s["pool_passed"])
                    for t in range(T):
                        pool.indirect_dma_start(
                            out=bins, out_offset=bass.IndirectOffsetOnAxis(ap=slot[b.h][:, t:t + 1], axis=0),
                            in_=pay[b.h][:, t, :], in_offset=None).then_inc(scat[b.h], 16)

                def split(b, g):
                    for j in (2 * g, 2 * g + 1):
                        i = j % NPB
                        wait(pool, s["p_hi"], NPAIR * b.k + j + 1, s["pool_passed"])
                        pool.tensor_tensor(p_l[i][:], p_f[i][:], p_h[i][:].bitcast(f32), ALU.subtract)\
                            .then_inc(s["p_low"], 1)

                def ctx_low(b):
                    wait(pool, s["ctx_hi"], b.k + 1, s["pool_passed"])
                    pool.tensor_tensor(c_l[:, 0, :], cn[:, 0, :], c_h[:, 0, :].bitcast(f32), ALU.subtract)\
                        .then_inc(s["ctx_lo0"], 1)

                def norm2_scale(c):
                    rstd(c, mv2, ve2, pay[c.h][:, :, C_RSTD], s["stat2_ready"], s["rstd2_ready"], s["eps2"])

                def other_keys():
                    pool.wait_ge(s["setup_dve"], KEYS_DVE + 1)
                    for m in range(1, B):
                        for c in range(HC):
                            pool.tensor_tensor(
                                kbd[:, m, c, :].rearrange("p (h k) -> p h k", k=SK),
                                kT_h[:, c, m, :].bitcast(f32).unsqueeze(1).broadcast_to([P, NH // 2, SK]),
                                headmask[:].unsqueeze(2).broadcast_to([P, NH // 2, SK]), ALU.mult)\
                                .then_inc(s["kbd_ready"], 1)

                def batch_keys(a):
                    if isinstance(a.k, int) and a.k == 0:
                        pool.wait_ge(s["setup_dve"], VALUES_DVE)
                    keys(a.m)

                def step(n, a, b, c, d):
                    if a is not None:
                        token_masks(a)
                    if b is not None:
                        split(b, 0)
                    if c is not None:
                        ctx_low(c)
                    if n is not None:
                        norm1_scales(n)
                    if b is not None:
                        split(b, 1)
                    if c is not None:
                        bias_rows(c)
                    if b is not None:
                        split(b, 2)
                    if c is not None:
                        norm2_scale(c)
                    if b is not None and a is None:
                        scatter(d)
                    if a is not None:
                        key_masks(a)
                    if a is not None and a.h == 0:
                        batch_keys(a)
                    if b is not None and a is not None:
                        split(b, 3)
                    if d is not None and not (b is not None and a is None):
                        scatter(d)

                run_blocks(pool, step)
                for h in range(2):
                    wait(pool, scat[h], 16 + 16 * T * NBLK // 2, s["pool_passed"])

            @blk.scalar
            def _(act):
                act.wait_ge(s["keys_in"], 16 * (HC + 2))
                act.copy(ctx_t[:, :, :, 1, :], ctx_t[:, :, :, 0, :]).then_inc(s["keys_twice"], 1)
                act.wait_ge(s["wo_in"], 16 * 4)
                act.activation(tgt[:], tg[:], ACT.Tanh).then_inc(s["setup_act"], 1)

                def norm1(n):
                    act.wait_ge(s["negated"], n.k + 1)
                    wait(act, s["xT_done"], HC * n.k)
                    for t in range(T):
                        act.activation(xn[:, t, :], xt[n.h][:, t, :], ACT.Identity, bias=nm[:, t:t + 1])\
                           .then_inc(s["x_centred"], 1)
                    act.wait_ge(s["rstd_ready"], n.k + 1)
                    for t in range(T):
                        act.wait_ge(s["x_centred"], T * n.k + t + 1)
                        act.activation(xn[:, t, :], xn[:, t, :], ACT.Copy, scale=rs[:, t:t + 1])\
                           .then_inc(s["xn_ready"], 1)

                def xn_hi(a, c):
                    act.wait_ge(s["xT_done"], HC * a.k + c + 1)
                    wait(act, s["q_done"], HC * a.k)
                    act.copy(xnT_h[:, c, :], X[c][:]).then_inc(s["xnT_hi"], 1)

                def q_hi(a):
                    for c in range(HC):
                        act.wait_ge(s["q_done"], HC * a.k + c + 1)
                        wait(act, s["tsc_done"], NPAIR * (a.k - 1))
                        act.activation(q_h[a.h][:, c, :], X[c][:], ACT.Identity, bias=bq_c[:, c:c + 1])\
                           .then_inc(s["q_hi"], 1)

                def maxima(a):
                    act.wait_ge(s["mxT_done"], a.k + 1)
                    act.copy(mx[a.h][SK:SK + NH, :], SC[0][0:NH, :]).then_inc(s["mx_ready"], 1)

                def exps(b, g):
                    if isinstance(b.k, int) and b.k == 0 and g == 0:
                        act.wait_ge(s["setup_dve"], VALUES_DVE)
                    for j in (2 * g, 2 * g + 1):
                        n = NPAIR * b.k + j
                        act.wait_ge(s["tsc_done"], n + 1)
                        wait(act, s["p_low"], n - NPB + 1)
                        act.activation(p_f[j % NPB][:], TS[j % 2][:], ACT.Exp).then_inc(s["exp_done"], 1)
                    for j in (2 * g, 2 * g + 1):
                        n = NPAIR * b.k + j
                        act.wait_ge(s["exp_done"], n + 1)
                        wait(act, s["pv_done"], n - NPB + 1)
                        act.copy(p_h[j % NPB][:], p_f[j % NPB][:]).then_inc(s["p_hi"], 1)

                def sums(b, g):
                    act.wait_ge(s["pv_done"], NPAIR * b.k + 2 * g + 2)
                    v, r = 64 * (g % 2), 64 - 64 * (g % 2)
                    if isinstance(b.k, int) and b.k == 0 and g == 0:
                        act.wait_ge(s["setup_dve"], SETUP_DVE)
                    if g % 2 == 0:
                        wait(act, s["ctx_done"], 2 * (b.k - 1) + g // 2 + 1)
                        wait(act, (s["ctx_lo0"], s["ctx_lo1"])[g // 2], b.k)
                    act.copy(den[v:v + 64, g // 2, :], O[g % 2][r:r + 64, :]).then_inc(s["den_ready"], 1)
                    act.copy(cn[v:v + 64, g // 2, :], O[g % 2][v:v + 64, :]).then_inc(s["den_ready"], 1)

                def place_values(m):
                    if isinstance(m, int) and m == 0:
                        act.wait_ge(s["setup_dve"], SETUP_DVE)
                    wait(act, s["pv_done"], NPAIR * 2 * m)
                    for src, dst in ((v_h, vbd_h), (v_l, vbd_l)):
                        for h2 in range(2):
                            r = slice(h2 * SK, (h2 + 1) * SK)
                            act.copy(
                                dst[r, :, :, DK * h2:DK * h2 + DK],
                                src[r, m, :].rearrange("p (c i h d) -> p c i h d", i=4, h=2, d=DK)[:, :, :, h2, :])\
                                .then_inc(s["v_ready"], 1)

                def ctx_high(b):
                    act.wait_ge(s["ctx_done"], 2 * b.k + 1)
                    wait(act, s["wo_done"], T * b.k)
                    act.copy(c_h[:, 0, :], cn[:, 0, :]).then_inc(s["ctx_hi"], 1)

                def xn2_copy(c):
                    for i in range(HC):
                        act.wait_ge(s["x2T_done"], HC * c.k + i + 1)
                        act.copy(xn2T[:, i, :], X[i][:]).then_inc(s["xn2T_ready"], 1)

                def route_exp(c):
                    act.wait_ge(s["lg_done"], c.k + 1)
                    wait(act, s["ezT_done"], c.k)
                    act.activation(ez[:], X[1][0:E, :], ACT.Exp, bias=nbr_c[:, 0:1], scale=-1.0)\
                       .then_inc(s["ez_ready"], 1)

                def step(n, a, b, c, d):
                    if b is not None:
                        exps(b, 0)
                    if c is not None and b is not None:
                        sums(c, 3)
                    if c is not None:
                        ctx_high(c)
                    if b is not None and b.h == 0:
                        place_values(b.m)
                    if b is not None:
                        exps(b, 1)
                    if a is not None:
                        q_hi(a)
                    if b is not None:
                        sums(b, 0)
                        exps(b, 2)
                    if n is not None:
                        norm1(n)
                    if b is not None:
                        sums(b, 1)
                        exps(b, 3)
                    if c is not None:
                        xn2_copy(c)
                    if b is not None:
                        sums(b, 2)
                    if b is not None and a is None:
                        sums(b, 3)
                    if c is not None:
                        route_exp(c)
                    if n is not None:
                        xn_hi(n, 0)
                    if a is not None:
                        maxima(a)
                    if n is not None:
                        xn_hi(n, 1)

                run_blocks(act, step)

            @blk.vector
            def _(dve):
                su = Chain(dve, s["setup_dve"], SETUP_DVE)
                su.begin(0)
                su.add(dve.memset(vbd_h[:].bitcast(f32), 0.0))
                su.add(dve.memset(vbd_l[:].bitcast(f32), 0.0))

                def key_setup():
                    dve.wait_ge(s["keys_in"], 16 * (HC + 2))
                    for c in range(HC):
                        dve.wait_ge(s["setup_pe"], c + 1)
                        su.add(dve.tensor_scalar(kT[:, c], X[c][:, 0:B * SK].rearrange("p (b k) -> p b k", b=B),
                                                 bk_c[:, c:c + 1], DK ** -0.5, ALU.add, ALU.mult))
                    assert su.n == KEYS_DVE
                    su.sync()
                    su.link(dve.tensor_copy(kT_h[:], kT[:]))
                    su.add(dve.tensor_tensor(kT_l[:], kT[:], kT_h[:].bitcast(f32), ALU.subtract))
                    dve.wait_ge(s["pool_const"], POOL_CONST)
                    for c in range(HC):
                        su.add(dve.tensor_tensor(
                            kbd[:, 0, c, :].rearrange("p (h k) -> p h k", k=SK),
                            kT_h[:, c, 0, :].bitcast(f32).unsqueeze(1).broadcast_to([P, NH // 2, SK]),
                            headmask[:].unsqueeze(2).broadcast_to([P, NH // 2, SK]), ALU.mult))
                    dve.wait_ge(s["wq_in"], 32)
                    su.link(dve.tensor_copy(wq_h[:], wq_t))
                    su.add(dve.tensor_tensor(wq_l[:], wq_t, wq_h[:].bitcast(f32), ALU.subtract))
                    assert su.n == QUERIES_DVE
                    for h2 in range(2):
                        for i in range(4):
                            o = P * i + (SK if i < 2 else 0) + 2 * DK * (i % 2) + DK * h2
                            su.add(dve.memset(vbd_h[h2 * SK:(h2 + 1) * SK].rearrange("p c i n -> p c (i n)")
                                              [:, :, o:o + DK].bitcast(f32), 1.0))
                    su.add(dve.tensor_copy(sel[:], sel_f.rearrange("p j h k -> p j (h k)")))
                    su.add(dve.tensor_reduce(halfmask[:], headmask[:].rearrange("p (a h) -> p h a", h=2), AX.X, ALU.add))
                    su.add(dve.tensor_copy(ecap[:], ecap_i[:]))
                    su.add(dve.tensor_copy(base[:], ecap_i[:]))
                    su.add(dve.tensor_copy(tokid[:], tokid_i[:]))
                    su.add(dve.tensor_copy(prio[:], prio_i[:]))
                    su.add(dve.tensor_copy(th[:], th_i[:]))
                    su.add(dve.tensor_copy(ti[:], ti_i[:]))

                def value_setup():
                    dve.wait_ge(s["wv_in"], 32)
                    for n in range(2):
                        dve.wait_ge(s["setup_pe"], 3 + n)
                        su.link(dve.tensor_tensor(vf[n], SC[n][:].rearrange("p (b c) -> p b c", b=2),
                                                  bv_b.unsqueeze(1).broadcast_to([P, 2, H]), ALU.add))
                        su.link(dve.tensor_copy(v_h[:, 2 * n:2 * n + 2, :], vf[n]))
                        su.add(dve.tensor_tensor(v_l[:, 2 * n:2 * n + 2, :], vf[n],
                                                 v_h[:, 2 * n:2 * n + 2, :].bitcast(f32), ALU.subtract))
                    assert su.n == VALUES_DVE

                def last_setup():
                    dve.wait_ge(s["router_in"], 32)
                    dve.wait_ge(s["setup_act"], 1)
                    su.add(dve.tensor_scalar(nbr_c[:], br_c[:], -1.0, None, ALU.mult))
                    su.link(dve.tensor_scalar(wos, wo_t, tgt[:, 0:1], None, ALU.mult))
                    su.link(dve.tensor_copy(wo_h[:], wos))
                    su.add(dve.tensor_tensor(wo_l[:], wos, wo_h[:].bitcast(f32), ALU.subtract))
                    su.add(dve.tensor_scalar(bo_b[:], bo_r, tgt[:, 0:1], None, ALU.mult))
                    su.end()

                def norm_stats(b, src, stats, moments, ready, ch):
                    for t in range(T):
                        ch.add(dve.bn_stats(stats[:, t, :], src[:, t, 0:H]))
                    wait(dve, ch.sem, ch.base + ch.n, s["dve_passed"])
                    for t in range(T):
                        dve.bn_aggr(moments[:, t, :], stats[:, t, :]).then_inc(ready, 1)

                lnc = Chain(dve, s["stats1"], T)
                ln2c = Chain(dve, s["stats2"], T)

                def x_ready(n):
                    dve.wait_ge(x_in[n.h], 16 * (n.m + 1))
                    wait(dve, s["x_centred"], T * n.k, s["dve_passed"])
                    lnc.begin(n.k)

                def x_stats(n, t):
                    lnc.add(dve.bn_stats(st[:, t, :], xt[n.h][:, t, :]))

                def x_moments(n, t):
                    if t == 0:
                        wait(dve, lnc.sem, lnc.base + T, s["dve_passed"])
                    dve.bn_aggr(mv[:, t, :], st[:, t, :]).then_inc(s["stat_ready"], 1)

                def xn_lo(a):
                    for c in range(HC):
                        dve.wait_ge(s["xnT_hi"], HC * a.k + c + 1)
                        dve.tensor_tensor(xnT_l[:, c, :], X[c][:], xnT_h[:, c, :].bitcast(f32), ALU.subtract)\
                           .then_inc(s["xnT_ready"], 1)

                def q_lo(a, c):
                    dve.wait_ge(s["q_hi"], HC * a.k + c + 1)
                    dve.scalar_tensor_tensor(q_l[a.h][:, c, :], X[c][:], bq_c[:, c:c + 1],
                                             q_h[a.h][:, c, :].bitcast(f32), ALU.add, ALU.subtract)\
                       .then_inc(s["q_ready"], 1)

                def maxes(a, t):
                    for c in range(HC):
                        n = HC * T * a.k + HC * t + c
                        dve.wait_ge(s["tok_scored"], n + 1)
                        if t == 0 and c == 0:
                            wait(dve, s["mxT_done"], a.k)
                        dve.tensor_reduce(smax[:, t, c * 8:c * 8 + 8], SC[c][:].rearrange("p (h k) -> p h k", k=SK),
                                          AX.X, ALU.max).then_inc(s["max_done"], 1)

                cch = Chain(dve, s["chain_ctx"], 1)

                def context(b, c):
                    cch.begin(HC * b.k + c)
                    dve.wait_ge(s["den_ready"], 8 * b.k + 4 * c + 4)
                    wait(dve, s["ctx_done"], 2 * b.k + c)
                    cch.link(dve.reciprocal(rden[:], den[:, c, :]))
                    dve.tensor_tensor(cn[:, c, :], cn[:, c, :], rden[:], ALU.mult).then_inc(s["ctx_done"], 1)

                c2h = Chain(dve, s["chain_high"], 1)

                def split_context(c):
                    dve.wait_ge(s["ctx_done"], 2 * (c.k + 1))
                    wait(dve, s["wo_done"], T * c.k)
                    c2h.begin(c.k)
                    c2h.link(dve.tensor_copy(c_h[:, 1, :], cn[:, 1, :]))
                    dve.tensor_tensor(c_l[:, 1, :], cn[:, 1, :], c_h[:, 1, :].bitcast(f32), ALU.subtract)\
                       .then_inc(s["ctx_lo1"], 1)

                def residual(b):
                    for u in range(2):
                        dve.wait_ge(s["wo_done"], T * b.k + 2 * u + 2)
                        if u == 0:
                            dve.wait_ge(s["xb_done"], b.k + 1)
                        dve.tensor_tensor(pay[b.h][:, 2 * u:2 * u + 2, 0:H],
                                          SC[u][:].rearrange("p (t c) -> p t c", t=2),
                                          pay[b.h][:, 2 * u:2 * u + 2, 0:H], ALU.add).then_inc(s["x1_done"], 1)

                def norm2_stats(c):
                    ln2c.begin(c.k)
                    dve.wait_ge(s["x1_done"], 2 * (c.k + 1))
                    norm_stats(c, pay[c.h], st2, mv2, s["stat2_ready"], ln2c)

                def norm2(c):
                    dve.wait_ge(s["rstd2_ready"], c.k + 1)
                    wait(dve, s["x2T_done"], HC * c.k)
                    for t in range(T):
                        dve.tensor_scalar(xn2[:, t, :], pay[c.h][:, t, 0:H], mv2[:, t, 0:1],
                                          pay[c.h][:, t, C_RSTD:C_RSTD + 1], ALU.subtract, ALU.mult)\
                           .then_inc(s["xn2_ready"], 1)
                    dve.tensor_copy(pay[c.h][:, :, C_MEAN], mv2[:, :, 0]).then_inc(s["pay_ready"], 1)

                rch = Chain(dve, s["chain_route"], 7)

                def route(n, c):
                    def stats(t):
                        if n is not None:
                            x_stats(n, t)

                    if n is not None:
                        x_ready(n)
                    rch.begin(c.k)
                    dve.wait_ge(s["ezT_done"], c.k + 1)
                    rch.add(dve.tensor_scalar(e1[:], O[0][:, 0:T * E].rearrange("p (t e) -> p t e", e=E),
                                              1.0, None, ALU.add))
                    stats(0)
                    rch.sync()
                    rch.add(dve.reciprocal(pr[:], e1[:]))
                    stats(1)
                    rch.sync()
                    rch.add(dve.tensor_reduce(pm[:], pr[:], AX.X, ALU.max))
                    stats(2)
                    rch.sync()
                    rch.add(dve.tensor_tensor(eq[:], pr[:], pm[:].unsqueeze(2).broadcast_to([P, T, E]), ALU.is_equal))
                    stats(3)
                    rch.sync()
                    rch.add(dve.tensor_tensor(w_[:], eq[:], prio[:].unsqueeze(1).broadcast_to([P, T, E]), ALU.mult))
                    dve.tensor_scalar(pay[c.h][:, :, C_COEF], pm[:], tgt[:, 1:2], None, ALU.mult)
                    rch.sync()
                    rch.add(dve.tensor_reduce(wm[:], w_[:], AX.X, ALU.max))
                    dve.tensor_copy(pay[c.h][:, :, C_ID], tokid[:]).then_inc(s["pay_ready"], 1)
                    rch.sync()
                    dve.tensor_tensor(onehot[:, 0:T, :], w_[:], wm[:].unsqueeze(2).broadcast_to([P, T, E]),
                                      ALU.is_equal).then_inc(s["onehot_ready"], 1)
                    rch.add(dve.tensor_scalar(tokid[:], tokid[:], float(BLK), None, ALU.add))
                    if n is not None:
                        for t in range(T):
                            x_moments(n, t)
                    rch.sync()
                    rch.end()

                sch = Chain(dve, s["chain_slot"], 4)

                def slots_and_q_lo(c, a):
                    if c is not None:
                        sch.begin(c.k)
                        dve.wait_ge(s["rank_done"], c.k + 1)
                        sch.add(dve.tensor_tensor(rk[:], O[1][:, 0:T * E].rearrange("p (t e) -> p t e", t=T),
                                                  base[:, 0:E].unsqueeze(1).broadcast_to([P, T, E]), ALU.add))
                    if a is not None:
                        q_lo(a, 0)
                    if c is not None:
                        sch.sync()
                        sch.add(dve.tensor_tensor(base[:, 0:E], base[:, 0:E], O[1][:, T * E:(T + 1) * E], ALU.add))
                        sch.add(dve.tensor_tensor(rsel[:], rk[:], onehot[:, 0:T, :], ALU.mult))
                    if a is not None:
                        q_lo(a, 1)
                    if c is not None:
                        sch.sync()
                        sch.link(dve.tensor_reduce(slot_f[:], rsel[:], AX.X, ALU.add))
                        sch.end()
                        dve.wait_ge(scat[c.h], 16 + 16 * T * c.m)
                        dve.tensor_copy(slot[c.h][:], slot_f[:]).then_inc(s["slot_ready"], 1)

                def first(n, d):
                    if d is not None:
                        route(n, d)
                    else:
                        x_ready(n)
                        for t in range(T):
                            x_stats(n, t)
                        for t in range(T):
                            x_moments(n, t)
                    if n is not None and isinstance(n.k, int) and n.k == 0:
                        key_setup()

                def last(n):
                    xn_lo(n)
                    if isinstance(n.k, int) and n.k == 0:
                        value_setup()
                    if isinstance(n.k, int) and n.k == 1:
                        last_setup()

                def split_last(b):
                    dve.wait_ge(s["p_low"], NPAIR * b.k + 6)
                    for j in (6, 7):
                        i = j % NPB
                        dve.wait_ge(s["p_hi"], NPAIR * b.k + j + 1)
                        dve.tensor_tensor(p_l[i][:], p_f[i][:], p_h[i][:].bitcast(f32), ALU.subtract)\
                           .then_inc(s["p_low"], 1)

                def step(n, a, b, c, d):
                    if b is None and c is not None:
                        context(c, 1)
                        split_context(c)
                        first(n, d)
                        residual(c)
                        norm2_stats(c)
                        slots_and_q_lo(d, None)
                        norm2(c)
                        return
                    if n is not None or d is not None:
                        first(n, d)
                    if c is not None:
                        context(c, 1)
                        split_context(c)
                    if a is not None or d is not None:
                        slots_and_q_lo(d, a)
                    if c is not None:
                        residual(c)
                        norm2_stats(c)
                    if a is not None:
                        maxes(a, 0)
                    if c is not None:
                        norm2(c)
                    if b is not None and a is None:
                        split_last(b)
                    if a is not None:
                        maxes(a, 1)
                        maxes(a, 2)
                        maxes(a, 3)
                    if b is not None:
                        context(b, 0)
                    if n is not None:
                        last(n)

                run_blocks(dve, step)

                tc = Chain(dve, s["chain_tab"], 13)
                tc.begin(0)
                dve.wait_ge(s["chain_slot"], 4 * NBLK)
                tc.add(dve.tensor_tensor(step_end[:], base[:, 1:E + 1], base[:, 0:E], ALU.subtract))
                tc.link(dve.tensor_tensor(cnt[:], base[:, 0:E], ecap[:, 0:E], ALU.subtract))
                tc.link(dve.tensor_tensor(over[:], cnt[:].unsqueeze(2).broadcast_to([P, E, MIN_TILES]),
                                          th[:].unsqueeze(1).broadcast_to([P, E, MIN_TILES]), ALU.is_gt))
                tc.link(dve.tensor_reduce(ntl[:], over[:], AX.X, ALU.add))
                tc.link(dve.tensor_tensor(ctri[:], tri[:], ntl[:].unsqueeze(1).broadcast_to([P, E, E]), ALU.mult))
                tc.link(dve.tensor_reduce(cend[:], ctri[:], AX.X, ALU.add))
                tc.link(dve.tensor_tensor(ge[:], cend[:].unsqueeze(1).broadcast_to([P, NT, E]),
                                          ti[:].unsqueeze(2).broadcast_to([P, NT, E]), ALU.is_le))
                tc.add(dve.tensor_reduce(et[:], ge[:], AX.X, ALU.add))
                tc.add(dve.tensor_tensor(gel[:], ge[:], step_end[:].unsqueeze(1).broadcast_to([P, NT, E]), ALU.mult))
                tc.link(dve.tensor_tensor(gen[:], ge[:], ntl[:].unsqueeze(1).broadcast_to([P, NT, E]), ALU.mult))
                tc.add(dve.tensor_reduce(lim[:], gel[:], AX.X, ALU.add))
                tc.link(dve.tensor_reduce(cs[:], gen[:], AX.X, ALU.add))
                tc.link(dve.tensor_tensor(cs[:], ti[:], cs[:], ALU.subtract))
                tc.end()
                tl = Chain(dve, s["chain_tab2"], 5)
                tl.begin(0)
                tl.link(dve.tensor_scalar(cs[:], cs[:], float(TT), float(2 * TT), ALU.mult, ALU.add))
                tl.link(dve.scalar_tensor_tensor(start[:], et[:], float(CAP), cs[:], ALU.mult, ALU.add))
                tl.link(dve.scalar_tensor_tensor(start[:], lim[:], base[:, 0:1], start[:], ALU.add, ALU.min))
                tl.add(dve.tensor_scalar(row_f[:, 0, :], start[:], float(TT), None, ALU.subtract))
                tl.link(dve.tensor_scalar(row_f[:, 1, :], et[:], float(E - 1), None, ALU.min))
                tl.end()
                dve.tensor_copy(tab[:], row_f[:]).then_inc(s["tab_ready"], 1)
                dve.wait_ge(s["tab_ready"], 1)

            @blk.tensor
            def _(pe):
                pe.wait_ge(s["keys_in"], 16 * (HC + 2))
                for oc in range(HC):
                    for c in range(HC):
                        mm = pe.matmul(X[oc][:, 0:B * SK], wk_t[:, c, oc * P:(oc + 1) * P],
                                       ctx_t[:, c, :, 0, :], start=(c == 0), stop=(c == HC - 1))
                    mm.then_inc(s["setup_pe"], 1)
                pe.wait_ge(s["keys_twice"], 1)
                pe.wait_ge(s["wv_in"], 32)
                for b in range(B):
                    for c in range(HC):
                        mm = pe.matmul(SC[b // 2][:, (b % 2) * H:(b % 2 + 1) * H],
                                       ctx_t[:, c, b].rearrange("p d k -> p (d k)"), wv_t[:, c, :],
                                       start=(c == 0), stop=(c == HC - 1))
                    if b % 2:
                        mm.then_inc(s["setup_pe"], 1)
                pe.wait_ge(s["pool_const"], POOL_CONST)
                pe.wait_ge(s["setup_dve"], KEYS_DVE)

                def product(o, terms):
                    for n, (l, r) in enumerate(terms):
                        mm = pe.matmul(o, l, r, start=(n == 0), stop=(n == len(terms) - 1))
                    return mm

                def turn_x(a, c):
                    wait(pe, s["q_ready"], HC * a.k)
                    if c == 0:
                        wait(pe, s["xn2T_ready"], HC * (a.k - 2))
                    else:
                        wait(pe, s["ez_ready"], a.k - 2)
                    for t in range(T):
                        if c == 0:
                            pe.wait_ge(s["xn_ready"], T * a.k + t + 1)
                        mm = pe.transpose(X[c][:, t * P:(t + 1) * P], xn[:, t, c * P:(c + 1) * P], identf[:])
                    mm.then_inc(s["xT_done"], 1)

                def queries(a):
                    if isinstance(a.k, int) and a.k == 0:
                        pe.wait_ge(s["setup_dve"], QUERIES_DVE)
                    pe.wait_ge(s["xnT_ready"], HC * (a.k + 1))
                    for oc in range(HC):
                        o = slice(oc * P, (oc + 1) * P)
                        product(X[oc][:], [(w[:, c, o], z[:, c, :]) for c in range(HC) for w, z in
                                           ((wq_h, xnT_h), (wq_l, xnT_h), (wq_h, xnT_l))])\
                            .then_inc(s["q_done"], 1)

                def token_scores(a, t):
                    pe.wait_ge(s["q_hi"], HC * (a.k + 1))
                    pe.wait_ge(s["tmask_ready"], a.k + 1)
                    if isinstance(a.k, int) and a.k == 0:
                        pe.wait_ge(s["setup_dve"], VALUES_DVE)
                    if isinstance(a.k, int) and a.k == 2:
                        pe.wait_ge(s["kbd_ready"], HC * (B - 1))
                    for c in range(HC):
                        n = HC * T * a.k + HC * t + c
                        wait(pe, s["max_done"], n - 1)
                        if t == 0 and c == 0:
                            wait(pe, s["mx_ready"], a.k)
                        if t == 0:
                            wait(pe, s["x1_done"], 2 * (a.k - 2) + c + 1)
                        pe.matmul(SC[c][:], q_h[a.h][:, c, t * P:(t + 1) * P], kbd[:, a.m, c, :],
                                  start=True, stop=False)
                        pe.matmul(SC[c][:], ident_bf[:], mb[a.h][:, t, :].unsqueeze(1).broadcast_to([P, NH // 2, SK]),
                                  start=False, stop=True).then_inc(s["tok_scored"], 1)

                def turn_maxima(a):
                    pe.wait_ge(s["max_done"], HC * T * (a.k + 1))
                    for t in range(T):
                        mm = pe.transpose(SC[0][0:NH, t * P:(t + 1) * P], smax[:, t, :], identf[:])
                    mm.then_inc(s["mxT_done"], 1)

                def key_scores(b, g):
                    if isinstance(b.k, int) and b.k == 0 and g == 0:
                        pe.wait_ge(s["setup_dve"], VALUES_DVE)
                    if g == 0:
                        pe.wait_ge(s["mx_ready"], b.k + 1)
                        pe.wait_ge(s["kmask_ready"], b.k + 1)
                        pe.wait_ge(s["k_ready"], 2 * HC * (b.m + 1))
                        pe.wait_ge(s["q_ready"], HC * (b.k + 1))
                    for j in (2 * g, 2 * g + 1):
                        wait(pe, s["exp_done"], NPAIR * b.k + j - 1)
                        pe.matmul(TS[j % 2][:], sel[:, j, :], mx[b.h][:], start=True, stop=False)
                    for n, (kk, qq) in enumerate(((kp_h, q_h), (kp_l, q_h), (kp_h, q_l))):
                        for j in (2 * g, 2 * g + 1):
                            r, c = slice(32 * (j % 4), 32 * (j % 4) + 32), j // 4
                            mm = pe.matmul(TS[j % 2][:], kk[r, c, :], qq[b.h][r, c, :], start=False, stop=(n == 2))
                            if n == 2:
                                mm.then_inc(s["tsc_done"], 1)

                def values(b, g, pairs=(0, 1)):
                    if g >= 2 and 0 in pairs:
                        pe.wait_ge(s["den_ready"], 8 * b.k + 2 * g - 2)
                    if g == 0:
                        pe.wait_ge(s["v_ready"], 4 * (b.m + 1))
                    if g == 0:
                        wait(pe, s["onehot_ready"], b.k - 1)
                    if g == 1:
                        wait(pe, s["chain_slot"], 4 * (b.k - 2) + 2)
                    for j in (2 * g + half for half in pairs):
                        i = j % NPB
                        pe.wait_ge(s["p_low"], NPAIR * b.k + j + 1)
                        for n, (vv, pp) in enumerate(((vbd_h, p_h), (vbd_l, p_h), (vbd_h, p_l))):
                            v = vv[:, j // 4].rearrange("p i n -> p (i n)")[:, P * (j % 4):P * (j % 4 + 1)]
                            mm = pe.matmul(O[g % 2][:], v, pp[i][:], start=(j % 2 == 0 and n == 0),
                                           stop=(j % 2 == 1 and n == 2))
                        mm.then_inc(s["pv_done"], 1)

                def project(b):
                    pe.wait_ge(s["ctx_lo0"], b.k + 1)
                    k = min(b.k + 2, NBLK) if isinstance(b.k, int) else b.k + 2
                    pe.wait_ge(s["max_done"], HC * T * k)
                    pe.wait_ge(s["mx_ready"], k)
                    for c in range(HC):
                        if c == 1:
                            pe.wait_ge(s["ctx_lo1"], b.k + 1)
                        for t in range(T):
                            z = slice(t * P, (t + 1) * P)
                            for n, (l, w) in enumerate(((c_h, wo_h), (c_h, wo_l), (c_l, wo_h))):
                                mm = pe.matmul(SC[t // 2][:, (t % 2) * H:(t % 2 + 1) * H], l[:, c, z], w[:, c, :],
                                               start=(c == 0 and t % 2 == 0 and n == 0), stop=(c == 1 and t % 2 == 1 and n == 2),
                                               skip_group_check=True)
                            if c == 1:
                                mm.then_inc(s["wo_done"], 1)

                def turn_x2(c):
                    pe.wait_ge(s["q_ready"], HC * min(c.k + 3, NBLK) if isinstance(c.k, int) else HC * (c.k + 3))
                    for i in range(HC):
                        for t in range(T):
                            if i == 0:
                                pe.wait_ge(s["xn2_ready"], T * c.k + t + 1)
                            mm = pe.transpose(X[i][:, t * P:(t + 1) * P], xn2[:, t, i * P:(i + 1) * P], identf[:])
                        mm.then_inc(s["x2T_done"], 1)

                def logits(c):
                    pe.wait_ge(s["xn2T_ready"], HC * (c.k + 1))
                    for i in range(HC):
                        mm = pe.matmul(X[1][0:E, :], wr_sb[:, i, :], xn2T[:, i, :], start=(i == 0), stop=(i == HC - 1))
                    mm.then_inc(s["lg_done"], 1)

                def turn_logits(c):
                    wait(pe, s["ez_ready"], c.k + 1, s["pe_passed"])
                    wait(pe, s["den_ready"], 8 * (c.k + 2) - 2 if not isinstance(c.k, int) or c.k + 2 <= NBLK else 8 * NBLK,
                         s["pe_passed"])
                    for t in range(T):
                        mm = pe.transpose(O[0][:, t * E:(t + 1) * E], ez[:, t * P:(t + 1) * P], identf[0:E, 0:E])
                    mm.then_inc(s["ezT_done"], 1)

                def ranks(c):
                    pe.wait_ge(s["onehot_ready"], c.k + 1)
                    pe.wait_ge(s["den_ready"], 8 * (min(c.k + 2, NBLK) if isinstance(c.k, int) else c.k + 2))
                    o = O[1][:, 0:(T + 1) * E].rearrange("p (t e) -> p t e", e=E)
                    for t in range(T):
                        pe.matmul(o[:, t + 1:T + 1, :], ones_bf[:],
                                  onehot[:, t:t + 1, :].broadcast_to([P, T - t, E]),
                                  start=(t == 0), stop=False, skip_group_check=True)
                    mm = pe.matmul(o, before_bf[:], onehot[:], start=False, stop=True, skip_group_check=True)
                    mm.then_inc(s["rank_done"], 1)

                def step(n, a, b, c, d):
                    if b is not None:
                        key_scores(b, 0)
                    if d is not None:
                        turn_logits(d)
                    if c is not None and b is not None:
                        values(c, 3, (1,))
                    if b is not None:
                        key_scores(b, 1)
                    if a is not None:
                        queries(a)
                    if b is not None:
                        values(b, 0)
                    if d is not None and not (b is None and c is not None):
                        ranks(d)
                    if b is not None:
                        key_scores(b, 2)
                    if c is not None:
                        project(c)
                    if d is not None and b is None and c is not None:
                        ranks(d)
                    if b is not None:
                        values(b, 1)
                    if a is not None:
                        token_scores(a, 0)
                    if b is not None:
                        key_scores(b, 3)
                    if a is not None:
                        token_scores(a, 1)
                    if b is not None:
                        values(b, 2)
                    if c is not None:
                        turn_x2(c)
                    if a is not None:
                        token_scores(a, 2)
                    if b is not None and a is None:
                        values(b, 3)
                    if c is not None:
                        logits(c)
                    if a is not None:
                        token_scores(a, 3)
                    if n is not None:
                        turn_x(n, 0)
                    if a is not None:
                        turn_maxima(a)
                    if n is not None:
                        turn_x(n, 1)
                    if b is not None and a is not None:
                        values(b, 3, (0,))

                run_blocks(pe, step)
        A.close()

        g_sb = [sb(f"g{i}", [P, 2, ROW], f32) for i in range(2)]
        xe = sb("xe", [P, 2, H], f32)
        gelu_0 = sb("gelu_0", [P, 1], f32)
        xeT_h = sb("xeT_h", [P, HC, TT], f32r)
        xeT_l = sb("xeT_l", [P, HC, TT], f32r)
        w1_h = [sb(f"w1_h{i}", [P, HC, F], f32r) for i in range(2)]
        w1_l = [sb(f"w1_l{i}", [P, HC, F], f32r) for i in range(2)]
        w2_h = [sb(f"w2_h{i}", [P, FC, H], f32r) for i in range(2)]
        w2_l = [sb(f"w2_l{i}", [P, FC, H], f32r) for i in range(2)]
        NU = FC // 2
        h_f = [sb(f"h_f{i}", [P, 2, TT], f32) for i in range(NU)]
        h_h = [sb(f"h_h{i}", [P, FC, TT], f32r) for i in range(2)]
        h_l = [sb(f"h_l{i}", [P, FC, TT], f32r) for i in range(2)]
        o_sb = [sb(f"o{i}", [P, 2, H], f32) for i in range(2)]
        o_idx = [sb(f"o_idx{i}", [P, 2], i32) for i in range(2)]

        def is_first(b):
            return isinstance(b.k, int) and b.k == 0

        def w1_parts(b):
            return [slice(c, c + 1) for c in range(HC)] if is_first(b) else [slice(0, HC)]

        def w1_count(b):
            return HC + b.k

        HB = [bank[n] for n in ("S0", "S1", "T0", "T1")]
        (w1_in, w2_in), (g_in, osc) = w_in, ([s[f"{n}{i}"] for i in range(2)] for n in ("g_in", "osc"))

        with nc.Block() as blk:

            @blk.sync
            def _(sp):
                def load_w1(b):
                    if not (isinstance(b.k, int) and b.k < 2):
                        wait(sp, s["w1_ready"], w1_count(b) - 2, s["sp_passed"])
                    load_weights(sp, 0, b)

                def load_w2(b):
                    wait(sp, s["w2_ready"], b.k - 1, s["sp_passed"])
                    load_weights(sp, 1, b)

                def load_rows(b):
                    wait(sp, s["o_ready"], 2 * (b.k - 1), s["sp_passed"])
                    r = sp.value_load(tab[0:1, 0, bass.ds(b.k, 1)], min_val=0, max_val=BINS - TT)
                    sp.dma_start(g_sb[b.h][:], bins[bass.ds(r, TT), :].rearrange("(n p) c -> p n c", p=P))\
                      .then_inc(g_in[b.h], 16)

                def load_tile(b):
                    load_w2(b)
                    load_rows(b)

                load_rows(Blk(0, 0))
                load_w2(Blk(0, 0))
                load_w1(Blk(0, 1))
                load_w1(Blk(1, 0))
                load_tile(Blk(0, 1))
                with sp.Fori(0, (NT - 3) // 2) as i:
                    load_w1(Blk(i + 1, 1))
                    load_tile(Blk(i + 1, 0))
                    load_w1(Blk(i + 2, 0))
                    load_tile(Blk(i + 1, 1))
                load_tile(Blk((NT - 1) // 2, 0))

            @blk.gpsimd
            def _(pool):
                def store(b):
                    wait(pool, s["o_ready"], 2 * (b.k + 1), s["pool_passed"])
                    wait(pool, osc[1 - b.h], 32 * (b.m + b.h), s["pool_passed"])
                    for t in range(2):
                        pool.indirect_dma_start(
                            out=out_rows, out_offset=bass.IndirectOffsetOnAxis(ap=o_idx[b.h][:, t:t + 1], axis=0),
                            in_=o_sb[b.h][:, t, :], in_offset=None, bounds_check=B * S - 1, oob_is_err=False)\
                            .then_inc(osc[b.h], 16)

                def step(w, a, b):
                    if b is not None:
                        store(b)

                run_tiles(pool, step)
                for h in range(2):
                    wait(pool, osc[h], 32 * ((NT + 1 - h) // 2), s["pool_passed"])

            @blk.scalar
            def _(act):
                def w1_high(w):
                    act.wait_ge(w1_in[w.h], 16 * (w.m + 1))
                    wait(act, s["l1_done"], NU * (w.k - 1))
                    for z in w1_parts(w):
                        act.copy(w1_h[w.h][:, z], w1_raw[w.h][:, z]).then_inc(s["w1_hi"], 1)

                def w2_high(a):
                    act.wait_ge(w2_in[a.h], 16 * (a.m + 1))
                    wait(act, s["y_done"], 2 * (a.k - 1))
                    act.copy(w2_h[a.h][:], w2_raw[a.h][:]).then_inc(s["w2_hi"], 1)

                def rows_high(a):
                    act.wait_ge(s["xeT_done"], a.k + 1)
                    act.copy(xeT_h[:].rearrange("p c n -> p (c n)"), X[0][:]).then_inc(s["xeT_hi"], 1)

                def hidden(a, u):
                    act.wait_ge(s["l1_done"], NU * a.k + u + 1)
                    wait(act, s["h_ready"], NU * (a.k - 1) + u + 1)
                    act.activation(h_f[u][:].rearrange("p c n -> p (c n)"), HB[u][:], ACT.Gelu)\
                       .then_inc(s["gelu_done"], 1)
                    if u == 0:
                        wait(act, s["y_done"], 2 * (a.k - 1))
                    act.wait_ge(s["gelu_done"], NU * a.k + u + 1)
                    act.copy(h_h[a.h][:, 2 * u:2 * u + 2, :], h_f[u][:]).then_inc(s["h_hi"], 1)

                def step(w, a, b):
                    if a is None and w is not None:
                        act.activation(gelu_0[:], padding[:, 0:1], ACT.Gelu)
                    if a is not None:
                        rows_high(a)
                        w2_high(a)
                    if w is not None:
                        w1_high(w)
                    if a is not None:
                        for u in range(NU):
                            hidden(a, u)

                run_tiles(act, step)

            @blk.vector
            def _(dve):
                def w1_low(w):
                    for n, z in enumerate(w1_parts(w)):
                        dve.wait_ge(s["w1_hi"], n + 1 if is_first(w) else w1_count(w))
                        dve.tensor_tensor(w1_l[w.h][:, z], w1_raw[w.h][:, z], w1_h[w.h][:, z].bitcast(f32),
                                          ALU.subtract).then_inc(s["w1_ready"], 1)

                def w2_low(a):
                    dve.wait_ge(s["w2_hi"], a.k + 1)
                    dve.tensor_tensor(w2_l[a.h][:], w2_raw[a.h][:], w2_h[a.h][:].bitcast(f32), ALU.subtract)\
                       .then_inc(s["w2_ready"], 1)

                def normalize(a):
                    dve.wait_ge(g_in[a.h], 16 * (a.m + 1))
                    wait(dve, s["xeT_done"], a.k)
                    g = g_sb[a.h]
                    for t in range(2):
                        dve.tensor_scalar(xe[:, t, :], g[:, t, 0:H], g[:, t, C_MEAN:C_MEAN + 1],
                                          g[:, t, C_RSTD:C_RSTD + 1], ALU.subtract, ALU.mult).then_inc(s["xe_ready"], 1)

                def hidden_low(a, u):
                    dve.wait_ge(s["h_hi"], NU * a.k + u + 1)
                    dve.tensor_tensor(h_l[a.h][:, 2 * u:2 * u + 2, :], h_f[u][:],
                                      h_h[a.h][:, 2 * u:2 * u + 2, :].bitcast(f32), ALU.subtract).then_inc(s["h_ready"], 1)

                def rows_low(a):
                    dve.wait_ge(s["xeT_hi"], a.k + 1)
                    dve.tensor_tensor(xeT_l[:].rearrange("p c n -> p (c n)"), X[0][:],
                                      xeT_h[:].rearrange("p c n -> p (c n)").bitcast(f32), ALU.subtract)\
                       .then_inc(s["xeT_ready"], 1)

                def output(b, t):
                    g = g_sb[b.h]
                    if t == 0:
                        wait(dve, osc[b.h], 32 * b.m)
                        dve.tensor_copy(o_idx[b.h][:], g[:, :, C_ID])
                    dve.wait_ge(s["y_done"], 2 * b.k + t + 1)
                    dve.scalar_tensor_tensor(o_sb[b.h][:, t, :], O[t][:, 0:H], g[:, t, C_COEF:C_COEF + 1],
                                             g[:, t, 0:H], ALU.mult, ALU.add).then_inc(s["o_ready"], 1)

                def step(w, a, b):
                    if a is not None:
                        rows_low(a)
                    if b is not None:
                        output(b, 0)
                    if a is not None:
                        w2_low(a)
                    if b is not None:
                        output(b, 1)
                    first = w is not None and a is None
                    if first:
                        normalize(w)
                    if w is not None:
                        w1_low(w)
                    if a is not None:
                        for u in range(NU - 1):
                            hidden_low(a, u)
                    if w is not None and not first:
                        normalize(w)
                    if a is not None:
                        hidden_low(a, NU - 1)

                run_tiles(dve, step)

            @blk.tensor
            def _(pe):
                def turn(a):
                    wait(pe, s["xeT_ready"], a.k)
                    for t in range(2):
                        pe.wait_ge(s["xe_ready"], 2 * a.k + t + 1)
                        for c in range(HC):
                            mm = pe.transpose(X[0][:, c * TT + t * P:c * TT + (t + 1) * P],
                                              xe[:, t, c * P:(c + 1) * P], identf[:])
                    mm.then_inc(s["xeT_done"], 1)

                def first_layer(a, u):
                    if u == 0:
                        pe.wait_ge(s["xeT_ready"], a.k + 1)
                        pe.wait_ge(s["w1_ready"], w1_count(a))
                    wait(pe, s["gelu_done"], NU * (a.k - 1) + u + 1)
                    for f in (2 * u, 2 * u + 1):
                        z = slice(f * P, (f + 1) * P)
                        terms = [(w[:, c, z], xx[:, c, :]) for c in range(HC) for w, xx in
                                 ((w1_h[a.h], xeT_h), (w1_h[a.h], xeT_l), (w1_l[a.h], xeT_h))]
                        for n, (l, r) in enumerate(terms):
                            mm = pe.matmul(HB[u][:, (f % 2) * TT:(f % 2 + 1) * TT], l, r,
                                           start=(n == 0), stop=(n == len(terms) - 1))
                    mm.then_inc(s["l1_done"], 1)

                def second_layer(b, t, chunks):
                    if t == 0 and chunks[0] == 0:
                        wait(pe, s["o_ready"], 2 * b.k)
                        pe.wait_ge(s["w2_ready"], b.k + 1)
                    z = slice(t * P, (t + 1) * P)
                    for f in chunks:
                        if t == 0 and f % 2 == 0:
                            pe.wait_ge(s["h_ready"], NU * b.k + f // 2 + 1)
                        for n, (hh, ww) in enumerate(((h_h, w2_h), (h_h, w2_l), (h_l, w2_h))):
                            mm = pe.matmul(O[t][:, 0:H], hh[b.h][:, f, z], ww[b.h][:, f, :],
                                           start=(f == 0 and n == 0), stop=(f == FC - 1 and n == 2))
                    if chunks[-1] == FC - 1:
                        mm.then_inc(s["y_done"], 1)

                def step(w, a, b):
                    if b is not None:
                        second_layer(b, 0, range(0, FC - 2))
                    if a is not None:
                        turn(a)
                    if b is not None:
                        second_layer(b, 0, range(FC - 2, FC))
                        second_layer(b, 1, range(FC))
                    if a is not None:
                        for u in range(NU):
                            first_layer(a, u)

                run_tiles(pe, step)


def kernel(**inputs):
    import numpy as np
    import concourse.bacc as bacc
    from concourse import mybir as mb
    from concourse.bass_utils import run_bass_kernel_spmd

    def host(name):
        return np.asarray(inputs[name])

    def flat_row(name):
        return np.ascontiguousarray(host(name).reshape(1, -1))

    arrays = {
        "x": host("x"),
        "ctxT": np.ascontiguousarray(host("ctx_1024").reshape(B * SK, H).T),
        "mask": host("mask_BxSxS2_if1"),
        "maskT": np.ascontiguousarray(host("mask_BxSxS2_if1").transpose(0, 2, 1)),
        "g_xattn": host("g_xattn").reshape(1), "g_ffn": host("g_ffn").reshape(1),
        "WqT": np.ascontiguousarray(host("L0_xattn_Wq").T),
        "bq": np.ascontiguousarray(host("L0_xattn_bq").reshape(HC, P).T),
        "WkT": np.ascontiguousarray(host("L0_xattn_Wk").T),
        "bk": np.ascontiguousarray(host("L0_xattn_bk").reshape(HC, P).T),
        "WvT": np.ascontiguousarray(host("L0_xattn_Wv").T), "bv": flat_row("L0_xattn_bv"),
        "WoT": np.ascontiguousarray(host("L0_xattn_Wo").T), "bo": flat_row("L0_xattn_bo"),
        "Wr": host("L0_ffn_Wr"), "br": np.ascontiguousarray(host("L0_ffn_br").reshape(E, 1)),
        "W1": host("L0_ffn_W1"), "W2": host("L0_ffn_W2"),
    }
    nc = bacc.Bacc("TRN2", target_bir_lowering=False, num_devices=1)
    args = [nc.dram_tensor(n, a.shape, mb.dt.from_np(a.dtype), kind="ExternalInput").ap() for n, a in arrays.items()]
    out = nc.dram_tensor("out", (B, S, H), mb.dt.float32, kind="ExternalOutput").ap()
    build(nc, *args, out)
    result = run_bass_kernel_spmd(nc, [{n: np.ascontiguousarray(a) for n, a in arrays.items()}], core_ids=[0])
    return result.results[0]["out"]
```
